# Optimizing a Trainium2 kernel written in Bass

```python
import numpy as np
import jax
import jax.numpy as jnp

def _softmax(x, axis=-1):
    return jax.nn.softmax(x, axis=axis)

def _gelu(x):
    return jax.nn.gelu(x, approximate=True)

def _silu(x):
    return jax.nn.silu(x)

def _sigmoid(x):
    return jax.nn.sigmoid(x)

def _layernorm(x, axis=-1, eps=1e-05):
    m = jnp.mean(x, axis=axis, keepdims=True)
    v = jnp.var(x, axis=axis, keepdims=True)
    return (x - m) / jnp.sqrt(v + eps)

def _scatter_add(tgt, idx, src, axis=0):
    return tgt.at[idx].add(src)

def _segment_sum(src, seg, n):
    return jax.ops.segment_sum(src, seg, n)
kernel_name = 'mk_adaln_attn_ffn_d2_seqx_r4_86d291'

def setup_inputs(seed: int=0):
    np.random.seed(seed)
    _w = jnp.asarray

    def _rec_inputs():
        import jax
        import jax.numpy as jnp
        _rk = jax.random.key(seed)
        x = 7.22e-05 + 1 * jax.random.normal(jax.random.fold_in(_rk, 1), (4, 512, 256), jnp.float32)
        _lenS = 512 - jax.random.randint(jax.random.fold_in(_rk, 7), (4,), 0, max(1, 512 // 4) + 1, jnp.int32)
        _lenS2 = 512 - jax.random.randint(jax.random.fold_in(_rk, 8), (4,), 0, max(1, 512 // 4) + 1, jnp.int32)
        cond_512 = 0.0061147 + 1.02565 * jax.random.normal(jax.random.fold_in(_rk, 11), (4, 128), jnp.float32)
        itok_BxS_0_999 = jax.random.randint(jax.random.fold_in(_rk, 12), (4, 512), 0, 250, jnp.int32)
        itok_BxS_0_4 = jax.random.randint(jax.random.fold_in(_rk, 13), (4, 512), 0, 5, jnp.int32)
        cond_64 = 0.0990542 + 1.04422 * jax.random.normal(jax.random.fold_in(_rk, 15), (4, 64), jnp.float32)
        fside_Bx32_0 = -0.136436 + 0.990155 * jax.random.normal(jax.random.fold_in(_rk, 16), (4, 32), jnp.float32)
        _validS = jnp.arange(512)[None, :] < _lenS[:, None]
        _validS2 = jnp.arange(512)[None, :] < _lenS2[:, None]
        _causal = jnp.tril(jnp.ones((512, 512), dtype=bool))
        mask_BxS_ik0 = jnp.where(jnp.broadcast_to(_validS[:, :], (4, 512)), 0, 1).astype(jnp.int32)
        return (x, cond_512, itok_BxS_0_999, itok_BxS_0_4, cond_64, fside_Bx32_0, mask_BxS_ik0)
    x, cond_512, itok_BxS_0_999, itok_BxS_0_4, cond_64, fside_Bx32_0, mask_BxS_ik0 = _rec_inputs()

    def _L0_cond_setup():
        import jax, jax.numpy as jnp
        import numpy as np
        import math
        HEAD_NUM = 16
        EPS = 1e-08

        def modulated_linear(x, s, aff_w, aff_b, w, b):
            style = s @ aff_w.T + aff_b
            w_mod = w[None, :, :] * style[:, None, :]
            demod = jax.lax.rsqrt(jnp.sum(w_mod * w_mod, axis=2) + EPS)
            w_mod = w_mod * demod[:, :, None]
            return jnp.einsum('bni,boi->bno', x, w_mod) + b
        key = jax.random.key(seed)
        ks = jax.random.split(key, 6)
        B, N, F, S = (8, 256, 256, 128)
        return {'x': jax.random.normal(ks[0], (B, N, F), dtype=jnp.float32), 's': jax.random.normal(ks[1], (B, S), dtype=jnp.float32), 'k_aff_w': jax.random.normal(ks[2], (F, S), dtype=jnp.float32) * 0.02, 'k_aff_b': jnp.ones((F,), dtype=jnp.float32), 'k_w': jax.random.normal(ks[3], (F, F), dtype=jnp.float32) * 0.02, 'k_b': jnp.zeros((F,), dtype=jnp.float32), 'o_aff_w': jax.random.normal(ks[4], (F, S), dtype=jnp.float32) * 0.02, 'o_aff_b': jnp.ones((F,), dtype=jnp.float32), 'o_w': jax.random.normal(ks[5], (F, F), dtype=jnp.float32) * 0.02, 'o_b': jnp.zeros((F,), dtype=jnp.float32)}
    _L0_cond_all = _L0_cond_setup()
    _L0_cond_in = {k: v for k, v in _L0_cond_all.items() if k in ('k_aff_w', 'k_aff_b', 'k_w', 'k_b', 'o_aff_w', 'o_aff_b', 'o_w', 'o_b')}
    del _L0_cond_all

    def _L0_attn_setup():
        import jax, jax.numpy as jnp
        import numpy as np
        D_MODEL = 256
        D_STATE = 16
        D_CONV = 4
        EXPAND = 2
        D_INNER = EXPAND * D_MODEL
        DT_RANK = D_MODEL // 16
        EPS = 1e-05

        def _mamba_block(x, gamma, beta, W_in, conv_w, conv_b, W_x, W_dt, b_dt, A_log, D, W_out):
            mu = x.mean(-1, keepdims=True)
            var = ((x - mu) ** 2).mean(-1, keepdims=True)
            xn = (x - mu) * jax.lax.rsqrt(var + EPS) * gamma + beta
            xz = xn @ W_in
            u, z = jnp.split(xz, 2, axis=-1)
            uc = jax.lax.conv_general_dilated(u.transpose(0, 2, 1), conv_w[:, None, :], window_strides=(1,), padding=[(D_CONV - 1, 0)], feature_group_count=D_INNER, dimension_numbers=('NCH', 'OIH', 'NCH'))
            u2 = jax.nn.silu(uc.transpose(0, 2, 1) + conv_b)
            dbl = u2 @ W_x
            dt_low = dbl[..., :DT_RANK]
            Bm = dbl[..., DT_RANK:DT_RANK + D_STATE]
            Cm = dbl[..., DT_RANK + D_STATE:]
            dt = jax.nn.softplus(dt_low @ W_dt + b_dt)
            A = -jnp.exp(A_log)

            def step(h, inp):
                dt_t, B_t, C_t, u_t = inp
                dA = jnp.exp(dt_t[:, :, None] * A)
                h = dA * h + (dt_t * u_t)[:, :, None] * B_t[:, None, :]
                y = jnp.einsum('bdn,bn->bd', h, C_t)
                return (h, y)
            Bb = x.shape[0]
            h0 = jnp.zeros((Bb, D_INNER, D_STATE), x.dtype)
            xs = (dt.transpose(1, 0, 2), Bm.transpose(1, 0, 2), Cm.transpose(1, 0, 2), u2.transpose(1, 0, 2))
            _, ys = jax.lax.scan(step, h0, xs)
            y = ys.transpose(1, 0, 2) + u2 * D
            y = y * jax.nn.silu(z)
            out = y @ W_out
            return x + out
        key = jax.random.key(seed)
        ks = jax.random.split(key, 8)
        B, L = (2, 512)
        x = jax.random.normal(ks[0], (B, L, D_MODEL), dtype=jnp.float32)
        gamma = jnp.ones((D_MODEL,), jnp.float32)
        beta = jnp.zeros((D_MODEL,), jnp.float32)
        W_in = jax.random.normal(ks[1], (D_MODEL, 2 * D_INNER), jnp.float32) * 0.02
        conv_w = jax.random.normal(ks[2], (D_INNER, D_CONV), jnp.float32) * 0.1
        conv_b = jnp.zeros((D_INNER,), jnp.float32)
        W_x = jax.random.normal(ks[3], (D_INNER, DT_RANK + 2 * D_STATE), jnp.float32) * 0.02
        W_dt = jax.random.normal(ks[4], (DT_RANK, D_INNER), jnp.float32) * DT_RANK ** (-0.5)
        b_dt = jnp.log(jnp.expm1(jnp.full((D_INNER,), 0.01, jnp.float32)))
        A_log = jnp.log(jnp.tile(jnp.arange(1, D_STATE + 1, dtype=jnp.float32), (D_INNER, 1)))
        D = jnp.ones((D_INNER,), jnp.float32)
        W_out = jax.random.normal(ks[5], (D_INNER, D_MODEL), jnp.float32) * 0.02
        return dict(x=x, gamma=gamma, beta=beta, W_in=W_in, conv_w=conv_w, conv_b=conv_b, W_x=W_x, W_dt=W_dt, b_dt=b_dt, A_log=A_log, D=D, W_out=W_out)
    _L0_attn_all = _L0_attn_setup()
    _L0_attn_in = {k: v for k, v in _L0_attn_all.items() if k in ('gamma', 'beta', 'W_in', 'conv_w', 'conv_b', 'W_x', 'W_dt', 'b_dt', 'A_log', 'D', 'W_out')}
    del _L0_attn_all

    def _L0_cond2_setup():
        import jax, jax.numpy as jnp
        import numpy as np
        W_DIM = 128
        CLAMP = 256.0
        key = jax.random.key(seed)
        ks = jax.random.split(key, 6)
        B, L, C = (8, 2048, 256)
        return {'x': jax.random.normal(ks[0], (B, L, C), dtype=jnp.float32), 'w': jax.random.normal(ks[1], (B, W_DIM), dtype=jnp.float32), 'weight': jax.random.normal(ks[2], (C, C), dtype=jnp.float32), 'bias': jax.random.normal(ks[3], (C,), dtype=jnp.float32), 'affine_w': jax.random.normal(ks[4], (C, W_DIM), dtype=jnp.float32), 'affine_b': jnp.ones((C,), dtype=jnp.float32)}
    _L0_cond2_all = _L0_cond2_setup()
    _L0_cond2_in = {k: v for k, v in _L0_cond2_all.items() if k in ('weight', 'bias', 'affine_w', 'affine_b')}
    del _L0_cond2_all

    def _L0_ffn_setup():
        import jax, jax.numpy as jnp
        import numpy as np
        FP8_MAX = 448.0
        SCALE = 1.0
        _FP8_DTYPE = getattr(jnp, 'float8_e4m3fn', jnp.float16)

        def quantize_e4m3(t, scale):
            return jnp.clip(t / scale, -FP8_MAX, FP8_MAX).astype(_FP8_DTYPE)
        key = jax.random.key(seed)
        kx, kw = jax.random.split(key)
        B, N, C, F = (8, 1024, 256, 256)
        x = jax.random.normal(kx, (B, N, C), dtype=jnp.float32)
        weight = jax.random.normal(kw, (F, C), dtype=jnp.float32) * 0.02
        bias = jnp.zeros((F,), dtype=jnp.float32)
        return {'x': x, 'weight': weight, 'bias': bias}
    _L0_ffn_all = _L0_ffn_setup()
    _L0_ffn_in = {k: v for k, v in _L0_ffn_all.items() if k in ('weight', 'bias')}
    del _L0_ffn_all

    def _L1_cond_setup():
        import jax, jax.numpy as jnp
        import numpy as np
        EPS = 1e-05

        def _ln(x, g, b):
            m = jnp.mean(x, axis=-1, keepdims=True)
            v = jnp.mean((x - m) ** 2, axis=-1, keepdims=True)
            return (x - m) * jax.lax.rsqrt(v + EPS) * g + b

        def _mlp_ln(s, W1, b1, W2, b2, g, b):
            h = jax.nn.silu(s @ W1 + b1) @ W2 + b2
            return _ln(h, g, b)
        key = jax.random.key(seed)
        B, S, D = (4, 512, 256)
        MEM, NOI, RES = (128, 64, 32)
        ks = jax.random.split(key, 40)
        ki = iter(range(40))

        def nrm(shape, scale=0.02):
            return jax.random.normal(ks[next(ki)], shape, jnp.float32) * scale

        def gamma(shape):
            return jnp.ones(shape, jnp.float32) + nrm(shape)
        inp = {'x': jax.random.normal(ks[next(ki)], (B, S, D), jnp.float32), 'pathway_ids': jax.random.randint(ks[next(ki)], (B, S), 0, 250), 'compartment_ids': jax.random.randint(ks[next(ki)], (B, S), 0, 5), 'time_steps': jax.random.randint(ks[next(ki)], (B, S), 0, 5), 'scale_type': jax.random.randint(ks[next(ki)], (B, S), 0, 3), 'memory_state': jax.random.normal(ks[next(ki)], (B, MEM), jnp.float32), 'noise_state': jax.random.normal(ks[next(ki)], (B, NOI), jnp.float32), 'resource_state': jax.random.normal(ks[next(ki)], (B, RES), jnp.float32), 'pw_g': gamma((250, D)), 'pw_b': nrm((250, D)), 'cp_g': gamma((5, D)), 'cp_b': nrm((5, D)), 'tm_g': gamma((5, D)), 'tm_b': nrm((5, D)), 'ms_g': gamma((3, D)), 'ms_b': nrm((3, D)), 'mem_W1': nrm((MEM, D)), 'mem_b1': jnp.zeros((D,)), 'mem_W2': nrm((D, D)), 'mem_b2': jnp.zeros((D,)), 'mem_g': gamma((D,)), 'mem_be': jnp.zeros((D,)), 'noi_W1': nrm((NOI, D)), 'noi_b1': jnp.zeros((D,)), 'noi_W2': nrm((D, D)), 'noi_b2': jnp.zeros((D,)), 'noi_g': gamma((D,)), 'noi_be': jnp.zeros((D,)), 'res_W1': nrm((RES, D)), 'res_b1': jnp.zeros((D,)), 'res_W2': nrm((D, D)), 'res_b2': jnp.zeros((D,)), 'res_g': gamma((D,)), 'res_be': jnp.zeros((D,)), 'int_W1': nrm((6 * D, D)), 'int_b1': jnp.zeros((D,)), 'int_W2': nrm((D, D)), 'int_b2': jnp.zeros((D,)), 'int_g': gamma((D,)), 'int_be': jnp.zeros((D,)), 'aw': jnp.ones((6,), jnp.float32) / 6.0}
        return inp
    _L1_cond_all = _L1_cond_setup()
    _L1_cond_in = {k: v for k, v in _L1_cond_all.items() if k in ('pw_g', 'pw_b', 'cp_g', 'cp_b', 'tm_g', 'tm_b', 'ms_g', 'ms_b', 'mem_W1', 'mem_b1', 'mem_W2', 'mem_b2', 'mem_g', 'mem_be', 'noi_W1', 'noi_b1', 'noi_W2', 'noi_b2', 'noi_g', 'noi_be', 'res_W1', 'res_b1', 'res_W2', 'res_b2', 'res_g', 'res_be', 'int_W1', 'int_b1', 'int_W2', 'int_b2', 'int_g', 'int_be', 'aw')}
    del _L1_cond_all

    def _L1_attn_setup():
        import jax, jax.numpy as jnp
        import numpy as np
        D = 256
        N_HEAD = 16
        D_HEAD = D // N_HEAD
        EPS = 1e-06

        def _rmsnorm_global(x, scale):
            rms = jnp.sqrt(jnp.mean(x * x))
            return x / (rms + EPS) * scale
        key = jax.random.key(seed)
        k1, k2, k3 = jax.random.split(key, 3)
        x = jax.random.normal(k1, (4, 256, D), dtype=jnp.float32)
        Wqkv = jax.random.normal(k2, (D, 3 * D), dtype=jnp.float32) * (1.0 / np.sqrt(D))
        Wo = jax.random.normal(k3, (D, D), dtype=jnp.float32) * (1.0 / np.sqrt(D))
        scale_q = jnp.ones((D_HEAD,), dtype=jnp.float32)
        scale_k = jnp.ones((D_HEAD,), dtype=jnp.float32)
        return {'x': x, 'Wqkv': Wqkv, 'Wo': Wo, 'scale_q': scale_q, 'scale_k': scale_k}
    _L1_attn_all = _L1_attn_setup()
    _L1_attn_in = {k: v for k, v in _L1_attn_all.items() if k in ('Wqkv', 'Wo', 'scale_q', 'scale_k')}
    del _L1_attn_all

    def _L1_cond2_setup():
        import jax, jax.numpy as jnp
        import numpy as np
        IN_DIM = 256
        OUT_DIM = 256
        MU_DIM = 128
        K = 30
        key = jax.random.key(seed)
        k1, k2, k3, k4, k5 = jax.random.split(key, 5)
        B, S = (16, 512)
        x = jax.random.normal(k1, (B, S, IN_DIM), dtype=jnp.float32)
        mu = jax.random.normal(k2, (B, MU_DIM), dtype=jnp.float32)
        W_dec = jax.random.normal(k3, (MU_DIM, (IN_DIM + 1) * K), dtype=jnp.float32) / np.sqrt(MU_DIM)
        b_dec = jax.random.normal(k4, ((IN_DIM + 1) * K,), dtype=jnp.float32) * 0.01
        V = jax.random.normal(k5, (K, OUT_DIM), dtype=jnp.float32) / np.sqrt(K)
        return {'x': x, 'mu': mu, 'W_dec': W_dec, 'b_dec': b_dec, 'V': V}
    _L1_cond2_all = _L1_cond2_setup()
    _L1_cond2_in = {k: v for k, v in _L1_cond2_all.items() if k in ('W_dec', 'b_dec', 'V')}
    del _L1_cond2_all

    def _L1_ffn_setup():
        import jax, jax.numpy as jnp
        import numpy as np
        TEMPERATURE = 0.5
        CAPACITY_FACTOR = 1.25
        TOP_K = 1
        key = jax.random.key(seed)
        ks = jax.random.split(key, 5)
        B, S, D, H, E = (4, 512, 256, 512, 8)
        s = 0.02
        return {'x': jax.random.normal(ks[0], (B, S, D), jnp.float32), 'gate_w': jax.random.normal(ks[1], (E, D), jnp.float32) * s, 'gate_b': jnp.zeros((E,), jnp.float32), 'rms_w': jnp.ones((E,), jnp.float32), 'w1': jax.random.normal(ks[2], (E, D, H), jnp.float32) * s, 'b1': jnp.zeros((E, H), jnp.float32), 'w2': jax.random.normal(ks[3], (E, H, D), jnp.float32) * s, 'b2': jnp.zeros((E, D), jnp.float32)}
    _L1_ffn_all = _L1_ffn_setup()
    _L1_ffn_in = {k: v for k, v in _L1_ffn_all.items() if k in ('gate_w', 'gate_b', 'rms_w', 'w1', 'b1', 'w2', 'b2')}
    del _L1_ffn_all
    return {'x': x, 'cond_512': cond_512, 'itok_BxS_0_999': itok_BxS_0_999, 'itok_BxS_0_4': itok_BxS_0_4, 'cond_64': cond_64, 'fside_Bx32_0': fside_Bx32_0, 'mask_BxS_ik0': mask_BxS_ik0, 'L0_cond_k_aff_w': _L0_cond_in['k_aff_w'], 'L0_cond_k_aff_b': _L0_cond_in['k_aff_b'], 'L0_cond_k_w': _L0_cond_in['k_w'], 'L0_cond_k_b': _L0_cond_in['k_b'], 'L0_cond_o_aff_w': _L0_cond_in['o_aff_w'], 'L0_cond_o_aff_b': _L0_cond_in['o_aff_b'], 'L0_cond_o_w': _L0_cond_in['o_w'], 'L0_cond_o_b': _L0_cond_in['o_b'], 'L0_attn_gamma': _L0_attn_in['gamma'], 'L0_attn_beta': _L0_attn_in['beta'], 'L0_attn_W_in': _L0_attn_in['W_in'], 'L0_attn_conv_w': _L0_attn_in['conv_w'], 'L0_attn_conv_b': _L0_attn_in['conv_b'], 'L0_attn_W_x': _L0_attn_in['W_x'], 'L0_attn_W_dt': _L0_attn_in['W_dt'], 'L0_attn_b_dt': _L0_attn_in['b_dt'], 'L0_attn_A_log': _L0_attn_in['A_log'], 'L0_attn_D': _L0_attn_in['D'], 'L0_attn_W_out': _L0_attn_in['W_out'], 'L0_cond2_weight': _L0_cond2_in['weight'], 'L0_cond2_bias': _L0_cond2_in['bias'], 'L0_cond2_affine_w': _L0_cond2_in['affine_w'], 'L0_cond2_affine_b': _L0_cond2_in['affine_b'], 'L0_ffn_weight': _L0_ffn_in['weight'], 'L0_ffn_bias': _L0_ffn_in['bias'], 'L1_cond_pw_g': _L1_cond_in['pw_g'], 'L1_cond_pw_b': _L1_cond_in['pw_b'], 'L1_cond_cp_g': _L1_cond_in['cp_g'], 'L1_cond_cp_b': _L1_cond_in['cp_b'], 'L1_cond_tm_g': _L1_cond_in['tm_g'], 'L1_cond_tm_b': _L1_cond_in['tm_b'], 'L1_cond_ms_g': _L1_cond_in['ms_g'], 'L1_cond_ms_b': _L1_cond_in['ms_b'], 'L1_cond_mem_W1': _L1_cond_in['mem_W1'], 'L1_cond_mem_b1': _L1_cond_in['mem_b1'], 'L1_cond_mem_W2': _L1_cond_in['mem_W2'], 'L1_cond_mem_b2': _L1_cond_in['mem_b2'], 'L1_cond_mem_g': _L1_cond_in['mem_g'], 'L1_cond_mem_be': _L1_cond_in['mem_be'], 'L1_cond_noi_W1': _L1_cond_in['noi_W1'], 'L1_cond_noi_b1': _L1_cond_in['noi_b1'], 'L1_cond_noi_W2': _L1_cond_in['noi_W2'], 'L1_cond_noi_b2': _L1_cond_in['noi_b2'], 'L1_cond_noi_g': _L1_cond_in['noi_g'], 'L1_cond_noi_be': _L1_cond_in['noi_be'], 'L1_cond_res_W1': _L1_cond_in['res_W1'], 'L1_cond_res_b1': _L1_cond_in['res_b1'], 'L1_cond_res_W2': _L1_cond_in['res_W2'], 'L1_cond_res_b2': _L1_cond_in['res_b2'], 'L1_cond_res_g': _L1_cond_in['res_g'], 'L1_cond_res_be': _L1_cond_in['res_be'], 'L1_cond_int_W1': _L1_cond_in['int_W1'], 'L1_cond_int_b1': _L1_cond_in['int_b1'], 'L1_cond_int_W2': _L1_cond_in['int_W2'], 'L1_cond_int_b2': _L1_cond_in['int_b2'], 'L1_cond_int_g': _L1_cond_in['int_g'], 'L1_cond_int_be': _L1_cond_in['int_be'], 'L1_cond_aw': _L1_cond_in['aw'], 'L1_attn_Wqkv': _L1_attn_in['Wqkv'], 'L1_attn_Wo': _L1_attn_in['Wo'], 'L1_attn_scale_q': _L1_attn_in['scale_q'], 'L1_attn_scale_k': _L1_attn_in['scale_k'], 'L1_cond2_W_dec': _L1_cond2_in['W_dec'], 'L1_cond2_b_dec': _L1_cond2_in['b_dec'], 'L1_cond2_V': _L1_cond2_in['V'], 'L1_ffn_gate_w': _L1_ffn_in['gate_w'], 'L1_ffn_gate_b': _L1_ffn_in['gate_b'], 'L1_ffn_rms_w': _L1_ffn_in['rms_w'], 'L1_ffn_w1': _L1_ffn_in['w1'], 'L1_ffn_b1': _L1_ffn_in['b1'], 'L1_ffn_w2': _L1_ffn_in['w2'], 'L1_ffn_b2': _L1_ffn_in['b2']}

def reference(x, cond_512, itok_BxS_0_999, itok_BxS_0_4, cond_64, fside_Bx32_0, mask_BxS_ik0, L0_cond_k_aff_w, L0_cond_k_aff_b, L0_cond_k_w, L0_cond_k_b, L0_cond_o_aff_w, L0_cond_o_aff_b, L0_cond_o_w, L0_cond_o_b, L0_attn_gamma, L0_attn_beta, L0_attn_W_in, L0_attn_conv_w, L0_attn_conv_b, L0_attn_W_x, L0_attn_W_dt, L0_attn_b_dt, L0_attn_A_log, L0_attn_D, L0_attn_W_out, L0_cond2_weight, L0_cond2_bias, L0_cond2_affine_w, L0_cond2_affine_b, L0_ffn_weight, L0_ffn_bias, L1_cond_pw_g, L1_cond_pw_b, L1_cond_cp_g, L1_cond_cp_b, L1_cond_tm_g, L1_cond_tm_b, L1_cond_ms_g, L1_cond_ms_b, L1_cond_mem_W1, L1_cond_mem_b1, L1_cond_mem_W2, L1_cond_mem_b2, L1_cond_mem_g, L1_cond_mem_be, L1_cond_noi_W1, L1_cond_noi_b1, L1_cond_noi_W2, L1_cond_noi_b2, L1_cond_noi_g, L1_cond_noi_be, L1_cond_res_W1, L1_cond_res_b1, L1_cond_res_W2, L1_cond_res_b2, L1_cond_res_g, L1_cond_res_be, L1_cond_int_W1, L1_cond_int_b1, L1_cond_int_W2, L1_cond_int_b2, L1_cond_int_g, L1_cond_int_be, L1_cond_aw, L1_attn_Wqkv, L1_attn_Wo, L1_attn_scale_q, L1_attn_scale_k, L1_cond2_W_dec, L1_cond2_b_dec, L1_cond2_V, L1_ffn_gate_w, L1_ffn_gate_b, L1_ffn_rms_w, L1_ffn_w1, L1_ffn_b1, L1_ffn_w2, L1_ffn_b2):
    import jax
    import jax.numpy as jnp

    def _L0_cond_ref(x, s, k_aff_w, k_aff_b, k_w, k_b, o_aff_w, o_aff_b, o_w, o_b):
        import jax, jax.numpy as jnp
        import numpy as np
        import math
        HEAD_NUM = 16
        EPS = 1e-08

        def modulated_linear(x, s, aff_w, aff_b, w, b):
            style = s @ aff_w.T + aff_b
            w_mod = w[None, :, :] * style[:, None, :]
            demod = jax.lax.rsqrt(jnp.sum(w_mod * w_mod, axis=2) + EPS)
            w_mod = w_mod * demod[:, :, None]
            return jnp.einsum('bni,boi->bno', x, w_mod) + b
        B, N, F = x.shape
        H = HEAD_NUM
        D = F // H
        kx = modulated_linear(x, s, k_aff_w, k_aff_b, k_w, k_b)
        kx = kx.reshape(B, N, H, D)
        q = k = v = kx
        scores = jnp.einsum('bnhd,bnjd->bnhj', q, k) / math.sqrt(D)
        A = jax.nn.softmax(scores, axis=-1)
        out = jnp.einsum('bnhj,bnjd->bnhd', A, v).reshape(B, N, F)
        out = modulated_linear(out, s, o_aff_w, o_aff_b, o_w, o_b)
        return out

    def _L0_attn_ref(x, gamma, beta, W_in, conv_w, conv_b, W_x, W_dt, b_dt, A_log, D, W_out):
        import jax, jax.numpy as jnp
        import numpy as np
        D_MODEL = 256
        D_STATE = 16
        D_CONV = 4
        EXPAND = 2
        D_INNER = EXPAND * D_MODEL
        DT_RANK = D_MODEL // 16
        EPS = 1e-05

        def _mamba_block(x, gamma, beta, W_in, conv_w, conv_b, W_x, W_dt, b_dt, A_log, D, W_out):
            mu = x.mean(-1, keepdims=True)
            var = ((x - mu) ** 2).mean(-1, keepdims=True)
            xn = (x - mu) * jax.lax.rsqrt(var + EPS) * gamma + beta
            xz = xn @ W_in
            u, z = jnp.split(xz, 2, axis=-1)
            uc = jax.lax.conv_general_dilated(u.transpose(0, 2, 1), conv_w[:, None, :], window_strides=(1,), padding=[(D_CONV - 1, 0)], feature_group_count=D_INNER, dimension_numbers=('NCH', 'OIH', 'NCH'))
            u2 = jax.nn.silu(uc.transpose(0, 2, 1) + conv_b)
            dbl = u2 @ W_x
            dt_low = dbl[..., :DT_RANK]
            Bm = dbl[..., DT_RANK:DT_RANK + D_STATE]
            Cm = dbl[..., DT_RANK + D_STATE:]
            dt = jax.nn.softplus(dt_low @ W_dt + b_dt)
            A = -jnp.exp(A_log)

            def step(h, inp):
                dt_t, B_t, C_t, u_t = inp
                dA = jnp.exp(dt_t[:, :, None] * A)
                h = dA * h + (dt_t * u_t)[:, :, None] * B_t[:, None, :]
                y = jnp.einsum('bdn,bn->bd', h, C_t)
                return (h, y)
            Bb = x.shape[0]
            h0 = jnp.zeros((Bb, D_INNER, D_STATE), x.dtype)
            xs = (dt.transpose(1, 0, 2), Bm.transpose(1, 0, 2), Cm.transpose(1, 0, 2), u2.transpose(1, 0, 2))
            _, ys = jax.lax.scan(step, h0, xs)
            y = ys.transpose(1, 0, 2) + u2 * D
            y = y * jax.nn.silu(z)
            out = y @ W_out
            return x + out
        return _mamba_block(x, gamma, beta, W_in, conv_w, conv_b, W_x, W_dt, b_dt, A_log, D, W_out)

    def _L0_cond2_ref(x, w, weight, bias, affine_w, affine_b):
        import jax, jax.numpy as jnp
        import numpy as np
        W_DIM = 128
        CLAMP = 256.0
        B, L, C = x.shape
        gain = 1.0 / np.sqrt(W_DIM).astype(np.float32)
        styles = w @ (affine_w * gain).T + affine_b
        ws = weight[None, :, :] * styles[:, None, :]
        dcoefs = jax.lax.rsqrt(jnp.sum(ws * ws, axis=2) + 1e-08)
        xm = x * styles[:, None, :]
        y = jnp.einsum('blc,oc->blo', xm, weight)
        y = y * dcoefs[:, None, :]
        y = jnp.clip(y + bias, -CLAMP, CLAMP)
        return y

    def _L0_ffn_ref(x, weight, bias):
        import jax, jax.numpy as jnp
        import numpy as np
        FP8_MAX = 448.0
        SCALE = 1.0
        _FP8_DTYPE = getattr(jnp, 'float8_e4m3fn', jnp.float16)

        def quantize_e4m3(t, scale):
            return jnp.clip(t / scale, -FP8_MAX, FP8_MAX).astype(_FP8_DTYPE)
        B, N, C = x.shape
        x2d = x.reshape(B * N, C)
        x_mat = quantize_e4m3(x2d, SCALE).astype(jnp.float16)
        w_mat = quantize_e4m3(weight, SCALE).astype(jnp.float16)
        out2d = (x_mat @ w_mat.T).astype(jnp.float32) * (SCALE * SCALE)
        out2d = out2d + bias
        return out2d.reshape(B, N, -1)

    def _L1_cond_ref(x, pathway_ids, compartment_ids, time_steps, scale_type, memory_state, noise_state, resource_state, pw_g, pw_b, cp_g, cp_b, tm_g, tm_b, ms_g, ms_b, mem_W1, mem_b1, mem_W2, mem_b2, mem_g, mem_be, noi_W1, noi_b1, noi_W2, noi_b2, noi_g, noi_be, res_W1, res_b1, res_W2, res_b2, res_g, res_be, int_W1, int_b1, int_W2, int_b2, int_g, int_be, aw):
        import jax, jax.numpy as jnp
        import numpy as np
        EPS = 1e-05

        def _ln(x, g, b):
            m = jnp.mean(x, axis=-1, keepdims=True)
            v = jnp.mean((x - m) ** 2, axis=-1, keepdims=True)
            return (x - m) * jax.lax.rsqrt(v + EPS) * g + b

        def _mlp_ln(s, W1, b1, W2, b2, g, b):
            h = jax.nn.silu(s @ W1 + b1) @ W2 + b2
            return _ln(h, g, b)
        h = _ln(x, pw_g[pathway_ids], pw_b[pathway_ids])
        h = _ln(h, cp_g[compartment_ids], cp_b[compartment_ids])
        t = _ln(x, tm_g[time_steps], tm_b[time_steps])
        m = x + _mlp_ln(memory_state, mem_W1, mem_b1, mem_W2, mem_b2, mem_g, mem_be)[:, None, :]
        n = x + _mlp_ln(noise_state, noi_W1, noi_b1, noi_W2, noi_b2, noi_g, noi_be)[:, None, :]
        r = x + _mlp_ln(resource_state, res_W1, res_b1, res_W2, res_b2, res_g, res_be)[:, None, :]
        s = _ln(x, ms_g[scale_type], ms_b[scale_type])
        w = jax.nn.softmax(aw)
        cat = jnp.concatenate([w[0] * h, w[1] * t, w[2] * m, w[3] * n, w[4] * r, w[5] * s], axis=-1)
        return _mlp_ln(cat, int_W1, int_b1, int_W2, int_b2, int_g, int_be)

    def _L1_attn_ref(x, Wqkv, Wo, scale_q, scale_k):
        import jax, jax.numpy as jnp
        import numpy as np
        D = 256
        N_HEAD = 16
        D_HEAD = D // N_HEAD
        EPS = 1e-06

        def _rmsnorm_global(x, scale):
            rms = jnp.sqrt(jnp.mean(x * x))
            return x / (rms + EPS) * scale
        b, s, d = x.shape
        qkv = x @ Wqkv
        q, k, v = jnp.split(qkv, 3, axis=-1)
        q = q.reshape(b, s, N_HEAD, D_HEAD)
        k = k.reshape(b, s, N_HEAD, D_HEAD)
        v = v.reshape(b, s, N_HEAD, D_HEAD)
        q = _rmsnorm_global(q, scale_q)
        k = _rmsnorm_global(k, scale_k)
        attn = jnp.einsum('bqhd,bkhd->bhqk', q, k)
        attn = jax.nn.softmax(attn, axis=-1)
        z = jnp.einsum('bhqk,bkhd->bqhd', attn, v)
        z = z.reshape(b, s, d)
        return z @ Wo

    def _L1_cond2_ref(x, mu, W_dec, b_dec, V):
        import jax, jax.numpy as jnp
        import numpy as np
        IN_DIM = 256
        OUT_DIM = 256
        MU_DIM = 128
        K = 30
        B = mu.shape[0]
        U = (mu @ W_dec + b_dec).reshape(B, IN_DIM + 1, K)
        param = jnp.einsum('bik,kj->bij', U, V)
        weight = param[:, :-1, :]
        bias = param[:, -1, :]
        out = jnp.einsum('bsd,bde->bse', x, weight)
        out = out + bias[:, None, :]
        return out

    def _L1_ffn_ref(x, gate_w, gate_b, rms_w, w1, b1, w2, b2):
        import jax, jax.numpy as jnp
        import numpy as np
        TEMPERATURE = 0.5
        CAPACITY_FACTOR = 1.25
        TOP_K = 1
        B, S, D = x.shape
        E = gate_w.shape[0]
        xf = x.reshape(-1, D)
        N = xf.shape[0]
        logits = xf @ gate_w.T + gate_b
        eps = jnp.finfo(logits.dtype).eps
        ms = jnp.mean(logits * logits, axis=-1, keepdims=True)
        logits = logits * jax.lax.rsqrt(ms + eps) * rms_w
        gates = jax.nn.softmax(logits / TEMPERATURE, axis=-1)
        g, idx = jax.lax.top_k(gates, TOP_K)
        g, idx = (g[:, 0], idx[:, 0])
        capacity = min(int(np.ceil(N * TOP_K / E * CAPACITY_FACTOR)), N)
        counts = jnp.zeros((E,), jnp.int32).at[idx].add(1)
        active = (counts > 0) & (capacity >= 1)
        mask = active[idx].astype(gates.dtype)
        masked = g * mask
        norm_g = masked / (masked + 1e-06)
        h = jax.nn.gelu(jnp.einsum('nd,edh->neh', xf, w1) + b1, approximate=False)
        y = jnp.einsum('neh,ehd->ned', h, w2) + b2
        out = (y * norm_g[:, None, None]).sum(axis=1)
        return out.reshape(B, S, D)
    x = x + _L0_attn_ref(_L0_cond_ref(x, cond_512, L0_cond_k_aff_w, L0_cond_k_aff_b, L0_cond_k_w, L0_cond_k_b, L0_cond_o_aff_w, L0_cond_o_aff_b, L0_cond_o_w, L0_cond_o_b), L0_attn_gamma, L0_attn_beta, L0_attn_W_in, L0_attn_conv_w, L0_attn_conv_b, L0_attn_W_x, L0_attn_W_dt, L0_attn_b_dt, L0_attn_A_log, L0_attn_D, L0_attn_W_out)
    x = x + _L0_ffn_ref(_L0_cond2_ref(x, cond_512, L0_cond2_weight, L0_cond2_bias, L0_cond2_affine_w, L0_cond2_affine_b), L0_ffn_weight, L0_ffn_bias)
    x = x + _L1_attn_ref(_L1_cond_ref(x, itok_BxS_0_999, itok_BxS_0_4, itok_BxS_0_4, mask_BxS_ik0, cond_512, cond_64, fside_Bx32_0, L1_cond_pw_g, L1_cond_pw_b, L1_cond_cp_g, L1_cond_cp_b, L1_cond_tm_g, L1_cond_tm_b, L1_cond_ms_g, L1_cond_ms_b, L1_cond_mem_W1, L1_cond_mem_b1, L1_cond_mem_W2, L1_cond_mem_b2, L1_cond_mem_g, L1_cond_mem_be, L1_cond_noi_W1, L1_cond_noi_b1, L1_cond_noi_W2, L1_cond_noi_b2, L1_cond_noi_g, L1_cond_noi_be, L1_cond_res_W1, L1_cond_res_b1, L1_cond_res_W2, L1_cond_res_b2, L1_cond_res_g, L1_cond_res_be, L1_cond_int_W1, L1_cond_int_b1, L1_cond_int_W2, L1_cond_int_b2, L1_cond_int_g, L1_cond_int_be, L1_cond_aw), L1_attn_Wqkv, L1_attn_Wo, L1_attn_scale_q, L1_attn_scale_k)
    x = x + _L1_ffn_ref(_L1_cond2_ref(x, cond_512, L1_cond2_W_dec, L1_cond2_b_dec, L1_cond2_V), L1_ffn_gate_w, L1_ffn_gate_b, L1_ffn_rms_w, L1_ffn_w1, L1_ffn_b1, L1_ffn_w2, L1_ffn_b2)
    return x

_drawn_inputs = setup_inputs


def setup_inputs(seed=0):
    import zlib

    import numpy as np

    out = dict(_drawn_inputs(seed))
    spreads = {'L0_cond_k_aff_b': (1.0, 0.2),
     'L0_cond_k_b': (0.0, 0.1),
     'L0_cond_o_aff_b': (1.0, 0.2),
     'L0_cond_o_b': (0.0, 0.1),
     'L0_attn_gamma': (1.0, 0.2),
     'L0_attn_beta': (0.0, 0.1),
     'L0_attn_conv_b': (0.0, 0.1),
     'L0_attn_b_dt': (-4.600166320800781, 0.2),
     'L0_attn_D': (1.0, 0.2),
     'L0_cond2_affine_b': (1.0, 0.2),
     'L0_ffn_bias': (0.0, 0.1),
     'L1_cond_mem_b1': (0.0, 0.1),
     'L1_cond_mem_b2': (0.0, 0.1),
     'L1_cond_mem_be': (0.0, 0.1),
     'L1_cond_noi_b1': (0.0, 0.1),
     'L1_cond_noi_b2': (0.0, 0.1),
     'L1_cond_noi_be': (0.0, 0.1),
     'L1_cond_res_b1': (0.0, 0.1),
     'L1_cond_res_b2': (0.0, 0.1),
     'L1_cond_res_be': (0.0, 0.1),
     'L1_cond_int_b1': (0.0, 0.1),
     'L1_cond_int_b2': (0.0, 0.1),
     'L1_cond_int_be': (0.0, 0.1),
     'L1_cond_aw': (0.1666666716337204, 0.2),
     'L1_attn_scale_q': (1.0, 0.2),
     'L1_attn_scale_k': (1.0, 0.2),
     'L1_ffn_gate_b': (0.0, 0.1),
     'L1_ffn_rms_w': (1.0, 0.2),
     'L1_ffn_b1': (0.0, 0.1),
     'L1_ffn_b2': (0.0, 0.1)}
    factors = {}
    for name, (base, spread) in spreads.items():
        noise = np.random.default_rng([zlib.crc32(name.encode()), seed]).standard_normal(out[name].shape)
        drawn = base * np.exp(spread * noise) if base else spread * noise
        out[name] = jnp.asarray(drawn.astype(out[name].dtype))
    for name, factor in factors.items():
        out[name] = (out[name] * factor).astype(out[name].dtype)
    return out
```

```python
from contextlib import ExitStack

import numpy as np

import concourse.bass as bass
from concourse import mybir

F32 = mybir.dt.float32
BF16 = mybir.dt.bfloat16
F16 = mybir.dt.float16
FP8 = mybir.dt.float8e4
I32 = mybir.dt.int32
ALU = mybir.AluOpType
ACT = mybir.ActivationFunctionType
AX = mybir.AxisListType.X

P = 128
B, S, D = 4, 512, 256
N = B * S
C = D // P
H, DH = 16, 16
TILES = S // P
DI, NS, RANK, TAPS = 512, 16, 16, 4
M = DI // P
G = 2
PW, CP, MS = 250, 5, 3
PWK = PW // 2
KU = 30
E, FH = 8, 512
FM = E * FH // P
SLOT = 32
HG = P // SLOT
NEG_EPS_LN = 1e-5


def layout(fields):
    at, out = 0, {}
    for name, width in fields:
        out[name] = (at, width)
        at += width
    return out, at


EARLY, EARLY_W = layout([
    ("condT", B), ("k_aff", D), ("o_aff", D), ("c2_aff", D), ("k_affb", C), ("o_affb", C), ("c2_affb", C),
    ("k_w", C * D), ("ident", P), ("mean", P), ("k_b", D), ("ones", P), ("o_w", C * D), ("o_b", C)])
MAMBA, MAMBA_W = layout([
    ("gamma", C), ("beta", C), ("w_u", C * DI), ("conv", TAPS * DI), ("w_z", C * DI), ("conv_b", M),
    ("w_x", M * 48), ("w_dt", DI), ("b_dt", M), ("a_log", M * NS), ("d", M), ("w_out", M * D)])
COND, COND_W = layout([
    ("c2_w", C * D), ("c2_b", C), ("ffn_w", C * D), ("ffn_b", C),
    ("pw", 2 * 2 * D), ("cp", 4 * D), ("ms", 2 * D), ("rows", 2), ("aw", 6),
    ("v_in", 3 * B), ("v_w1", 3 * D), ("v_w2", 3 * C * D), ("v_b1", 3 * C), ("v_b2", 3 * C),
    ("v_g", 3 * C), ("v_be", 3 * C),
    ("i_w1", 6 * C * D), ("i_w2", C * D), ("i_b1", C), ("i_b2", C), ("i_g", C), ("i_be", C),
    ("w_q", C * HG * P), ("w_k", C * HG * P), ("w_v", C * HG * P), ("v_one", HG * P), ("s_q", 1), ("s_k", 1), ("slot_one", 1)])
FFN, FFN_W = layout([
    ("w_o", C * D), ("v_dec", D), ("gate_w", C * E), ("gate_b", E), ("rms_w", E), ("b1", FM), ("b2", C * E),
    ("w1", C * E * FH), ("w2", FM * D)])
UD = (D + 1) * KU


def view(ap, dims, off=0):
    return bass.AP(ap.tensor, ap.offset + off, [list(ap.ap[0])] + [list(d) for d in dims])


def tok(b, n=S):
    return bass.ds(b * n, n)


def program(nc, t_in, out, dbg=()):
    ctx = ExitStack()
    with ctx:
        def sb(name, shape, dt=F32):
            return ctx.enter_context(nc.sbuf_tensor(name, shape, dt))

        def sem(name):
            return ctx.enter_context(nc.semaphore(name))

        ps = ctx.enter_context(nc.psum_tensor("ps", [P, 8, 512], F32))

        early = sb("early", [P, EARLY_W])
        xT = sb("xT", [P, C, N])
        hT = sb("hT", [P, C, N])
        arena = sb("arena", [P, ARENA])

        def fields(tensor, spec, base=0):
            return {k: tensor[:, base + a:base + a + w] for k, (a, w) in spec.items()}

        w = fields(early, EARLY)
        k_w = w["k_w"].rearrange("p (c o) -> p c o", c=C)
        o_w = w["o_w"].rearrange("p (c o) -> p c o", c=C)
        ident, ones, mean = w["ident"], w["ones"], w["mean"]

        def carve(at, *shape):
            n = int(np.prod(shape))
            assert at + n <= ARENA, (at + n, ARENA)
            flat = arena[:, at:at + n]
            dims, st = [], n
            for s in shape:
                st //= s
                dims.append([st, s])
            return view(flat, dims), at + n

        style = sb("style", [P, 3, C, B])
        style2 = sb("style2", [P, 3, C, B])
        dem = sb("dem", [P, 2, C, B])
        eps = sb("eps", [P, 3])
        at = 0
        w2k, at = carve(at, C, D)
        w2o, at = carve(at, C, D)
        demk, at = carve(at, B, D)
        kw_mod, at = carve(at, B, C, D)
        xb, at = carve(at, C, S)
        kx, at = carve(at, 2, 2 * D)
        prod, at = carve(at, 2, DH, D)
        diff, at = carve(at, 2, D)
        att, at = carve(at, 2, D)
        att_p, at = carve(at, 2, D)
        mx, at = carve(at, 2, H)
        ssum, at = carve(at, 2, H)
        mix, at = carve(at, 2, H, D)
        aoT, at = carve(at, 2, C, S)
        stage1_end = at

        s_early = sem("early_loaded")
        s_x = sem("x_loaded")
        s_style_mm = sem("style_products")
        s_style = sem("style_ready")
        s_sq = sem("squares_ready")
        s_dem_mm = sem("demod_products")
        s_dem_ln = sem("demod_ready")
        s_kw = sem("kw_ready")
        s_xb = sem("xb_loaded")
        s_kx_mm = sem("kx_products")
        s_kx = sem("kx_ready")
        s_prod = sem("prod_ready")
        s_sc = sem("scores_ready")
        s_diff = sem("diff_ready")
        s_exp = sem("exp_ready")
        s_att = sem("att_ready")
        s_mixv = sem("mix_by_vector")
        s_mixp = sem("mix_by_pool")
        s_ao_mm = sem("ao_products")
        s_ao = sem("ao_ready")
        s_o_mm = sem("o_products")
        s_h0 = sem("h0_ready")
        s_dbg = sem("dbg_out")

        POOL_SH = 10

        s_apart = sem("kept_apart")

        def apart(eng):
            eng.sem_inc(s_apart, 1)


        mam = sb("mam", [P, MAMBA_W])
        wm = fields(mam, MAMBA)
        w_u = wm["w_u"].rearrange("p (c o) -> p c o", c=C)
        w_z = wm["w_z"].rearrange("p (c o) -> p c o", c=C)
        w_x = wm["w_x"].rearrange("p (m o) -> p m o", m=M)
        w_out = wm["w_out"].rearrange("p (m o) -> p m o", m=M)
        a_neg = wm["a_log"]
        sz = wm["conv"].rearrange("p (m s) -> p m s", m=M)
        diag = sb("diag", [P, M, P])
        one = sb("one", [P, 1])
        at = 0
        u2, at = carve(at, M, N)
        dt, at = carve(at, M, N)
        xn, at = carve(at, B, C, S + TAPS - 1)
        head_at = at
        w_tap, at = carve(at, TAPS, C, DI)
        ln_xc, at = carve(at, C, S)
        ln_sq, at = carve(at, C, S)
        ln_rstd, at = carve(at, S)
        rest, _ = carve(head_at + TAPS * C * DI, M, S)
        dbl, at = carve(at, N)
        soft_e, at = carve(at, M, S)
        soft_l, at = carve(at, M, S)
        at = head_at
        decay, at = carve(at, 2, M, S)
        state, at = carve(at, 3, M, S)
        bc, at = carve(at, 2, 2, G, S)
        bc_dram = nc.dram_tensor("bc_scratch", (B, 2 * NS, S), F32, kind="Internal").ap()

        s_mam = sem("mamba_loaded")
        s_a = sem("a_exponent_ready")
        s_ln_mu = sem("ln_mean_product")
        s_ln_xc = sem("ln_centred")
        s_ln_sq = sem("ln_squared")
        s_ln_var = sem("ln_var_product")
        s_ln_rstd = sem("ln_rstd_ready")
        s_ln_out = sem("ln_scaled")
        s_tap = sem("taps_ready")
        s_u_mm = sem("u_products")
        s_u2 = sem("u2_ready")
        s_x_mm = sem("x_products")
        s_dbl = sem("dbl_ready")
        s_bc = sem("bc_written")
        s_dt_mm = sem("dt_products")
        s_soft = sem("softplus_parts")
        s_dt = sem("dt_ready")
        s_z_mm = sem("z_products")
        s_sz = sem("sz_ready")
        s_dterm = sem("d_term_product")
        s_du = sem("du_ready")
        s_bcl = [sem(f"bc_loaded{i}") for i in range(2)]
        s_decay = sem("decay_ready")
        s_dbu = sem("dbu_ready")
        s_scan = sem("scan_done")
        s_hc = sem("state_times_c")
        s_y = sem("y_accumulated")
        s_yz = sem("yz_ready")
        s_out_mm = sem("out_products")
        s_x1 = sem("x1_ready")


        UT = UD // 3
        dec_w = mam[:, 0:UT]
        dec_b = mam[0:1, UT:2 * UT]
        hflat = hT[:, :, :].rearrange("p c n -> p (c n)")
        u_rows = hflat[0:B, 0:UT]
        u_tall = view(hflat[:, UT:UT + C * B * KU], [[B * KU, C], [KU, B], [1, KU]])
        u_bias = view(hflat[0:1, UT + 256:UT + 256 + B * KU], [[KU, B], [1, KU]])
        u_t = view(hflat[0:KU, 3000:3000 + B * (D + 1)], [[D + 1, B], [1, D + 1]])
        u_dram = nc.dram_tensor("u_scratch", (B, UD), F32, kind="Internal").ap()
        s_dec = sem("decoder_loaded")
        s_u_mm3 = sem("decoder_products")
        s_u_rows = sem("u_rows_ready")
        s_u_out = sem("u_written")
        s_u_in = sem("u_read_back")
        s_u_tr = sem("u_transposed")
        s_u_t = sem("u_t_ready")

        at = 0
        cw, at = carve(at, COND_W)
        wc = {k: view(cw, [[1, n]], a) for k, (a, n) in COND.items()}
        cut = lambda name, *dims: view(wc[name], [[int(np.prod(dims[j + 1:])), d] for j, d in enumerate(dims)])
        c2_w, ffn_w = cut("c2_w", C, D), cut("ffn_w", C, D)
        pw_t, cp_t, ms_t = cut("pw", 2, 2, C, P), cut("cp", 2, 2, C, P), cut("ms", 2, C, P)
        i_w1, i_w2 = cut("i_w1", 6, C, D), cut("i_w2", C, D)
        w_q, w_k, w_v = (cut(x, C, HG * P) for x in ("w_q", "w_k", "w_v"))
        xm, at = carve(at, C, S)
        xh, at = carve(at, C, S)
        hh, at = carve(at, C, S)
        tt, at = carve(at, C, S)
        ss, at = carve(at, C, S)
        y3, at = carve(at, C, S)
        i1, at = carve(at, C, S)
        qs, at = carve(at, HG, S)
        w2c, at = carve(at, C, D)
        assert at <= head_at + TAPS * C * DI, at
        at = head_at + TAPS * C * DI + 5 * S
        ks, at = carve(at, HG, S)
        vs, at = carve(at, TILES, HG * P)
        oh_pw, at = carve(at, 2, S)
        oh_cp, at = carve(at, S)
        oh_ms, at = carve(at, S)
        wx, at = carve(at, C, D)
        ids = mam[:, 0:3 * S].bitcast(I32).rearrange("p (k s) -> p k s", k=3)

        def narrow(at, dtype, n):
            width = C * n * mybir.dt.size(dtype) // 4
            return arena[:, at:at + width].bitcast(dtype).rearrange("p (c s) -> p c s", c=C), at + width

        at3 = head_at + TAPS * C * DI + 5 * S
        q8, at3 = narrow(at3, FP8, S)
        q8b, at3 = narrow(at3, FP8, D)
        q8c, at3 = narrow(at3, FP8, D)
        low, at3 = narrow(at3, BF16, S)
        yq, at3 = narrow(at3, BF16, S)
        wq8, at3 = narrow(at3, BF16, D)
        f16, at3 = narrow(at3, F16, S)
        awn = sb("awn", [P, 8])
        vh = sb("vh", [P, 3, C, B])
        vz = sb("vz", [P, 3, C, B])
        vsq = sb("vsq", [P, 3, C, B])
        vr = sb("vr", [P, 3, B])
        cvec = sb("cvec", [P, C, B])
        sums = sb("sums", [P, 2, B])
        sqk = sb("sqk", [P, 1])
        rho = sb("rho", [P, 2])
        q_dram = nc.dram_tensor("q_scratch", (B, P, HG, S), F32, kind="Internal").ap()
        k_dram = nc.dram_tensor("k_scratch", (B, P, HG, S), F32, kind="Internal").ap()
        v_dram = nc.dram_tensor("v_scratch", (B, P, TILES, HG * P), F32, kind="Internal").ap()

        s_cond = sem("cond_loaded")
        s_prep = sem("prep_by_vector")
        s_prep_mm = sem("prep_products")
        s_prep_act = sem("prep_by_scalar")
        s_xm = sem("xm_ready")
        s_c2_mm = sem("c2_products")
        s_yq = sem("yq_ready")
        s_ffn_mm = sem("ffn_products")
        s_f16 = sem("f16_ready")
        s_x2 = sem("x2_ready")
        s_ids = sem("ids_loaded")
        s_oh = sem("onehot_ready")
        s_xh = sem("xh_ready")
        s_g_mm = sem("gathered")
        s_g_used = sem("gathered_used")
        s_h1 = sem("h1_ready")
        s_cat = sem("cat_ready")
        s_i1_mm = sem("i1_products")
        s_i1 = sem("i1_ready")
        s_i2_mm = sem("i2_products")
        s_i2 = sem("i2_ready")
        s_y3 = sem("y3_ready")
        s_q_mm = sem("q_products")
        s_k_mm = sem("k_products")
        s_v_mm = sem("v_products")
        s_qs = sem("q_ready")
        s_ks = sem("k_ready")
        s_vs = sem("v_ready")
        s_vt = sem("v_tile_copied")
        s_q_out = sem("q_written")
        s_k_out = sem("k_written")
        s_v_out = sem("v_written")

        at = 0
        fw, at = carve(at, FFN_W)
        wf = {k: view(fw, [[1, n]], a) for k, (a, n) in FFN.items()}
        fcut = lambda name, *dims: view(wf[name], [[int(np.prod(dims[j + 1:])), d] for j, d in enumerate(dims)])
        w_o = fcut("w_o", C, D)
        qa, at = carve(at, HG, S)
        ka, at = carve(at, HG, S)
        va, at = carve(at, TILES, HG * P)
        pt, at = carve(at, 2, 2, S)
        zt, at = carve(at, S)
        mxs, at = carve(at, TILES, P)
        zn, at = carve(at, TILES, D)
        zn_t, at = carve(at, C, S)
        zrec, at = carve(at, TILES, HG)
        stage4_end = at
        ssq = sb("ssq", [P, 2])
        s_fw = sem("w_o_loaded")
        s_ew = sem("expert_weights_loaded")
        s_rho_mm = sem("rho_product")
        s_rho_sum = sem("rho_mean_ready")
        s_rho_root = sem("rho_root_ready")
        s_rho = sem("rho_ready")
        s_att_in = sem("qkv_loaded")
        s_s_mm = sem("score_products")
        s_max = sem("max_ready")
        s_m_tr = sem("max_transposed")
        s_qm = sem("q_carries_max")
        s_t_mm = sem("scoreT_products")
        s_pt = sem("exp_scores_ready")
        s_pv = sem("value_products")
        s_zt = sem("z_copied")
        s_z_tr = sem("z_transposed")
        s_zn = sem("z_normalised")
        s_zn_tr = sem("zn_transposed")
        s_znt = sem("zn_copied")
        s_wo_mm = sem("attention_out_products")
        s_x3 = sem("x3_ready")

        at = FFN_W
        assert FFN_W + 8 * S * 2 < ARENA
        gate_w, w1, w2 = fcut("gate_w", C, E), fcut("w1", C, E * FH), fcut("w2", FM, D)
        wgt_all, at = carve(at, B, C, D)
        wgt, at = carve(at, C, D)
        y4, at = carve(at, C, S)
        hid, at = carve(at, 4, S)
        ngb, at = carve(at, S)
        moe, at = carve(at, C, S)
        dbias = sb("dbias", [P, C, B])
        b2s = sb("b2s", [P, C])
        lg = sb("lg", [P, TILES, E])
        lg2 = sb("lg2", [P, TILES, E])
        gs = sb("gs", [P, 4, TILES])
        eps32 = sb("eps32", [P, 1])
        s_wgt_mm = sem("decoded_products")
        s_wgt_all = sem("decoded_ready")
        s_wgt = sem("decoded_copied")
        s_y4_mm = sem("y4_products")
        s_y4 = sem("y4_ready")
        s_gate_mm = sem("gate_products")
        s_gate_sq = sem("gate_squares")
        s_gate_r = sem("gate_rstd")
        s_gate_d = sem("gate_less_max")
        s_gate_e = sem("gate_exp")
        s_ng = sem("gate_factor")
        s_ngb_mm = sem("gate_factor_product")
        s_ngb = sem("gate_factor_spread")
        s_h_mm = sem("hidden_products")
        s_hid = sem("hidden_ready")
        s_e_mm = sem("expert_products")
        s_x4 = sem("x4_ready")
        s_out = sem("out_written")

        def ln_tensor(pe, x, k):
            pe.wait_ge(s_ln_xc, k + 1)
            for c in range(C):
                last = pe.matmul(ps[:, 6, :], mean, x[:, c, :], start=(c == 0), stop=(c == C - 1))
            last.then_inc(s_ln_mu, 1)
            pe.wait_ge(s_ln_sq, k + 1)
            pe.wait_ge(s_ln_rstd, k + 1)
            for c in range(C):
                last = pe.matmul(ps[:, 7, :], mean, ln_sq[:, c, :], start=(c == 0), stop=(c == C - 1))
            last.then_inc(s_ln_var, 1)

        def ln_scalar(act, k):
            act.wait_ge(s_ln_xc, k + 2)
            act.wait_ge(s_ln_var, k + 1)
            act.activation(ln_sq, ln_xc, ACT.Square).then_inc(s_ln_sq, 1)
            act.wait_ge(s_ln_var, k + 2)
            act.wait_ge(s_ln_out, k + 1)
            act.activation(ln_rstd, ps[:, 7, :], ACT.Ln, bias=eps[:, 1:2])
            act.drain()
            act.activation(ln_rstd, ln_rstd, ACT.Exp, scale=-0.5).then_inc(s_ln_rstd, 1)

        def ln_vector(dve, x, k):
            dve.wait_ge(s_ln_mu, k + 1)
            dve.wait_ge(s_ln_out, k + 1)
            mu = view(ps[:, 6, :], [[0, C], [1, S]])
            dve.tensor_tensor(ln_xc, x, mu, ALU.subtract).then_inc(s_ln_xc, 1)
            dve.wait_ge(s_ln_rstd, k + 2)
        block = ctx.enter_context(nc.Block())

        def debug_out(sp, name, ap):
            if name in dbg:
                sp.dma_start(dbg[name], ap).then_inc(s_dbg, 16)

        @block.sync
        def _(sp):
            for started in (s_q_out, s_k_out, s_v_out):
                sp.sem_inc(started, 1)
            sp.dma_start(early[:, :], t_in["early"]).then_inc(s_early, 16)
            x_dram = t_in["xT"]
            sp.dma_start(xT[:, :, :], x_dram).then_inc(s_x, 16)
            sp.dma_start(mam[:, :], t_in["mamba"]).then_inc(s_mam, 16)
            with sp.Fori(0, B) as b:
                sp.wait_ge(s_kx_mm, b * TILES + 1)
                sp.dma_start(xb, x_dram[:, :, tok(b)]).then_inc(s_xb, 16)
            sp.wait_ge(s_h0, B + 1)
            debug_out(sp, "h0", hT[:, :, :])
            if "h0" in dbg:
                sp.wait_ge(s_dbg, 16)
                sp.sem_inc(s_x, 16)
            with sp.Fori(0, B) as b:
                sp.wait_ge(s_dbl, b + 2)
                sp.dma_start(bc_dram[bass.ds(b, 1)].rearrange("b r s -> r (b s)"),
                             dbl[RANK:RANK + 2 * NS, tok(b)]).then_inc(s_bc, 16)
            sp.wait_ge(s_bc, 16 * B)
            with sp.Fori(0, B) as b:
                for g in range(NS // G):
                    sp.wait_ge(s_hc, b * NS + G * (g + 1))
                    if g == 0:
                        sp.wait_ge(s_dt, B + 1)
                    src = bc_dram[bass.ds(b, 1)]
                    src = bass.AP(src.tensor, src.offset + g * G * S, [[0, P], [NS * S, 2], [S, G], [1, S]])
                    sp.dma_start(bc[:, g % 2], src).then_inc(s_bcl[g % 2], 16)
            sp.wait_ge(s_x1, B + 1)
            debug_out(sp, "x1", xT[:, :, :])
            if "x1" in dbg:
                sp.wait_ge(s_dbg, 32)
            sp.dma_start(cw, t_in["cond"]).then_inc(s_cond, 16)
            for j in range(3):
                sp.wait_ge(s_u_mm3, j)
                sp.dma_start(dec_w, t_in["dec_w"][:, j * UT:(j + 1) * UT]).then_inc(s_dec, 16)
                sp.dma_start(dec_b, t_in["dec_b"][:, j * UT:(j + 1) * UT]).then_inc(s_dec, 16)
                sp.wait_ge(s_u_rows, j + 1)
                sp.dma_start(u_dram[:, j * UT:(j + 1) * UT], u_rows).then_inc(s_u_out, 16)
            sp.wait_ge(s_u_out, 48)
            for b in range(B):
                for c in range(C):
                    sp.dma_start(u_tall[:, c, b, :],
                                 u_dram[b, c * P * KU:(c + 1) * P * KU].rearrange("(p k) -> p k", k=KU)).then_inc(s_u_in, 16)
            sp.dma_start(u_bias, bass.AP(u_dram.tensor, u_dram.offset + D * KU, [[UD, 1], [UD, B], [1, KU]])).then_inc(s_u_in, 16)
            with sp.Fori(0, B) as b:
                sp.wait_ge(s_oh, b + 1)
                src = t_in["ids"][:, tok(b)]
                sp.dma_start(ids, bass.AP(src.tensor, src.offset, [[0, P], [N, 3], [1, S]])).then_inc(s_ids, 16)
                sp.wait_ge(s_qs, b + 1)
                sp.dma_start(q_dram[bass.ds(b, 1)].rearrange("b p g s -> p (b g) s"), qs).then_inc(s_q_out, 16)
                sp.wait_ge(s_ks, b + 1)
                sp.dma_start(k_dram[bass.ds(b, 1)].rearrange("b p g s -> p (b g) s"), ks).then_inc(s_k_out, 16)
                sp.wait_ge(s_vs, b + 2)
                sp.dma_start(v_dram[bass.ds(b, 1)].rearrange("b p g s -> p (b g) s"), vs).then_inc(s_v_out, 16)
            debug_out(sp, "x2", xT[:, :, :])
            sp.wait_ge(s_vs, B + 1)
            sp.wait_ge(s_q_out, 16 * B + 1)
            sp.wait_ge(s_k_out, 16 * B + 1)
            sp.wait_ge(s_v_out, 16 * B + 1)
            cut_at = FFN["w1"][0]
            sp.dma_start(fw[:, 0:cut_at], t_in["ffn"][:, 0:cut_at]).then_inc(s_fw, 16)
            sp.dma_start(qa, q_dram[0]).then_inc(s_att_in, 16)
            sp.dma_start(ka, k_dram[0]).then_inc(s_att_in, 16)
            sp.dma_start(va, v_dram[0]).then_inc(s_att_in, 16)
            sp.dma_start(fw[:, cut_at:], t_in["ffn"][:, cut_at:]).then_inc(s_ew, 16)
            with sp.Fori(1, B) as b:
                sp.wait_ge(s_pv, b * HG * 8 + 2)
                sp.dma_start(qa, q_dram[bass.ds(b, 1)].rearrange("b p g s -> p (b g) s")).then_inc(s_att_in, 16)
                sp.dma_start(ka, k_dram[bass.ds(b, 1)].rearrange("b p g s -> p (b g) s")).then_inc(s_att_in, 16)
                sp.dma_start(va, v_dram[bass.ds(b, 1)].rearrange("b p g s -> p (b g) s")).then_inc(s_att_in, 16)
            if "x3" in dbg:
                sp.wait_ge(s_x3, B + 1)
                debug_out(sp, "x3", xT[:, :, :])
            with sp.Fori(0, B) as b:
                sp.wait_ge(s_x4, b + 2)
                sp.dma_start(out[:, :, tok(b)], xT[:, :, tok(b)]).then_inc(s_out, 16)
            sp.wait_ge(s_out, 16 * B)
            sp.wait_ge(s_dbg, 16 * len(dbg))

        @block.tensor
        def _(pe):
            for started in (s_kx_mm, s_ln_var, s_ao_mm, s_out_mm, s_c2_mm, s_i2_mm, s_i1_mm, s_z_tr, s_wo_mm, s_h_mm, s_zn_tr, s_ngb_mm):
                pe.sem_inc(started, 1)
            pe.wait_ge(s_early, 16)
            for j, name in enumerate(("k_aff", "o_aff", "c2_aff")):
                for c in range(C):
                    last = pe.matmul(ps[:, 0, (j * C + c) * B:(j * C + c + 1) * B],
                                     w[name][:, c * P:(c + 1) * P], w["condT"], start=True, stop=True)
            last.then_inc(s_style_mm, 1)
            pe.wait_ge(s_sq, 1)
            for b in range(B):
                for c in range(C):
                    pe.matmul(ps[:, 1 + b // 2, (b % 2) * D:(b % 2 + 1) * D],
                              style2[:, 0, c, b:b + 1].to_broadcast([P, P]), w2k[:, c, :],
                              start=(c == 0), stop=(c == C - 1))
            for o in range(C):
                for c in range(C):
                    last = pe.matmul(ps[:, 3, o * B:(o + 1) * B], w2o[:, c, o * P:(o + 1) * P],
                                     style2[:, 1, c, :], start=(c == 0), stop=(c == C - 1))
            last.then_inc(s_dem_mm, 1)
            pe.wait_ge(s_kw, 1)

            def mix_products(b, t):
                n = b * TILES + t
                pe.wait_ge(s_mixv, n + 2)
                pe.wait_ge(s_mixp, n + 2)
                for c in range(C):
                    for s in range(H):
                        last = pe.matmul(ps[:, 4 + t % 2, c * P:(c + 1) * P],
                                         mix[:, t % 2, s, c * P:(c + 1) * P], ident,
                                         start=(s == 0), stop=(s == H - 1))
                last.then_inc(s_ao_mm, 1)

            with pe.Fori(0, B) as b:
                pe.wait_ge(s_xb, b * 16 + 16)
                for t in range(TILES):
                    n = b * TILES + t
                    pe.wait_ge(s_kx, n + 1)
                    for c in range(C):
                        pe.matmul(ps[:, t % 2, 0:D], xb[:, c, t * P:(t + 1) * P],
                                  kw_mod[:, bass.ds(b, 1), c, :], start=(c == 0), stop=False)
                    pe.matmul(ps[:, t % 2, 0:D], ones[0:1, :], w["k_b"][0:1, :],
                              start=False, stop=True).then_inc(s_kx_mm, 1)
                    pe.wait_ge(s_prod, n + 1)
                    pe.wait_ge(s_diff, n + 1)
                    for d in range(DH):
                        last = pe.matmul(ps[:, 2 + t % 2, 0:D], ident, prod[:, t % 2, d, :],
                                         start=(d == 0), stop=(d == DH - 1))
                    last.then_inc(s_sc, 1)
                    if t:
                        mix_products(b, t - 1)
                mix_products(b, TILES - 1)
                pe.wait_ge(s_ao, (b + 1) * TILES)
                pe.wait_ge(s_h0, b + 1)
                for o in range(C):
                    for c in range(C):
                        last = pe.matmul(ps[:, 6 + o, :], o_w[:, c, o * P:(o + 1) * P], aoT[:, 0, c, :],
                                         start=(c == 0), stop=(c == C - 1))
                last.then_inc(s_o_mm, 1)

            pe.wait_ge(s_h0, B + 1)
            with pe.Fori(0, B) as b:
                ln_tensor(pe, hT[:, :, tok(b)], b)
            pe.wait_ge(s_tap, 1)
            with pe.Fori(0, B) as b:
                pe.wait_ge(s_ln_out, b + 2)
                for m in range(M):
                    pe.wait_ge(s_u2, b * M + m + 1)
                    for k in range(TAPS):
                        for c in range(C):
                            last = pe.matmul(ps[:, m, :], w_tap[:, k, c, m * P:(m + 1) * P],
                                             xn[:, bass.ds(b, 1), c, k:k + S],
                                             start=(k + c == 0), stop=(k == TAPS - 1 and c == C - 1))
                    last.then_inc(s_u_mm, 1)
            with pe.Fori(0, B) as b:
                pe.wait_ge(s_u2, (b + 2) * M)
                pe.wait_ge(s_dbl, b + 1)
                for m in range(M):
                    last = pe.matmul(ps[0:48, 4, :], w_x[:, m, :], u2[:, m, tok(b)],
                                     start=(m == 0), stop=(m == M - 1))
                last.then_inc(s_x_mm, 1)
                pe.wait_ge(s_dbl, b + 2)
                pe.wait_ge(s_u2, (B + 1) * M)
                pe.wait_ge(s_soft, b + 1)
                for m in range(M):
                    last = pe.matmul(ps[:, m, :], wm["w_dt"][0:RANK, m * P:(m + 1) * P], dbl[0:RANK, tok(b)],
                                     start=True, stop=True)
                last.then_inc(s_dt_mm, 1)
            pe.wait_ge(s_soft, B + 1)
            with pe.Fori(0, B) as b:
                pe.wait_ge(s_x1, b + 1)
                pe.wait_ge(s_sz, b + 1)
                for m in range(M):
                    for c in range(C):
                        last = pe.matmul(ps[:, 4 + m, :], w_z[:, c, m * P:(m + 1) * P],
                                         xn[:, bass.ds(b, 1), c, TAPS - 1:TAPS - 1 + S],
                                         start=(c == 0), stop=(c == C - 1))
                last.then_inc(s_z_mm, 1)
                pe.wait_ge(s_yz, b + 1)
                for m in range(M):
                    last = pe.matmul(ps[:, m, :], diag[:, m, :], u2[:, m, tok(b)], start=True, stop=False)
                last.then_inc(s_dterm, 1)
                for n in range(NS):
                    pe.wait_ge(s_hc, b * NS + n + 1 + 2 * G)
                    for m in range(M):
                        last = pe.matmul(ps[:, m, :], ident, state[:, n % 3, m, :],
                                         start=False, stop=(n == NS - 1))
                    last.then_inc(s_y, 1)
                pe.wait_ge(s_yz, b + 2)
                pe.wait_ge(s_sz, b + 2)
                for o in range(C):
                    for m in range(M):
                        last = pe.matmul(ps[:, 4 + o, :], w_out[:, m, o * P:(o + 1) * P], sz[:, m, :],
                                         start=(m == 0), stop=(m == M - 1))
                last.then_inc(s_out_mm, 1)

            pe.wait_ge(s_x1, B + 1)
            for j in range(3):
                pe.wait_ge(s_dec, 32 * (j + 1))
                pe.wait_ge(s_u_rows, j)
                for q in range(-(-UT // 512)):
                    cols = slice(q * 512, min(UT, (q + 1) * 512))
                    n = cols.stop - cols.start
                    pe.matmul(ps[0:B, q, 0:n], w["condT"], dec_w[:, cols], start=True, stop=False)
                    last = pe.matmul(ps[0:B, q, 0:n], ones[0:1, 0:B], dec_b[:, cols], start=False, stop=True)
                last.then_inc(s_u_mm3, 1)
            pe.wait_ge(s_u_in, 16 * (B * C + 1))
            pe.wait_ge(s_u_rows, 3)
            for b in range(B):
                for c in range(C):
                    last = pe.transpose(ps[0:KU, b // 2, (b % 2) * D + c * P:(b % 2) * D + (c + 1) * P],
                                        u_tall[:, c, b, :], ident)
            for b in range(B):
                last = pe.transpose(ps[0:KU, 2, b:b + 1], u_bias[:, b, :], ident[0:1, 0:1])
            last.then_inc(s_u_tr, 1)

            pe.wait_ge(s_prep, 1)
            for o in range(C):
                for c in range(C):
                    pe.matmul(ps[:, 3, o * B:(o + 1) * B], w2c[:, c, o * P:(o + 1) * P],
                              style2[:, 2, c, :], start=(c == 0), stop=(c == C - 1))
            for j, rows_in in enumerate((128, 64, 32)):
                for o in range(C):
                    last = pe.matmul(ps[:, 4, (j * C + o) * B:(j * C + o + 1) * B],
                                     cut("v_w1", 3, D)[0:rows_in, j, o * P:(o + 1) * P],
                                     cut("v_in", 3, B)[0:rows_in, j, :], start=True, stop=True)
            last.then_inc(s_prep_mm, 1)
            pe.wait_ge(s_prep_act, 1)
            for j in range(3):
                for o in range(C):
                    for c in range(C):
                        last = pe.matmul(ps[:, 5, (j * C + o) * B:(j * C + o + 1) * B],
                                         cut("v_w2", 3, C, D)[:, j, c, o * P:(o + 1) * P], vh[:, j, c, :],
                                         start=(c == 0), stop=(c == C - 1))
            last.then_inc(s_prep_mm, 1)
            for k, x in enumerate((vz, vsq)):
                pe.wait_ge(s_prep, k + 2)
                for j in range(3):
                    for c in range(C):
                        last = pe.matmul(ps[:, 6 + k, j * B:(j + 1) * B], mean, x[:, j, c, :],
                                         start=(c == 0), stop=(c == C - 1))
                last.then_inc(s_prep_mm, 1)
            pe.wait_ge(s_prep, 4)
            for o in range(C):
                for j in range(3):
                    for c in range(C):
                        last = pe.matmul(ps[:, 5, o * B:(o + 1) * B], i_w1[:, 2 + j, c, o * P:(o + 1) * P],
                                         vz[:, j, c, :], start=(j + c == 0), stop=(j == 2 and c == C - 1))
            last.then_inc(s_prep_mm, 1)

            pe.wait_ge(s_prep, 5)
            pe.wait_ge(s_u_t, 1)
            with pe.Fori(0, B) as b:
                pe.wait_ge(s_xm, b + 1)
                pe.wait_ge(s_yq, b + 1)
                for o in range(C):
                    for c in range(C):
                        last = pe.matmul(ps[:, o, :], c2_w[:, c, o * P:(o + 1) * P], xm[:, c, :],
                                         start=(c == 0), stop=(c == C - 1))
                last.then_inc(s_c2_mm, 1)
                pe.wait_ge(s_yq, b + 2)
                pe.wait_ge(s_f16, b + 1)
                for o in range(C):
                    for c in range(C):
                        last = pe.matmul(ps[:, 2 + o, :], wq8[:, c, o * P:(o + 1) * P], yq[:, c, :],
                                         start=(c == 0), stop=(c == C - 1))
                last.then_inc(s_ffn_mm, 1)

            def gather(b, i, table, onehot, parts):
                pe.wait_ge(s_g_used, b * 5 + i + 1)
                for j in range(2):
                    for c in range(C):
                        for k in range(parts):
                            last = pe.matmul(ps[:, 2 * j + c, :], table(k, j, c), onehot(k),
                                             start=(k == 0), stop=(k == parts - 1))
                last.then_inc(s_g_mm, 1)

            pe.wait_ge(s_x2, B + 1)
            with pe.Fori(0, B) as b:
                ln_tensor(pe, xT[:, :, tok(b)], B + 3 * b)
                pe.wait_ge(s_oh, b + 2)
                gather(b, 0, lambda k, j, c: pw_t[0:PWK, k, j, c, :], lambda k: oh_pw[0:PWK, k, :], 2)
                pe.wait_ge(s_h1, b + 1)
                ln_tensor(pe, hh, B + 3 * b + 1)
                gather(b, 1, lambda k, j, c: cp_t[0:CP, 0, j, c, :], lambda k: oh_cp[0:CP, :], 1)
                gather(b, 2, lambda k, j, c: cp_t[0:CP, 1, j, c, :], lambda k: oh_cp[0:CP, :], 1)
                gather(b, 3, lambda k, j, c: ms_t[0:MS, j, c, :], lambda k: oh_ms[0:MS, :], 1)
                pe.wait_ge(s_g_used, b * 5 + 5)
                pe.wait_ge(s_i1, b + 1)
                for o in range(C):
                    src = [(i_w1[:, 0], hh), (i_w1[:, 1], tt), (i_w1[:, 5], ss), (wx, xT[:, :, tok(b)])]
                    for i, (wt, x) in enumerate(src):
                        for c in range(C):
                            last = pe.matmul(ps[:, 4 + o, :], wt[:, c, o * P:(o + 1) * P], x[:, c, :],
                                             start=(i + c == 0), stop=(i == 3 and c == C - 1))
                last.then_inc(s_i1_mm, 1)
                pe.wait_ge(s_i1, b + 2)
                for o in range(C):
                    for c in range(C):
                        last = pe.matmul(ps[:, o, :], i_w2[:, c, o * P:(o + 1) * P], i1[:, c, :],
                                         start=(c == 0), stop=(c == C - 1))
                last.then_inc(s_i2_mm, 1)
                pe.wait_ge(s_i2, b + 1)
                ln_tensor(pe, y3, B + 3 * b + 2)
                pe.wait_ge(s_y3, b + 1)
                for wt, done in ((w_q, s_q_mm), (w_k, s_k_mm)):
                    if done is s_k_mm:
                        pe.wait_ge(s_qs, b + 1)
                    for g in range(HG):
                        for c in range(C):
                            last = pe.matmul(ps[:, g, :], wt[:, c, g * P:(g + 1) * P], y3[:, c, :],
                                             start=(c == 0), stop=(c == C - 1))
                    last.then_inc(done, 1)
                for t in range(TILES):
                    pe.wait_ge(s_vs, b + 1)
                    if t >= 2:
                        pe.wait_ge(s_vt, b * TILES + t - 1)
                    for c in range(C):
                        pe.matmul(ps[:, 4 + t % 2, :], y3[:, c, t * P:(t + 1) * P], w_v[:, c, :],
                                  start=(c == 0), stop=False)
                    pe.matmul(ps[:, 4 + t % 2, :], ones[0:1, :], wc["v_one"][0:1, :],
                              start=False, stop=True).then_inc(s_v_mm, 1)
                pe.wait_ge(s_ks, b + 1)
                pe.wait_ge(s_vs, b + 2)

            pe.matmul(ps[:, 5, 0:2 * B], ones, sums[:, :, :], start=True, stop=True).then_inc(s_rho_mm, 1)

            def scores(b, hg, s):
                i, qc = s % HG, s // HG
                pe.wait_ge(s_max, (b * HG + hg) * 16 + s + 1)
                rows_i = slice(i * SLOT, (i + 1) * SLOT)
                pe.matmul(ps[:, s % 2, :], qa[rows_i, hg, qc * P:(qc + 1) * P], ka[rows_i, hg, :],
                          start=True, stop=True).then_inc(s_s_mm, 1)

            def max_rows(b, hg):
                g = b * HG + hg
                pe.wait_ge(s_max, g * 16 + 18)
                pe.wait_ge(s_zn, b * HG + max(hg - 1, 0) + 1)
                for t in range(TILES):
                    last = pe.transpose(ps[:, 7, t * P:(t + 1) * P], mxs[:, t, :], ident)
                last.then_inc(s_m_tr, 1)

            def values(b, hg, j):
                g, kc, pair = b * HG + hg, j // 2, j % 2
                pe.wait_ge(s_pt, g * 8 + j + 3)
                if j == 0:
                    pe.wait_ge(s_zt, g + 1)
                for i in (2 * pair, 2 * pair + 1):
                    h = hg * HG + i
                    last = pe.matmul(ps[i * SLOT:(i + 1) * SLOT, 6, :], va[:, kc, h * SLOT:(h + 1) * SLOT],
                                     pt[:, j % 2, i % 2, :], start=(kc == 0), stop=(kc == TILES - 1))
                last.then_inc(s_pv, 1)

            def z_rows(b, hg):
                g = b * HG + hg
                pe.wait_ge(s_zt, g + 2)
                for t in range(TILES):
                    last = pe.transpose(ps[:, 7, t * P:(t + 1) * P], zt[:, t * P:(t + 1) * P], ident)
                last.then_inc(s_z_tr, 1)

            pe.wait_ge(s_fw, 16)
            pe.wait_ge(s_rho_sum, 1)
            with pe.Fori(0, B) as b:
                pe.wait_ge(s_att_in, 48 * (b + 1))
                for s in range(16):
                    scores(b, 0, s)
                max_rows(b, 0)
                for hg in range(HG):
                    g = b * HG + hg
                    pe.wait_ge(s_qm, g + 1)
                    pe.wait_ge(s_x3, b + 1)
                    for j in range(8):
                        kc, pair = j // 2, j % 2
                        pe.wait_ge(s_pt, g * 8 + j + 1)
                        for i in (2 * pair, 2 * pair + 1):
                            rows_i = slice(i * SLOT, (i + 1) * SLOT)
                            last = pe.matmul(ps[:, 2 + 2 * pair + i % 2, :], ka[rows_i, hg, kc * P:(kc + 1) * P],
                                             qa[rows_i, hg, :], start=True, stop=True)
                        last.then_inc(s_t_mm, 1)
                        if hg < HG - 1:
                            scores(b, hg + 1, 2 * j)
                            scores(b, hg + 1, 2 * j + 1)
                        if j:
                            values(b, hg, j - 1)
                        if j == 2 and hg:
                            z_rows(b, hg - 1)
                    values(b, hg, 7)
                    if hg < HG - 1:
                        max_rows(b, hg + 1)
                pe.wait_ge(s_zn, b * HG + HG - 1 + 1)
                z_rows(b, HG - 1)
                pe.wait_ge(s_zn, (b + 1) * HG + 1)
                for c in range(C):
                    for t in range(TILES):
                        last = pe.transpose(ps[:, c, t * P:(t + 1) * P], zn[:, t, c * P:(c + 1) * P], ident)
                last.then_inc(s_zn_tr, 1)
                pe.wait_ge(s_znt, b + 1)
                for o in range(C):
                    for c in range(C):
                        last = pe.matmul(ps[:, 2 + o, :], w_o[:, c, o * P:(o + 1) * P], zn_t[:, c, :],
                                         start=(c == 0), stop=(c == C - 1))
                last.then_inc(s_wo_mm, 1)

            pe.wait_ge(s_ew, 16)
            pe.wait_ge(s_x3, B + 1)
            for b in range(B):
                for c in range(C):
                    pe.matmul(ps[:, b, c * D:(c + 1) * D], u_t[:, b, c * P:(c + 1) * P], wf["v_dec"][0:KU, :],
                              start=True, stop=True)
            for o in range(C):
                last = pe.matmul(ps[:, 4, o * B:(o + 1) * B], wf["v_dec"][0:KU, o * P:(o + 1) * P], u_t[:, :, D],
                                 start=True, stop=True)
            last.then_inc(s_wgt_mm, 1)

            def hidden(n, f):
                pe.wait_ge(s_hid, n * FM + f + 1)
                for c in range(C):
                    last = pe.matmul(ps[:, 2 + f % 4, :], w1[:, c, f * P:(f + 1) * P], y4[:, c, :],
                                     start=(c == 0), stop=(c == C - 1))
                last.then_inc(s_h_mm, 1)

            with pe.Fori(0, B) as b:
                pe.wait_ge(s_wgt, b + 1)
                pe.wait_ge(s_x4, b + 1)
                for o in range(C):
                    for c in range(C):
                        last = pe.matmul(ps[:, o, :], wgt[:, c, o * P:(o + 1) * P], xT[:, c, tok(b)],
                                         start=(c == 0), stop=(c == C - 1))
                last.then_inc(s_y4_mm, 1)
                pe.wait_ge(s_y4, b + 2)
                for t in range(TILES):
                    for c in range(C):
                        last = pe.matmul(ps[:, 6, t * E:(t + 1) * E], y4[:, c, t * P:(t + 1) * P], gate_w[:, c, :],
                                         start=(c == 0), stop=(c == C - 1))
                last.then_inc(s_gate_mm, 1)
                for f in range(FM + 2):
                    if f < FM:
                        hidden(b, f)
                    if f >= 2:
                        pe.wait_ge(s_hid, b * FM + f - 2 + 5)
                        for o in range(C):
                            last = pe.matmul(ps[:, o, :], w2[:, f - 2, o * P:(o + 1) * P], hid[:, (f - 2) % 4, :],
                                             start=(f == 2), stop=(f == FM + 1))
                        last.then_inc(s_e_mm, 1)
                    if f == FM // 2:
                        pe.wait_ge(s_ng, b + 1)
                        for t in range(TILES):
                            last = pe.matmul(ps[:, 7, t * P:(t + 1) * P], gs[:, 3, t:t + 1].to_broadcast([P, P]),
                                             ident, start=True, stop=True)
                        last.then_inc(s_ngb_mm, 1)


        @block.scalar
        def _(act):
            for started in (s_h0, s_ln_rstd, s_dbl, s_soft, s_sz, s_f16, s_i1, s_zt, s_y4):
                act.sem_inc(started, 1)
            act.preload_act_table_set("natural_log_exp_and_others")
            act.sem_inc(s_kx, 2)
            act.wait_ge(s_dem_mm, 1)
            act.activation(demk, ps[:, 1:3, :], ACT.Ln, bias=eps[:, 0:1])
            act.activation(dem[:, 0], ps[:, 3, 0:C * B], ACT.Ln, bias=eps[:, 0:1])
            act.drain()
            act.activation(dem[:, 0], dem[:, 0], ACT.Exp, scale=-0.5)
            act.activation(demk, demk, ACT.Exp, scale=-0.5).then_inc(s_dem_ln, 1)
            with act.Fori(0, B) as b:
                def exponent(t):
                    n = b * TILES + t
                    act.wait_ge(s_diff, n + 3)
                    act.activation(att[:, t % 2, :], diff[:, t % 2, :], ACT.Exp, scale=0.25).then_inc(s_exp, 1)

                def gathered(t):
                    n = b * TILES + t
                    act.wait_ge(s_ao_mm, n + 2)
                    apart(act)
                    for c in range(C):
                        last = act.activation(aoT[:, 0, c, t * P:(t + 1) * P], ps[:, 4 + t % 2, c * P:(c + 1) * P],
                                              ACT.Copy, scale=style[:, 1, c, bass.ds(b, 1)])
                    last.then_inc(s_ao, 1)

                for t in range(TILES):
                    n = b * TILES + t
                    act.wait_ge(s_kx_mm, n + 2)
                    act.wait_ge(s_mixv, n + 1)
                    act.wait_ge(s_mixp, n + 1)
                    act.activation(kx[:, t % 2, 0:D], ps[:, t % 2, 0:D], ACT.Copy)
                    act.activation(kx[:, t % 2, D:2 * D], ps[:, t % 2, 0:D], ACT.Copy).then_inc(s_kx, 1)
                    exponent(t)
                    if t:
                        gathered(t - 1)
                gathered(TILES - 1)
                act.wait_ge(s_o_mm, b + 1)
                apart(act)
                for o in range(C):
                    last = act.activation(hT[:, o, tok(b)], ps[:, 6 + o, :], ACT.Identity,
                                          bias=w["o_b"][:, o:o + 1], scale=dem[:, 0, o, bass.ds(b, 1)])
                last.then_inc(s_h0, 1)

            act.wait_ge(s_mam, 16)
            act.activation(a_neg, a_neg, ACT.Exp).then_inc(s_a, 1)
            with act.Fori(0, B) as b:
                ln_scalar(act, b)
            act.sem_inc(s_u2, M)
            with act.Fori(0, B) as b:
                for m in range(M):
                    act.wait_ge(s_u_mm, b * M + m + 1)
                    apart(act)
                    act.activation(u2[:, m, tok(b)], ps[:, m, :], ACT.Silu,
                                   bias=wm["conv_b"][:, m:m + 1]).then_inc(s_u2, 1)
            act.preload_act_table_set("natural_log_exp_and_others")
            with act.Fori(0, B) as b:
                act.wait_ge(s_x_mm, b + 1)
                apart(act)
                act.activation(dbl[0:48, tok(b)], ps[0:48, 4, :], ACT.Copy).then_inc(s_dbl, 1)
                act.wait_ge(s_dt_mm, b + 1)
                act.wait_ge(s_dt, b + 1)
                apart(act)
                for m in range(M):
                    act.activation(soft_e[:, m, :], ps[:, m, :], ACT.Abs, bias=wm["b_dt"][:, m:m + 1])
                    act.activation(dt[:, m, tok(b)], ps[:, m, :], ACT.Relu, bias=wm["b_dt"][:, m:m + 1])
                act.drain()
                act.activation(soft_e, soft_e, ACT.Exp, scale=-1.0)
                act.drain()
                act.activation(soft_l, soft_e, ACT.Ln, bias=one[:, 0:1]).then_inc(s_soft, 1)
            act.sem_inc(s_scan, 2)
            act.wait_ge(s_dt, B + 1)
            act.drain()
            with act.Fori(0, B) as b:
                act.wait_ge(s_z_mm, b + 1)
                act.wait_ge(s_out_mm, b + 1)
                act.activation(sz, ps[:, 4:8, :], ACT.Silu).then_inc(s_sz, 1)
                for n in range(NS):
                    act.wait_ge(s_scan, b * NS + n + 1)
                    apart(act)
                    for m in range(M):
                        last = act.activation(decay[:, n % 2, m, 1:S], dt[:, m, bass.ds(b * S + 1, S - 1)],
                                              ACT.Exp, scale=a_neg[:, m * NS + n:m * NS + n + 1])
                    last.then_inc(s_decay, 1)

            for j in range(3):
                act.wait_ge(s_u_mm3, j + 1)
                act.wait_ge(s_u_out, 16 * j)
                for q in range(-(-UT // 512)):
                    cols = slice(q * 512, min(UT, (q + 1) * 512))
                    last = act.activation(u_rows[:, cols], ps[0:B, q, 0:cols.stop - cols.start], ACT.Copy)
                last.then_inc(s_u_rows, 1)
            act.wait_ge(s_u_tr, 1)
            act.activation(u_t[:, 0:2, 0:D], ps[0:KU, 0, 0:2 * D].rearrange("p (b d) -> p b d", b=2), ACT.Copy)
            act.activation(u_t[:, 2:4, 0:D], ps[0:KU, 1, 0:2 * D].rearrange("p (b d) -> p b d", b=2), ACT.Copy)
            act.activation(u_t[:, :, D], ps[0:KU, 2, 0:B], ACT.Copy).then_inc(s_u_t, 1)
            act.wait_ge(s_prep_mm, 1)
            for j in range(3):
                for c in range(C):
                    last = act.activation(vh[:, j, c, :], ps[:, 4, (j * C + c) * B:(j * C + c + 1) * B], ACT.Silu,
                                          bias=cut("v_b1", 3, C)[:, j, c:c + 1])
            last.then_inc(s_prep_act, 1)
            act.preload_act_table_set("natural_log_exp_and_others")
            act.activation(dem[:, 1], ps[:, 3, 0:C * B], ACT.Ln, bias=eps[:, 0:1])
            act.drain()
            act.activation(dem[:, 1], dem[:, 1], ACT.Exp, scale=-0.5).then_inc(s_prep_act, 1)
            act.wait_ge(s_prep, 1)
            act.activation(awn[:, 0:6], awn[:, 0:6], ACT.Exp).then_inc(s_prep_act, 1)
            act.wait_ge(s_prep_mm, 4)
            act.activation(vr[:, :, :], ps[:, 7, 0:3 * B], ACT.Ln, bias=eps[:, 1:2])
            act.drain()
            act.activation(vr[:, :, :], vr[:, :, :], ACT.Exp, scale=-0.5).then_inc(s_prep_act, 1)
            with act.Fori(0, B) as b:
                act.wait_ge(s_x1, B + 1)
                act.wait_ge(s_c2_mm, b + 1)
                apart(act)
                for c in range(C):
                    last = act.activation(xm[:, c, :], xT[:, c, tok(b)], ACT.Copy, scale=style[:, 2, c, bass.ds(b, 1)])
                last.then_inc(s_xm, 1)
                act.wait_ge(s_ffn_mm, b + 1)
                act.wait_ge(s_x2, b + 1)
                act.activation(f16, ps[:, 2:4, :], ACT.Copy).then_inc(s_f16, 1)
            with act.Fori(0, B) as b:
                act.preload_act_table_set("natural_log_exp_and_others")
                ln_scalar(act, B + 3 * b)
                ln_scalar(act, B + 3 * b + 1)
                act.wait_ge(s_i1_mm, b + 2)
                act.wait_ge(s_i2_mm, b + 1)
                apart(act)
                for o in range(C):
                    last = act.activation(i1[:, o, :], ps[:, 4 + o, :], ACT.Silu, bias=cvec[:, o, bass.ds(b, 1)])
                last.then_inc(s_i1, 1)
                act.preload_act_table_set("natural_log_exp_and_others")
                ln_scalar(act, B + 3 * b + 2)
                act.wait_ge(s_q_mm, b + 1)
                act.wait_ge(s_q_out, 16 * b + 1)
                apart(act)
                act.activation(qs, ps[:, 0:4, :], ACT.Square, accum_out=sums[:, 0, bass.ds(b, 1)])
                act.drain()
                act.activation(qs, ps[:, 0:4, :], ACT.Copy, scale=sqk[:, 0:1]).then_inc(s_qs, 1)
                act.wait_ge(s_k_mm, b + 1)
                act.wait_ge(s_k_out, 16 * b + 1)
                apart(act)
                act.activation(ks, ps[:, 0:4, :], ACT.Square, accum_out=sums[:, 1, bass.ds(b, 1)])
                act.drain()
                act.activation(ks, ps[:, 0:4, :], ACT.Identity, bias=wc["slot_one"]).then_inc(s_ks, 1)
            act.wait_ge(s_rho_sum, 1)
            act.activation(rho[:, :], ssq[:, :], ACT.Ln, scale=1.0 / (N * D))
            act.drain()
            act.activation(rho[:, :], rho[:, :], ACT.Exp, scale=0.5).then_inc(s_rho_root, 1)
            act.sem_inc(s_pt, 2)
            act.wait_ge(s_rho, 1)
            with act.Fori(0, B) as b:
                for hg in range(HG):
                    for j in range(8):
                        n = (b * HG + hg) * 8 + j
                        act.wait_ge(s_t_mm, n + 1)
                        act.wait_ge(s_pv, n + 1)
                        act.activation(pt[:, j % 2], ps[:, 2 + 2 * (j % 2):4 + 2 * (j % 2), :], ACT.Exp,
                                       scale=rho[:, 0:1]).then_inc(s_pt, 1)
                    g = b * HG + hg
                    act.wait_ge(s_pv, g * 8 + 10)
                    act.wait_ge(s_z_tr, g + 1)
                    act.activation(zt, ps[:, 6, :], ACT.Copy).then_inc(s_zt, 1)
                act.wait_ge(s_zn_tr, b + 2)
                act.wait_ge(s_wo_mm, b + 1)
                act.activation(zn_t, ps[:, 0:2, :], ACT.Copy).then_inc(s_znt, 1)
            act.sem_inc(s_hid, 4)
            with act.Fori(0, B) as b:
                act.wait_ge(s_y4_mm, b + 1)
                act.wait_ge(s_h_mm, b * FM + 1)
                apart(act)
                for o in range(C):
                    last = act.activation(y4[:, o, :], ps[:, o, :], ACT.Identity, bias=dbias[:, o, bass.ds(b, 1)])
                last.then_inc(s_y4, 1)
                act.wait_ge(s_gate_sq, b + 1)
                act.activation(gs[:, 1, :], gs[:, 0, :], ACT.Ln, scale=1.0 / E, bias=eps32[:, 0:1])
                act.drain()
                act.activation(gs[:, 1, :], gs[:, 1, :], ACT.Exp, scale=-0.5).then_inc(s_gate_r, 1)
                act.wait_ge(s_gate_d, b + 1)
                act.activation(lg[:, :, :], lg[:, :, :], ACT.Exp, scale=2.0).then_inc(s_gate_e, 1)
                for f in range(FM):
                    n = b * FM + f
                    act.wait_ge(s_h_mm, n + 2)
                    act.wait_ge(s_e_mm, n + 1)
                    act.activation(hid[:, f % 4, :], ps[:, 2 + f % 4, :], ACT.Gelu,
                                   bias=wf["b1"][:, f:f + 1]).then_inc(s_hid, 1)
                act.preload_act_table_set("natural_log_exp_and_others")
                act.wait_ge(s_ngb_mm, b + 2)
                act.wait_ge(s_x4, b + 1)
                act.activation(ngb, ps[:, 7, :], ACT.Copy).then_inc(s_ngb, 1)


        @block.vector
        def _(dve):
            for started in (s_ln_xc, s_ln_out, s_x1, s_yz, s_yq, s_g_used, s_vs, s_x3, s_x4, s_dt, s_x2, s_mixv, s_zn, s_oh):
                dve.sem_inc(started, 1)
            for j, v in enumerate((1e-8, 1e-5, 1e-6)):
                dve.memset(eps[:, j:j + 1], v)
            dve.sem_inc(s_diff, 2)
            dve.wait_ge(s_early, 16)
            dve.tensor_tensor(w2k, k_w, k_w, ALU.mult)
            dve.tensor_tensor(w2o, o_w, o_w, ALU.mult)
            dve.wait_ge(s_style_mm, 1)
            for j, (name, gain) in enumerate((("k_affb", 1.0), ("o_affb", 1.0), ("c2_affb", float(P) ** -0.5))):
                for c in range(C):
                    dve.tensor_scalar(style[:, j, c, :], ps[:, 0, (j * C + c) * B:(j * C + c + 1) * B],
                                      gain, w[name][:, c:c + 1], ALU.mult, ALU.add)
            dve.drain()
            dve.tensor_tensor(style2[:, :, :, :], style[:, :, :, :], style[:, :, :, :], ALU.mult).then_inc(s_sq, 1)
            dve.wait_ge(s_dem_ln, 1)
            for b in range(B):
                for c in range(C):
                    last = dve.scalar_tensor_tensor(kw_mod[:, b, c, :], k_w[:, c, :], style[:, 0, c, b:b + 1],
                                                    demk[:, b, :], ALU.mult, ALU.mult)
            last.then_inc(s_kw, 1)
            with dve.Fori(0, B) as b:
                for t in range(TILES):
                    n = b * TILES + t
                    u = t % 2
                    dve.wait_ge(s_kx, n + 3)
                    k = kx[:, u, :]
                    dve.tensor_tensor(view(prod[:, u], [[D, DH], [H, H], [1, H]]),
                                      view(k, [[1, DH], [0, H], [DH, H]]),
                                      view(k, [[1, DH], [DH, H], [DH, H]]), ALU.mult).then_inc(s_prod, 1)
                    dve.wait_ge(s_sc, n + 1)
                    scores = ps[:, 2 + u, 0:D]
                    dve.tensor_reduce(mx[:, u, :], view(scores, [[1, H], [H, H]]), AX, ALU.max)
                    dve.drain()
                    dve.tensor_tensor(view(diff[:, u], [[H, H], [1, H]]), view(scores, [[H, H], [1, H]]),
                                      view(mx[:, u], [[0, H], [1, H]]), ALU.subtract).then_inc(s_diff, 1)
                    dve.wait_ge(s_exp, n + 1)
                    dve.tensor_reduce(ssum[:, u, :], view(att[:, u], [[1, H], [H, H]]), AX, ALU.add)
                    dve.drain()
                    dve.reciprocal(ssum[:, u, :], ssum[:, u, :])
                    dve.drain()
                    dve.wait_ge(s_ao_mm, n + 1)
                    dve.tensor_tensor(view(att_p[:, u], [[H, H], [1, H]]), view(att[:, u], [[H, H], [1, H]]),
                                      view(ssum[:, u], [[0, H], [1, H]]), ALU.mult).then_inc(s_att, 1)
                    dve.drain()
                    dve.tensor_tensor(view(mix[:, u, POOL_SH], [[D, H - POOL_SH], [DH, H], [1, DH]]),
                                      view(att_p[:, u], [[H, H - POOL_SH], [1, H], [0, DH]], POOL_SH * H),
                                      view(k, [[DH, H - POOL_SH], [DH, H], [1, DH]], POOL_SH * DH),
                                      ALU.mult).then_inc(s_mixv, 1)

            dve.memset(one[:, :], 1.0)
            dve.wait_ge(s_h0, B + 1)
            dve.wait_ge(s_mam, 16)
            dve.wait_ge(s_a, 1)
            dve.tensor_scalar(a_neg, a_neg, -1.0, None, ALU.mult)
            for m in range(M):
                dve.tensor_scalar(diag[:, m, :], ident, wm["d"][:, m:m + 1], None, ALU.mult)
            for b in range(B):
                dve.memset(xn[:, b, :, 0:TAPS - 1], 0.0)
            for k in range(TAPS):
                last = dve.tensor_tensor(w_tap[:, k], w_u, view(wm["conv"], [[0, C], [1, DI]], k * DI), ALU.mult)
            last.then_inc(s_tap, 1)
            if "h0" in dbg:
                dve.wait_ge(s_x, 32)
            with dve.Fori(0, B) as b:
                ln_vector(dve, hT[:, :, tok(b)], b)
                for c in range(C):
                    dve.scalar_tensor_tensor(ln_xc[:, c, :], ln_xc[:, c, :], wm["gamma"][:, c:c + 1], ln_rstd,
                                             ALU.mult, ALU.mult)
                dve.drain()
                for c in range(C):
                    last = dve.tensor_scalar(xn[:, bass.ds(b, 1), c, TAPS - 1:TAPS - 1 + S], ln_xc[:, c, :],
                                             wm["beta"][:, c:c + 1], None, ALU.add)
                last.then_inc(s_ln_out, 1)
            with dve.Fori(0, B) as b:
                dve.wait_ge(s_soft, b + 2)
                dve.wait_ge(s_dt, b + 1)
                dve.tensor_scalar(rest, soft_e, 1.0, -1.0, ALU.add, ALU.add)
                dve.drain()
                dve.tensor_tensor(rest, soft_e, rest, ALU.subtract)
                dve.drain()
                dve.tensor_tensor(rest, soft_l, rest, ALU.add)
                dve.drain()
                dve.tensor_tensor(dt[:, :, tok(b)], dt[:, :, tok(b)], rest, ALU.add).then_inc(s_dt, 1)
            dve.sem_inc(s_hc, 2 * G)
            dve.sem_inc(s_y, 3)
            dve.drain()
            dve.memset(view(decay[:, 0], [[S, 2 * M]]), 0.0)
            with dve.Fori(0, B) as b:
                dve.wait_ge(s_dterm, b + 1)
                dve.tensor_tensor(u2[:, :, tok(b)], u2[:, :, tok(b)], dt[:, :, tok(b)], ALU.mult).then_inc(s_du, 1)
                for n in range(NS):
                    g = n // G
                    flat = view(state[:, n % 3], [[1, M * S]])
                    dve.wait_ge(s_decay, b * NS + n + 1)
                    dve.wait_ge(s_dbu, b * NS + n + 1)
                    dve.tensor_tensor_scan(flat, view(decay[:, n % 2], [[1, M * S]]), flat, 0.0,
                                           ALU.mult, ALU.add).then_inc(s_scan, 1)
                    dve.drain()
                    dve.wait_ge(s_bcl[g % 2], (b * (NS // G // 2) + g // 2 + 1) * 16)
                    dve.tensor_tensor(state[:, n % 3], state[:, n % 3],
                                      view(bc[:, g % 2, 1, n % G, :], [[0, M], [1, S]]),
                                      ALU.mult).then_inc(s_hc, 1)
                dve.wait_ge(s_y, (b + 1) * NS + 3)
                dve.wait_ge(s_sz, b + 2)
                dve.tensor_tensor(sz, ps[:, 0:4, :], sz, ALU.mult).then_inc(s_yz, 1)
                dve.wait_ge(s_out_mm, b + 2)
                dve.tensor_tensor(hT[:, :, tok(b)], ps[:, 4:6, :], hT[:, :, tok(b)], ALU.add)
                dve.drain()
                dve.wait_ge(s_x, 16)
                dve.tensor_tensor(xT[:, :, tok(b)], xT[:, :, tok(b)], hT[:, :, tok(b)], ALU.add).then_inc(s_x1, 1)

            dve.wait_ge(s_cond, 16)
            dve.tensor_tensor(w2c, c2_w, c2_w, ALU.mult)
            dve.tensor_tensor(sqk[:, :], wc["s_q"], wc["s_k"], ALU.mult)
            dve.tensor_reduce(awn[:, 6:7], wc["aw"], AX, ALU.max)
            wbig, wsml = xm[:, :, 0:D], xh[:, :, 0:D]
            dve.tensor_scalar(wbig, ffn_w, 448.0, -448.0, ALU.min, ALU.max)
            dve.tensor_scalar(wsml, ffn_w, 1.0, -1.0, ALU.min, ALU.max)
            dve.drain()
            dve.tensor_scalar(q8[:, :, 0:D], wbig, 0.5, None, ALU.mult, saturate=False)
            dve.tensor_scalar(q8b, wsml, 1.0, None, ALU.mult, saturate=False)
            dve.tensor_scalar(q8c, wsml, 0.5, None, ALU.mult, saturate=False)
            dve.drain()
            dve.scalar_tensor_tensor(wbig, q8[:, :, 0:D], 2.0, q8b, ALU.mult, ALU.add)
            dve.drain()
            dve.scalar_tensor_tensor(wq8, q8c, -2.0, wbig, ALU.mult, ALU.add)
            dve.tensor_scalar(awn[:, 0:6], wc["aw"], awn[:, 6:7], None, ALU.subtract)
            dve.drain()
            dve.engine_nop().then_inc(s_prep, 1)
            dve.wait_ge(s_prep_act, 3)
            dve.tensor_reduce(awn[:, 6:7], awn[:, 0:6], AX, ALU.add)
            dve.drain()
            dve.reciprocal(awn[:, 7:8], awn[:, 6:7])
            dve.drain()
            dve.tensor_scalar(awn[:, 0:6], awn[:, 0:6], awn[:, 7:8], None, ALU.mult)
            dve.drain()
            for j in range(6):
                dve.tensor_scalar(i_w1[:, j], i_w1[:, j], awn[:, j:j + 1], None, ALU.mult)
            dve.drain()
            dve.tensor_tensor(wx, i_w1[:, 2], i_w1[:, 3], ALU.add)
            dve.drain()
            dve.tensor_tensor(wx, wx, i_w1[:, 4], ALU.add)
            dve.wait_ge(s_prep_mm, 2)
            dve.tensor_tensor(view(vz[:, 0, 0, :], [[B, 3 * C], [1, B]]), view(ps[:, 5, :], [[B, 3 * C], [1, B]]),
                              view(wc["v_b2"], [[1, 3 * C], [0, B]]), ALU.add).then_inc(s_prep, 1)
            dve.wait_ge(s_prep_mm, 3)
            dve.drain()
            dve.tensor_tensor(vz[:, :, :, :], vz[:, :, :, :], view(ps[:, 6, :], [[B, 3], [0, C], [1, B]]), ALU.subtract)
            dve.drain()
            dve.tensor_tensor(vsq[:, :, :, :], vz[:, :, :, :], vz[:, :, :, :], ALU.mult).then_inc(s_prep, 1)
            dve.wait_ge(s_prep_act, 4)
            dve.tensor_tensor(vz[:, :, :, :], vz[:, :, :, :], view(vr[:, 0, :], [[B, 3], [0, C], [1, B]]), ALU.mult)
            dve.drain()
            dve.tensor_tensor(view(vz[:, 0, 0, :], [[B, 3 * C], [1, B]]), view(vz[:, 0, 0, :], [[B, 3 * C], [1, B]]),
                              view(wc["v_g"], [[1, 3 * C], [0, B]]), ALU.mult)
            dve.drain()
            dve.tensor_tensor(view(vz[:, 0, 0, :], [[B, 3 * C], [1, B]]), view(vz[:, 0, 0, :], [[B, 3 * C], [1, B]]),
                              view(wc["v_be"], [[1, 3 * C], [0, B]]), ALU.add).then_inc(s_prep, 1)
            dve.wait_ge(s_prep_mm, 5)
            dve.tensor_tensor(cvec[:, :, :], view(ps[:, 5, :], [[B, C], [1, B]]),
                              view(wc["i_b1"], [[1, C], [0, B]]), ALU.add).then_inc(s_prep, 1)
            dve.wait_ge(s_prep_act, 4)
            with dve.Fori(0, B) as b:
                dve.wait_ge(s_c2_mm, b + 2)
                dve.wait_ge(s_x2, b + 1)
                y2 = tt
                for o in range(C):
                    dve.tensor_scalar(y2[:, o, :], ps[:, o, :], dem[:, 1, o, bass.ds(b, 1)], wc["c2_b"][:, o:o + 1],
                                      ALU.mult, ALU.add)
                dve.drain()
                dve.tensor_scalar(y2, y2, 256.0, -256.0, ALU.min, ALU.max)
                dve.drain()
                dve.tensor_scalar(q8, y2, 240.0, -240.0, ALU.min, ALU.max, saturate=False)
                dve.tensor_scalar(low, y2, -248.0, None, ALU.is_le)
                dve.drain()
                dve.scalar_tensor_tensor(low, y2, 248.0, low, ALU.is_ge, ALU.subtract)
                dve.drain()
                dve.scalar_tensor_tensor(yq, low, 16.0, q8, ALU.mult, ALU.add).then_inc(s_yq, 1)
                dve.wait_ge(s_f16, b + 2)
                for o in range(C):
                    last = dve.scalar_tensor_tensor(xT[:, o, tok(b)], f16[:, o, :], wc["ffn_b"][:, o:o + 1],
                                                    xT[:, o, tok(b)], ALU.add, ALU.add)
                last.then_inc(s_x2, 1)

            def embed(b, i, out, x):
                dve.wait_ge(s_g_mm, b * 4 + i + 1)
                dve.tensor_tensor(out, x, ps[:, 0:2, :], ALU.mult)
                dve.drain()
                last = dve.tensor_tensor(out, out, ps[:, 2:4, :], ALU.add)
                last.then_inc(s_g_used, 1)

            with dve.Fori(0, B) as b:
                dve.wait_ge(s_ids, 16 * (b + 1))
                dve.wait_ge(s_i1_mm, b + 1)
                for k in range(2):
                    dve.tensor_scalar(oh_pw[0:PWK, k, :], ids[0:PWK, 0, :], wc["rows"][0:PWK, k:k + 1], None, ALU.is_equal)
                dve.tensor_scalar(oh_cp[0:CP, :], ids[0:CP, 1, :], wc["rows"][0:CP, 0:1], None, ALU.is_equal)
                dve.tensor_scalar(oh_ms[0:MS, :], ids[0:MS, 2, :], wc["rows"][0:MS, 0:1], None,
                                  ALU.is_equal).then_inc(s_oh, 1)
                ln_vector(dve, xT[:, :, tok(b)], B + 3 * b)
                rstd2 = view(ln_rstd, [[0, C], [1, S]])
                dve.tensor_tensor(xh, ln_xc, rstd2, ALU.mult).then_inc(s_ln_out, 1)
                dve.drain()
                embed(b, 0, hh, xh)
                dve.drain()
                dve.engine_nop().then_inc(s_h1, 1)
                ln_vector(dve, hh, B + 3 * b + 1)
                dve.tensor_tensor(hh, ln_xc, rstd2, ALU.mult).then_inc(s_ln_out, 1)
                dve.drain()
                embed(b, 1, hh, hh)
                embed(b, 2, tt, xh)
                embed(b, 3, ss, xh)
                dve.wait_ge(s_i2_mm, b + 2)
                for o in range(C):
                    last = dve.tensor_scalar(y3[:, o, :], ps[:, o, :], wc["i_b2"][:, o:o + 1], None, ALU.add)
                last.then_inc(s_i2, 1)
                dve.engine_nop().then_inc(s_g_used, 1)
                dve.drain()
                ln_vector(dve, y3, B + 3 * b + 2)
                for c in range(C):
                    dve.scalar_tensor_tensor(y3[:, c, :], ln_xc[:, c, :], wc["i_g"][:, c:c + 1], ln_rstd,
                                             ALU.mult, ALU.mult)
                dve.drain()
                for c in range(C):
                    last = dve.tensor_scalar(y3[:, c, :], y3[:, c, :], wc["i_be"][:, c:c + 1], None, ALU.add)
                last.then_inc(s_ln_out, 1)
                dve.drain()
                dve.engine_nop().then_inc(s_y3, 1)
                dve.wait_ge(s_v_out, 16 * b + 1)
                for t in range(TILES):
                    dve.wait_ge(s_v_mm, b * TILES + t + 1)
                    dve.tensor_copy(vs[:, t, :], ps[:, 4 + t % 2, :]).then_inc(s_vt, 1)
                dve.drain()
                dve.engine_nop().then_inc(s_vs, 1)
            dve.wait_ge(s_rho_mm, 1)
            dve.tensor_reduce(ssq[:, :], view(ps[:, 5, :], [[B, 2], [1, B]]), AX, ALU.add).then_inc(s_rho_sum, 1)
            dve.wait_ge(s_rho_root, 1)
            dve.tensor_scalar(rho[:, :], rho[:, :], 1e-6, None, ALU.add)
            dve.drain()
            dve.tensor_tensor(rho[:, 0:1], rho[:, 0:1], rho[:, 1:2], ALU.mult)
            dve.drain()
            dve.reciprocal(rho[:, 0:1], rho[:, 0:1]).then_inc(s_rho, 1)
            dve.sem_inc(s_pv, 2)
            dve.sem_inc(s_max, 2)
            dve.wait_ge(s_vs, B + 1)
            dve.wait_ge(s_k_out, 16 * B + 1)
            dve.wait_ge(s_v_out, 16 * B + 1)
            dve.memset(mxs, 0.0)
            dve.drain()

            def maximum(b, hg, s):
                i, qc = s % HG, s // HG
                dve.wait_ge(s_s_mm, (b * HG + hg) * 16 + s + 1)
                col = i * SLOT + DH
                dve.tensor_reduce(mxs[:, qc, col:col + 1], ps[:, s % 2, :], AX, ALU.max).then_inc(s_max, 1)

            def normalise(b, hg):
                g = b * HG + hg
                dve.wait_ge(s_z_tr, g + 2)
                dve.reciprocal(zrec, view(ps[:, 7, DH:], [[P, TILES], [SLOT, HG]]))
                dve.drain()
                dve.tensor_tensor(view(zn, [[D, TILES], [DH, HG], [1, DH]], hg * HG * DH),
                                  view(ps[:, 7, :], [[P, TILES], [SLOT, HG], [1, DH]]),
                                  view(zrec, [[HG, TILES], [1, HG], [0, DH]]), ALU.mult).then_inc(s_zn, 1)

            with dve.Fori(0, B) as b:
                for s in range(16):
                    maximum(b, 0, s)
                dve.wait_ge(s_zn_tr, b + 1)
                for hg in range(HG):
                    dve.wait_ge(s_m_tr, b * HG + hg + 1)
                    dve.tensor_tensor(qa[:, hg, :], qa[:, hg, :], ps[:, 7, :], ALU.subtract).then_inc(s_qm, 1)
                    if hg < HG - 1:
                        for s in range(16):
                            maximum(b, hg + 1, s)
                            if s == 7 and hg:
                                normalise(b, hg - 1)
                    else:
                        normalise(b, hg - 1)
                normalise(b, HG - 1)
                dve.wait_ge(s_wo_mm, b + 2)
                dve.tensor_tensor(xT[:, :, tok(b)], ps[:, 2:4, :], xT[:, :, tok(b)], ALU.add).then_inc(s_x3, 1)

            dve.memset(eps32[:, :], float(np.finfo(np.float32).eps))
            dve.sem_inc(s_e_mm, 4)
            dve.wait_ge(s_ew, 16)
            if "x3" in dbg:
                dve.wait_ge(s_dbg, 16 * len(dbg))
            dve.tensor_reduce(b2s[:, :], fcut("b2", C, E), AX, ALU.add)
            dve.wait_ge(s_wgt_mm, 1)
            dve.tensor_copy(view(wgt_all, [[C * D, B], [1, C * D]]), ps[:, 0:B, :])
            dve.tensor_copy(dbias[:, :, :], ps[:, 4, 0:C * B]).then_inc(s_wgt_all, 1)
            with dve.Fori(0, B) as b:
                dve.wait_ge(s_gate_mm, b + 1)
                dve.tensor_tensor(lg[:, :, :], view(ps[:, 6, :], [[E, TILES], [1, E]]),
                                  view(wf["gate_b"], [[0, TILES], [1, E]]), ALU.add)
                dve.drain()
                dve.tensor_tensor(lg2[:, :, :], lg[:, :, :], lg[:, :, :], ALU.mult)
                dve.drain()
                dve.tensor_reduce(gs[:, 0, :], lg2[:, :, :], AX, ALU.add).then_inc(s_gate_sq, 1)
                dve.drain()
                dve.tensor_tensor(lg2[:, :, :], lg[:, :, :], view(wf["rms_w"], [[0, TILES], [1, E]]), ALU.mult)
                dve.drain()
                dve.wait_ge(s_gate_r, b + 1)
                dve.tensor_tensor(lg2[:, :, :], lg2[:, :, :], view(gs[:, 1, :], [[1, TILES], [0, E]]), ALU.mult)
                dve.drain()
                dve.tensor_reduce(gs[:, 2, :], lg2[:, :, :], AX, ALU.max)
                dve.drain()
                dve.tensor_tensor(lg[:, :, :], lg2[:, :, :], view(gs[:, 2, :], [[1, TILES], [0, E]]),
                                  ALU.subtract).then_inc(s_gate_d, 1)
                dve.wait_ge(s_gate_e, b + 1)
                dve.tensor_reduce(gs[:, 0, :], lg[:, :, :], AX, ALU.add)
                dve.drain()
                dve.reciprocal(gs[:, 2, :], gs[:, 0, :])
                dve.drain()
                dve.tensor_scalar(gs[:, 1, :], gs[:, 2, :], 1e-6, None, ALU.add)
                dve.drain()
                dve.reciprocal(gs[:, 0, :], gs[:, 1, :])
                dve.drain()
                dve.wait_ge(s_ngb_mm, b + 1)
                dve.tensor_tensor(gs[:, 3, :], gs[:, 2, :], gs[:, 0, :], ALU.mult).then_inc(s_ng, 1)
                dve.wait_ge(s_ngb, b + 1)
                dve.wait_ge(s_e_mm, (b + 1) * FM + 4)
                for o in range(C):
                    dve.scalar_tensor_tensor(moe[:, o, :], ps[:, o, :], b2s[:, o:o + 1], ngb, ALU.add, ALU.mult)
                dve.drain()
                dve.tensor_tensor(xT[:, :, tok(b)], xT[:, :, tok(b)], moe, ALU.add).then_inc(s_x4, 1)


        @block.gpsimd
        def _(pool):
            for started in (s_mixp,):
                pool.sem_inc(started, 1)
            with pool.Fori(0, B) as b:
                for t in range(TILES):
                    n = b * TILES + t
                    u = t % 2
                    pool.wait_ge(s_att, n + 1)
                    pool.tensor_tensor(view(mix[:, u], [[D, POOL_SH], [DH, H], [1, DH]]),
                                       view(att_p[:, u], [[H, POOL_SH], [1, H], [0, DH]]),
                                       view(kx[:, u, :], [[DH, POOL_SH], [DH, H], [1, DH]]),
                                       ALU.mult).then_inc(s_mixp, 1)

            with pool.Fori(0, B) as b:
                pool.wait_ge(s_du, b + 1)
                for n in range(NS):
                    g = n // G
                    pool.wait_ge(s_bcl[g % 2], (b * (NS // G // 2) + g // 2 + 1) * 16)
                    pool.wait_ge(s_y, b * NS + (n + 1 if n else 3))
                    apart(pool)
                    pool.tensor_tensor(state[:, n % 3], u2[:, :, tok(b)],
                                       view(bc[:, g % 2, 0, n % G, :], [[0, M], [1, S]]),
                                       ALU.mult).then_inc(s_dbu, 1)
            pool.wait_ge(s_wgt_all, 1)
            with pool.Fori(0, B) as b:
                pool.wait_ge(s_y4, b + 1)
                apart(pool)
                pool.tensor_copy(wgt, wgt_all[:, bass.ds(b, 1)]).then_inc(s_wgt, 1)


ARENA = 35000


def chunked(a):
    a = np.asarray(a)
    k = a.shape[0] // P
    return a.reshape(k, P, -1).transpose(1, 0, 2).reshape(P, -1)


def rows(a):
    a = np.asarray(a, np.float32)
    out = np.zeros((P, a.shape[1]), np.float32)
    out[:a.shape[0]] = a
    return out


def pack(spec, width, parts):
    out = np.zeros((P, width), np.float32)
    for name, (at, n) in spec.items():
        a = parts[name]
        assert a.shape == (P, n), (name, a.shape, n)
        out[:, at:at + n] = a
    return out


def slots(a):
    a = np.asarray(a).reshape(D, H, DH)
    out = np.zeros((D, H, SLOT), np.float32)
    out[:, :, :DH] = a
    return chunked(out.reshape(D, H * SLOT))


def host_arrays(i):
    col = lambda v: chunked(np.asarray(v).reshape(-1, 1))
    wide = lambda v: np.broadcast_to(np.asarray(v).reshape(1, -1), (P, np.asarray(v).size))
    x = np.asarray(i["x"]).reshape(N, D).T
    early = pack(EARLY, EARLY_W, dict(
        condT=np.asarray(i["cond_512"]).T, k_aff=np.asarray(i["L0_cond_k_aff_w"]).T,
        o_aff=np.asarray(i["L0_cond_o_aff_w"]).T, c2_aff=np.asarray(i["L0_cond2_affine_w"]).T,
        k_affb=col(i["L0_cond_k_aff_b"]), o_affb=col(i["L0_cond_o_aff_b"]), c2_affb=col(i["L0_cond2_affine_b"]),
        k_w=chunked(np.asarray(i["L0_cond_k_w"]).T), o_w=chunked(np.asarray(i["L0_cond_o_w"]).T),
        ident=np.eye(P, dtype=np.float32), mean=np.full((P, P), 1.0 / D, np.float32),
        ones=np.ones((P, P), np.float32), k_b=wide(i["L0_cond_k_b"]), o_b=col(i["L0_cond_o_b"])))
    w_in = np.asarray(i["L0_attn_W_in"])
    mamba = pack(MAMBA, MAMBA_W, dict(
        gamma=col(i["L0_attn_gamma"]), beta=col(i["L0_attn_beta"]), w_u=chunked(w_in[:, :DI]),
        conv=wide(np.asarray(i["L0_attn_conv_w"]).T), w_z=chunked(w_in[:, DI:]), conv_b=col(i["L0_attn_conv_b"]),
        w_x=chunked(i["L0_attn_W_x"]), w_dt=rows(i["L0_attn_W_dt"]), b_dt=col(i["L0_attn_b_dt"]),
        a_log=chunked(i["L0_attn_A_log"]), d=col(i["L0_attn_D"]), w_out=chunked(i["L0_attn_W_out"])))
    slot = np.arange(HG * P) % SLOT
    table = lambda g, b: np.concatenate([np.asarray(i[g]), np.asarray(i[b])], axis=1)
    pw = table("L1_cond_pw_g", "L1_cond_pw_b")
    three = lambda f: np.concatenate([f(x) for x in ("mem", "noi", "res")], axis=1)
    wqkv = np.asarray(i["L1_attn_Wqkv"])
    in_slots = lambda v: np.concatenate([np.pad(np.asarray(v), (0, SLOT - DH))] * HG).reshape(P, 1)
    cond = pack(COND, COND_W, dict(
        c2_w=chunked(np.asarray(i["L0_cond2_weight"]).T), c2_b=col(i["L0_cond2_bias"]),
        ffn_w=chunked(np.asarray(i["L0_ffn_weight"]).T), ffn_b=col(i["L0_ffn_bias"]),
        pw=np.concatenate([rows(pw[:PWK]), rows(pw[PWK:])], axis=1),
        cp=rows(np.concatenate([table("L1_cond_cp_g", "L1_cond_cp_b"), table("L1_cond_tm_g", "L1_cond_tm_b")], axis=1)),
        ms=rows(table("L1_cond_ms_g", "L1_cond_ms_b")),
        rows=np.stack([np.arange(P), np.arange(P) + PWK], axis=1).astype(np.float32), aw=wide(i["L1_cond_aw"]),
        v_in=np.concatenate([rows(np.asarray(i[x]).T) for x in ("cond_512", "cond_64", "fside_Bx32_0")], axis=1),
        v_w1=three(lambda x: rows(i[f"L1_cond_{x}_W1"])), v_w2=three(lambda x: chunked(i[f"L1_cond_{x}_W2"])),
        v_b1=three(lambda x: col(i[f"L1_cond_{x}_b1"])), v_b2=three(lambda x: col(i[f"L1_cond_{x}_b2"])),
        v_g=three(lambda x: col(i[f"L1_cond_{x}_g"])), v_be=three(lambda x: col(i[f"L1_cond_{x}_be"])),
        i_w1=chunked(i["L1_cond_int_W1"]), i_w2=chunked(i["L1_cond_int_W2"]), i_b1=col(i["L1_cond_int_b1"]),
        i_b2=col(i["L1_cond_int_b2"]), i_g=col(i["L1_cond_int_g"]), i_be=col(i["L1_cond_int_be"]),
        w_q=slots(wqkv[:, :D]), w_k=slots(wqkv[:, D:2 * D]), w_v=slots(wqkv[:, 2 * D:]),
        v_one=np.broadcast_to((slot == DH).astype(np.float32), (P, HG * P)),
        s_q=in_slots(i["L1_attn_scale_q"]), s_k=in_slots(i["L1_attn_scale_k"]),
        slot_one=(np.arange(P) % SLOT == DH).astype(np.float32).reshape(P, 1)))
    ids = np.stack([np.asarray(i[k]).reshape(-1) for k in ("itok_BxS_0_999", "itok_BxS_0_4", "mask_BxS_ik0")])
    per = lambda a: np.asarray(a).transpose(1, 0, 2).reshape(np.asarray(a).shape[1], -1)
    ffn = pack(FFN, FFN_W, dict(
        w_o=chunked(i["L1_attn_Wo"]), v_dec=rows(i["L1_cond2_V"]), gate_w=chunked(np.asarray(i["L1_ffn_gate_w"]).T),
        gate_b=wide(i["L1_ffn_gate_b"]), rms_w=wide(i["L1_ffn_rms_w"]),
        b1=np.asarray(i["L1_ffn_b1"]).reshape(FM, P).T, b2=chunked(np.asarray(i["L1_ffn_b2"]).T),
        w1=chunked(per(i["L1_ffn_w1"])), w2=chunked(np.asarray(i["L1_ffn_w2"]).reshape(E * FH, D))))
    return {
        "cond": cond, "ffn": ffn, "ids": ids.astype(np.int32), "dec_w": np.asarray(i["L1_cond2_W_dec"]),
        "dec_b": np.asarray(i["L1_cond2_b_dec"]).reshape(1, -1),
        "mamba": mamba,
        "xT": np.ascontiguousarray(x.reshape(C, P, N).transpose(1, 0, 2)),
        "early": early,
    }


def kernel(**inputs):
    import concourse.bacc as bacc
    from concourse.bass_utils import run_bass_kernel_spmd
    arrays = host_arrays(inputs)
    nc = bacc.Bacc("TRN2", target_bir_lowering=False, num_devices=1)
    t_in = {k: nc.dram_tensor(f"in_{k}", a.shape, mybir.dt.from_np(a.dtype), kind="ExternalInput").ap()
            for k, a in arrays.items()}
    out = nc.dram_tensor("out", (P, C, N), F32, kind="ExternalOutput").ap()
    program(nc, t_in, out)
    r = run_bass_kernel_spmd(nc, [{f"in_{k}": a for k, a in arrays.items()}], core_ids=[0])
    got = r.results[0]["out"]
    return np.ascontiguousarray(got.transpose(1, 0, 2).reshape(D, N).T).reshape(B, S, D)
```

```python
from contextlib import ExitStack

import numpy as np

import concourse.bass as bass
from concourse import mybir

F32 = mybir.dt.float32
BF16 = mybir.dt.bfloat16
F16 = mybir.dt.float16
FP8 = mybir.dt.float8e4
I32 = mybir.dt.int32
ALU = mybir.AluOpType
ACT = mybir.ActivationFunctionType
AX = mybir.AxisListType.X

P = 128
B, S, D = 4, 512, 256
N = B * S
C = D // P
H, DH = 16, 16
TILES = S // P
DI, NS, RANK, TAPS = 512, 16, 16, 4
M = DI // P
G = 2
PW, CP, MS = 250, 5, 3
PWK = PW // 2
KU = 30
E, FH = 8, 512
FM = E * FH // P
SLOT = 32
Q_PARTS = (0, 0, 1, 0, 2, 1)
K_PARTS = (0, 1, 0, 2, 0, 1)
STACK = len(Q_PARTS) * DH
HG = P // SLOT
HALF = H // 2 + 1


def layout(fields):
    at, out = 0, {}
    for name, width in fields:
        out[name] = (at, width)
        at += width
    return out, at


EARLY, EARLY_W = layout([
    ("condT", B), ("k_aff", D), ("o_aff", D), ("c2_aff", D), ("k_affb", C), ("o_affb", C), ("c2_affb", C),
    ("k_w", C * D), ("ident", P), ("mean", P), ("k_b", D), ("ones", P), ("o_w", C * D), ("o_b", C)])
MAMBA, MAMBA_W = layout([
    ("gamma", C), ("beta", C), ("w_u", C * DI), ("conv", M * TAPS), ("w_z", C * DI), ("conv_b", M),
    ("w_x", M * 48), ("w_dt", DI), ("b_dt", M), ("a_log", M * NS), ("d", M), ("w_out", M * D)])
COND, COND_W = layout([
    ("c2_w", C * D), ("c2_b", C), ("ffn_w", C * D), ("ffn_b", C),
    ("pw", 2 * 2 * D), ("cp", 4 * D), ("ms", 2 * D), ("rows", 2), ("aw", 6),
    ("v_in", 3 * B), ("v_w1", 3 * D), ("v_w2", 3 * C * D), ("v_b1", 3 * C), ("v_b2", 3 * C),
    ("v_g", 3 * C), ("v_be", 3 * C),
    ("i_w1", 6 * C * D), ("i_w2", C * D), ("i_b1", C), ("i_b2", C), ("i_g", C), ("i_be", C),
    ("w_q", C * D), ("w_k", C * D), ("w_v", C * D), ("s_q", 1), ("s_k", 1)])
FFN, FFN_W = layout([
    ("w_o", C * D), ("v_dec", D), ("gate_w", C * E), ("gate_b", E), ("rms_w", E), ("b1", FM), ("b2", C * E),
    ("w1", C * E * FH), ("w2", FM * D)])
UD = (D + 1) * KU


def view(ap, dims, off=0):
    return bass.AP(ap.tensor, ap.offset + off, [list(ap.ap[0])] + [list(d) for d in dims])


def tok(b, n=S):
    return bass.ds(b * n, n)


def program(nc, t_in, out, dbg=()):
    ctx = ExitStack()
    with ctx:
        def sb(name, shape, dt=F32):
            return ctx.enter_context(nc.sbuf_tensor(name, shape, dt))

        def sem(name):
            return ctx.enter_context(nc.semaphore(name))

        ps = ctx.enter_context(nc.psum_tensor("ps", [P, 8, 512], F32))

        early = sb("early", [P, EARLY_W])
        xT = sb("xT", [P, C, N])
        hT = sb("hT", [P, C, N])
        arena = sb("arena", [P, ARENA])

        def fields(tensor, spec, base=0):
            return {k: tensor[:, base + a:base + a + w] for k, (a, w) in spec.items()}

        w = fields(early, EARLY)
        k_w = w["k_w"].rearrange("p (c o) -> p c o", c=C)
        o_w = w["o_w"].rearrange("p (c o) -> p c o", c=C)
        ident, ones, mean = w["ident"], w["ones"], w["mean"]

        def carve(at, *shape):
            n = int(np.prod(shape))
            assert at + n <= ARENA, (at + n, ARENA)
            flat = arena[:, at:at + n]
            dims, st = [], n
            for s in shape:
                st //= s
                dims.append([st, s])
            return view(flat, dims), at + n

        style = sb("style", [P, 3, C, B])
        style2 = sb("style2", [P, 3, C, B])
        dem = sb("dem", [P, 2, C, B])
        eps = sb("eps", [P, 3])
        at = 0
        w2k, at = carve(at, C, D)
        w2o, at = carve(at, C, D)
        demk, at = carve(at, B, D)
        kw_mod, at = carve(at, B, C, D)
        xb, at = carve(at, C, S)
        kx, at = carve(at, TILES, 2 * D)
        prod, at = carve(at, HALF, H, DH)
        full, at = carve(at, 2, H, 2 * H)
        diff, at = carve(at, 2, D)
        att, at = carve(at, 2, D)
        att_p, at = carve(at, 2, D)
        mx, at = carve(at, 2, H)
        ssum, at = carve(at, 2, H)
        mix, at = carve(at, 2, H, D)
        aoT, at = carve(at, C, N)
        stage1_end = at

        s_early = sem("early_loaded")
        s_x = sem("x_loaded")
        s_style_mm = sem("style_products")
        s_style = sem("style_ready")
        s_sq = sem("squares_ready")
        s_dem_mm = sem("demod_products")
        s_dem_ln = sem("demod_ready")
        s_kw = sem("kw_ready")
        s_xb = sem("xb_loaded")
        s_kx_mm = sem("kx_products")
        s_kx = sem("kx_ready")
        s_red = sem("half_scores_ready")
        s_full = sem("scores_ready")
        s_diff = sem("diff_ready")
        s_exp = sem("exp_ready")
        s_att = sem("att_ready")
        s_mixv = sem("mix_by_vector")
        s_mixp = sem("mix_by_pool")
        s_ao_mm = sem("ao_products")
        s_ao = sem("ao_ready")
        s_o_mm = sem("o_products")
        s_h0 = sem("h0_ready")
        s_dbg = sem("dbg_out")

        POOL_SH = 12

        s_apart = sem("kept_apart")

        def apart(eng):
            eng.sem_inc(s_apart, 1)


        mam = sb("mam", [P, MAMBA_W])
        wm = fields(mam, MAMBA)
        w_u = wm["w_u"].rearrange("p (c o) -> p c o", c=C)
        w_z = wm["w_z"].rearrange("p (c o) -> p c o", c=C)
        w_x = wm["w_x"].rearrange("p (m o) -> p m o", m=M)
        w_out = wm["w_out"].rearrange("p (m o) -> p m o", m=M)
        a_neg = wm["a_log"]
        conv = wm["conv"].rearrange("p (m k) -> p m k", m=M)
        hflat = hT[:, :, :].rearrange("p c n -> p (c n)")
        sz = view(hflat, [[M * S, 2], [S, M], [1, S]])
        diag = sb("diag", [P, M, P])
        one = sb("one", [P, 1])
        at = 0
        u2, at = carve(at, M, N)
        dt, at = carve(at, M, N)
        xn, at = carve(at, B, C, S + TAPS - 1)
        head_at = at
        at += 2 * M * S
        ln_xc, at = carve(at, C, S)
        ln_sq, at = carve(at, C, S)
        ln_rstd, at = carve(at, S)
        ln_end = at
        up, at = carve(at, M, S + TAPS - 1)
        uc, at = carve(at, M, S)
        at = ln_end
        dec_w, at = carve(at, UD)
        dec_b, at = carve(at, D + 1)
        at = ln_end
        rest, _ = carve(head_at + 2 * M * S, M, S)
        dbl, at = carve(at, N)
        soft_e, at = carve(at, M, S)
        soft_l, at = carve(at, M, S)
        at = head_at
        decay, at = carve(at, 2, M, S)
        state, at = carve(at, 3, M, S)
        bc, at = carve(at, 2, 2, G, S)
        bc_dram = nc.dram_tensor("bc_scratch", (B, 2 * NS, S), F32, kind="Internal").ap()

        s_mam = sem("mamba_loaded")
        s_a = sem("a_exponent_ready")
        s_ln_mu = sem("ln_mean_product")
        s_ln_xc = sem("ln_centred")
        s_ln_sq = sem("ln_squared")
        s_ln_var = sem("ln_var_product")
        s_ln_rstd = sem("ln_rstd_ready")
        s_ln_out = sem("ln_scaled")
        s_up = sem("u_copied")
        s_cv = sem("convolved")
        s_pad = sem("pads_ready")
        s_xh0 = sem("residual_took_h0")
        s_u_mm = sem("u_products")
        s_u2 = sem("u2_ready")
        s_x_mm = sem("x_products")
        s_dbl = sem("dbl_ready")
        s_bc = sem("bc_written")
        s_dt_mm = sem("dt_products")
        s_soft = sem("softplus_parts")
        s_dt = sem("dt_ready")
        s_z_mm = sem("z_products")
        s_sz = sem("sz_ready")
        s_dterm = sem("d_term_product")
        s_du = sem("du_ready")
        s_bcl = [sem(f"bc_loaded{i}") for i in range(2)]
        s_decay = sem("decay_ready")
        s_dbu = sem("dbu_ready")
        s_scan = sem("scan_done")
        s_hc = sem("state_times_c")
        s_y = sem("y_accumulated")
        s_yz = sem("yz_ready")
        s_out_mm = sem("out_products")
        s_x1 = sem("x1_ready")


        u_t = sb("u_t", [KU, B, D + 1])
        s_dec = sem("decoder_loaded")
        s_dec_mm = sem("decoder_products")
        s_u_t = sem("u_t_ready")

        at = 0
        cw, at = carve(at, COND_W)
        wc = {k: view(cw, [[1, n]], a) for k, (a, n) in COND.items()}
        cut = lambda name, *dims: view(wc[name], [[int(np.prod(dims[j + 1:])), d] for j, d in enumerate(dims)])
        c2_w, ffn_w = cut("c2_w", C, D), cut("ffn_w", C, D)
        pw_t, cp_t, ms_t = cut("pw", 2, 2, C, P), cut("cp", 2, 2, C, P), cut("ms", 2, C, P)
        i_w1, i_w2 = cut("i_w1", 6, C, D), cut("i_w2", C, D)
        w_q, w_k, w_v = (cut(x, C, D) for x in ("w_q", "w_k", "w_v"))
        xm, at = carve(at, C, S)
        xh, at = carve(at, C, S)
        hh, at = carve(at, C, S)
        tt, at = carve(at, C, S)
        ss, at = carve(at, C, S)
        y3, at = carve(at, C, S)
        i1, at = carve(at, C, S)
        qf, at = carve(at, C, S)
        kf, at = carve(at, C, S)
        w2c, at = carve(at, C, D)
        rest_q, at = carve(at, C, S)
        oh_pw, at = carve(at, 2, S)
        oh_cp, at = carve(at, S)
        oh_ms, at = carve(at, S)
        wx, at = carve(at, C, D)
        assert at <= head_at + 2 * M * S, at
        qp, kp = (arena[:, ln_end + j * 3 * C * S // 2:ln_end + (j + 1) * 3 * C * S // 2]
                  .bitcast(BF16).rearrange("p (k c s) -> p k c s", k=3, c=C) for j in range(2))
        v_all, _ = carve(ARENA - B * TILES * D, B, TILES * D)
        ids = mam[:, 0:3 * S].bitcast(I32).rearrange("p (k s) -> p k s", k=3)

        def narrow(at, dtype, n):
            width = C * n * mybir.dt.size(dtype) // 4
            return arena[:, at:at + width].bitcast(dtype).rearrange("p (c s) -> p c s", c=C), at + width

        at3 = ln_end
        q8, at3 = narrow(at3, FP8, S)
        q8b, at3 = narrow(at3, FP8, D)
        q8c, at3 = narrow(at3, FP8, D)
        low, at3 = narrow(at3, BF16, S)
        yq, at3 = narrow(at3, BF16, S)
        wq8, at3 = narrow(at3, BF16, D)
        f16, at3 = narrow(at3, F16, S)
        awn = sb("awn", [P, 8])
        vh = sb("vh", [P, 3, C, B])
        vz = sb("vz", [P, 3, C, B])
        vsq = sb("vsq", [P, 3, C, B])
        vr = sb("vr", [P, 3, B])
        cvec = sb("cvec", [P, C, B])
        sums = sb("sums", [P, 2, B])
        sqk = sb("sqk", [P, 1])
        rho = sb("rho", [P, 2])
        q_dram = nc.dram_tensor("q_scratch", (B, P, 3 * C * S), BF16, kind="Internal").ap()
        k_dram = nc.dram_tensor("k_scratch", (B, P, 3 * C * S), BF16, kind="Internal").ap()

        s_cond = sem("cond_loaded")
        s_prep = sem("prep_by_vector")
        s_prep_mm = sem("prep_products")
        s_prep_act = sem("prep_by_scalar")
        s_xm = sem("xm_ready")
        s_c2_mm = sem("c2_products")
        s_yq = sem("yq_ready")
        s_ffn_mm = sem("ffn_products")
        s_f16 = sem("f16_ready")
        s_x2 = sem("x2_ready")
        s_ids = sem("ids_loaded")
        s_oh = sem("onehot_ready")
        s_xh = sem("xh_ready")
        s_g_mm = sem("gathered")
        s_g_used = sem("gathered_used")
        s_h1 = sem("h1_ready")
        s_cat = sem("cat_ready")
        s_i1_mm = sem("i1_products")
        s_i1 = sem("i1_ready")
        s_i2_mm = sem("i2_products")
        s_i2 = sem("i2_ready")
        s_y3 = sem("y3_ready")
        s_q_mm = sem("q_products")
        s_k_mm = sem("k_products")
        s_v_mm = sem("v_products")
        s_qf = sem("q_ready")
        s_kf = sem("k_ready")
        s_qp = sem("q_parts_ready")
        s_kp = sem("k_parts_ready")
        s_vs = sem("v_ready")
        s_q_out = sem("q_written")
        s_k_out = sem("k_written")

        at = 0
        fw, at = carve(at, FFN_W)
        wf = {k: view(fw, [[1, n]], a) for k, (a, n) in FFN.items()}
        fcut = lambda name, *dims: view(wf[name], [[int(np.prod(dims[j + 1:])), d] for j, d in enumerate(dims)])
        w_o = fcut("w_o", C, D)
        stack_at = at
        qstack, kstack = (arena[:, stack_at + j * H * S // 2:stack_at + (j + 1) * H * S // 2].bitcast(BF16)
                   .rearrange("p (g i s) -> p g i s", g=HG, i=HG) for j in range(2))
        at += H * S
        va, at = carve(at, TILES, H * SLOT)
        pt, at = carve(at, 4, 2, S)
        zn, zn_t, zt = (view(hflat, dims, off) for dims, off in (
            ([[D, TILES], [1, D]], 0), ([[S, C], [1, S]], TILES * D), ([[1, S]], TILES * D + C * S)))
        assert at <= ARENA - B * TILES * D, at
        mxs = sb("mxs", [P, 2, TILES, HG])
        mrow = sb("mrow", [HG, 2, S], BF16)
        zrec = sb("zrec", [P, TILES, HG])
        ssq = sb("ssq", [P, 2])
        s_fw = sem("w_o_loaded")
        s_ew = sem("expert_weights_loaded")
        s_rho_mm = sem("rho_product")
        s_rho_sum = sem("rho_mean_ready")
        s_rho_root = sem("rho_root_ready")
        s_rho = sem("rho_ready")
        s_heads = [sem(f"qk_stack_loaded{i}") for i in range(HG)]
        s_ones = sem("constant_rows_ready")
        s_va = sem("v_slots_ready")
        s_mrow = sem("max_row_ready")
        s_mrow_in = sem("max_row_in_stack")
        s_s_mm = sem("score_products")
        s_max = sem("max_ready")
        s_m_tr = sem("max_transposed")
        s_t_mm = sem("scoreT_products")
        s_pt = sem("exp_scores_ready")
        s_pv = sem("value_products")
        s_zt = sem("z_copied")
        s_z_tr = sem("z_transposed")
        s_zn = sem("z_normalised")
        s_zn_tr = sem("zn_transposed")
        s_znt = sem("zn_copied")
        s_wo_mm = sem("attention_out_products")
        s_x3 = sem("x3_ready")

        at = FFN_W
        assert FFN_W + 8 * S * 2 < ARENA
        gate_w, w1, w2 = fcut("gate_w", C, E), fcut("w1", C, E * FH), fcut("w2", FM, D)
        wgt_all, at = carve(at, B, C, D)
        wgt, at = carve(at, C, D)
        y4, at = carve(at, C, S)
        hid, at = carve(at, 4, S)
        ngb, at = carve(at, S)
        moe, at = carve(at, C, S)
        dbias = sb("dbias", [P, C, B])
        b2s = sb("b2s", [P, C])
        lg = sb("lg", [P, TILES, E])
        lg2 = sb("lg2", [P, TILES, E])
        gs = sb("gs", [P, 4, TILES])
        eps32 = sb("eps32", [P, 1])
        s_wgt_mm = sem("decoded_products")
        s_wgt_all = sem("decoded_ready")
        s_wgt = sem("decoded_copied")
        s_y4_mm = sem("y4_products")
        s_y4 = sem("y4_ready")
        s_gate_mm = sem("gate_products")
        s_gate_sq = sem("gate_squares")
        s_gate_r = sem("gate_rstd")
        s_gate_d = sem("gate_less_max")
        s_gate_e = sem("gate_exp")
        s_ng = sem("gate_factor")
        s_ngb_mm = sem("gate_factor_product")
        s_ngb = sem("gate_factor_spread")
        s_h_mm = sem("hidden_products")
        s_hid = sem("hidden_ready")
        s_e_mm = sem("expert_products")
        s_x4 = sem("x4_ready")
        s_out = sem("out_written")

        def ln_tensor(pe, x, k):
            pe.wait_ge(s_ln_xc, k + 1)
            for c in range(C):
                last = pe.matmul(ps[:, 6, :], mean, x[:, c, :], start=(c == 0), stop=(c == C - 1))
            last.then_inc(s_ln_mu, 1)
            pe.wait_ge(s_ln_sq, k + 1)
            pe.wait_ge(s_ln_rstd, k + 1)
            for c in range(C):
                last = pe.matmul(ps[:, 7, :], mean, ln_sq[:, c, :], start=(c == 0), stop=(c == C - 1))
            last.then_inc(s_ln_var, 1)

        def ln_scalar(act, k):
            act.wait_ge(s_ln_xc, k + 2)
            act.wait_ge(s_ln_var, k + 1)
            act.activation(ln_sq, ln_xc, ACT.Square).then_inc(s_ln_sq, 1)
            act.wait_ge(s_ln_var, k + 2)
            act.wait_ge(s_ln_out, k + 1)
            act.activation(ln_rstd, ps[:, 7, :], ACT.Ln, bias=eps[:, 1:2])
            act.drain()
            act.activation(ln_rstd, ln_rstd, ACT.Exp, scale=-0.5).then_inc(s_ln_rstd, 1)

        def ln_vector(dve, x, k):
            dve.wait_ge(s_ln_mu, k + 1)
            dve.wait_ge(s_ln_out, k + 1)
            mu = view(ps[:, 6, :], [[0, C], [1, S]])
            dve.tensor_tensor(ln_xc, x, mu, ALU.subtract).then_inc(s_ln_xc, 1)
            dve.wait_ge(s_ln_rstd, k + 2)
        block = ctx.enter_context(nc.Block())

        def debug_out(sp, name, ap):
            if name in dbg:
                sp.dma_start(dbg[name], ap).then_inc(s_dbg, 16)

        @block.sync
        def _(sp):
            for started in (s_q_out, s_k_out, s_mrow_in):
                sp.sem_inc(started, 1)
            sp.dma_start(early[:, :], t_in["early"]).then_inc(s_early, 16)
            x_dram = t_in["xT"]
            sp.dma_start(xb, x_dram[:, :, tok(0)]).then_inc(s_xb, 16)
            sp.dma_start(mam[:, :], t_in["mamba"]).then_inc(s_mam, 16)
            sp.dma_start(dec_w, t_in["dec_w"]).then_inc(s_dec, 16)
            sp.dma_start(dec_b[0:KU, :], t_in["dec_b"]).then_inc(s_dec, 16)
            sp.dma_start(xT[:, :, :], x_dram).then_inc(s_x, 16)
            with sp.Fori(1, B) as b:
                sp.wait_ge(s_kx_mm, b * TILES + 1)
                sp.dma_start(xb, x_dram[:, :, tok(b)]).then_inc(s_xb, 16)
            sp.wait_ge(s_h0, B + 1)
            debug_out(sp, "h0", hT[:, :, :])
            if "h0" in dbg:
                sp.wait_ge(s_dbg, 16)
                sp.sem_inc(s_x, 16)
            with sp.Fori(0, B) as b:
                sp.wait_ge(s_dbl, b + 2)
                sp.dma_start(bc_dram[bass.ds(b, 1)].rearrange("b r s -> r (b s)"),
                             dbl[RANK:RANK + 2 * NS, tok(b)]).then_inc(s_bc, 16)
            sp.wait_ge(s_bc, 16 * B)
            with sp.Fori(0, B) as b:
                for g in range(NS // G):
                    sp.wait_ge(s_hc, b * NS + G * (g + 1))
                    if g == 0:
                        sp.wait_ge(s_dt, B + 1)
                    src = bc_dram[bass.ds(b, 1)]
                    src = bass.AP(src.tensor, src.offset + g * G * S, [[0, P], [NS * S, 2], [S, G], [1, S]])
                    sp.dma_start(bc[:, g % 2], src).then_inc(s_bcl[g % 2], 16)
            sp.wait_ge(s_x1, B + 1)
            debug_out(sp, "x1", xT[:, :, :])
            if "x1" in dbg:
                sp.wait_ge(s_dbg, 32)
            sp.dma_start(cw, t_in["cond"]).then_inc(s_cond, 16)

            def load_ids(b):
                src = t_in["ids"][:, tok(b)]
                sp.dma_start(ids, bass.AP(src.tensor, src.offset, [[0, P], [N, 3], [1, S]])).then_inc(s_ids, 16)

            def store_parts(b):
                for stack, dram, ready, stored in ((qp, q_dram, s_qp, s_q_out), (kp, k_dram, s_kp, s_k_out)):
                    sp.wait_ge(ready, b + 2)
                    dst = dram[b] if isinstance(b, int) else dram[bass.ds(b, 1)].rearrange("b p n -> p (b n)")
                    sp.dma_start(dst, view(stack, [[1, 3 * C * S]])).then_inc(stored, 16)

            load_ids(0)
            with sp.Fori(0, B - 1) as b:
                sp.wait_ge(s_oh, b + 2)
                load_ids(b + 1)
                store_parts(b)
            store_parts(B - 1)
            debug_out(sp, "x2", xT[:, :, :])
            sp.wait_ge(s_vs, B + 1)
            sp.wait_ge(s_q_out, 16 * B + 1)
            sp.wait_ge(s_k_out, 16 * B + 1)
            cut_at = FFN["w1"][0]
            sp.dma_start(fw[:, 0:cut_at], t_in["ffn"][:, 0:cut_at]).then_inc(s_fw, 16)

            def load_heads(b, hg):
                for dram, stack, parts in ((q_dram, qstack, Q_PARTS), (k_dram, kstack, K_PARTS)):
                    for j, part in enumerate(parts):
                        src = dram[bass.ds(b, 1)] if not isinstance(b, int) else dram[b]
                        row = 3 * C * S
                        off = (hg % 2) * HG * DH * row + part * C * S + (hg // 2) * S
                        sp.dma_start(stack[j * DH:(j + 1) * DH, hg],
                                     bass.AP(src.tensor, src.offset + off, [[row, DH], [DH * row, HG], [1, S]])
                                     ).then_inc(s_heads[hg], 16)

            for hg in range(HG):
                load_heads(0, hg)
            sp.wait_ge(s_mrow, 2)
            sp.wait_ge(s_ones, 1)
            sp.dma_start(qstack[STACK:STACK + 1, 0], mrow[0:HG, 0, :]).then_inc(s_mrow_in, 16)
            sp.dma_start(fw[:, cut_at:], t_in["ffn"][:, cut_at:]).then_inc(s_ew, 16)

            def feed(b, last):
                for hg in range(HG):
                    g = b * HG + hg
                    nxt = (hg + 1) % HG
                    if not (last and hg == HG - 1):
                        sp.wait_ge(s_mrow, g + 3)
                        sp.dma_start(qstack[STACK:STACK + 1, nxt], mrow[0:HG, nxt % 2, :]).then_inc(s_mrow_in, 16)
                    if not last:
                        sp.wait_ge(s_t_mm, g * 8 + 8)
                        load_heads(b + 1, hg)

            with sp.Fori(0, B - 1) as b:
                feed(b, False)
            feed(B - 1, True)
            if "x3" in dbg:
                sp.wait_ge(s_x3, B * C + 1)
                debug_out(sp, "x3", xT[:, :, :])
            with sp.Fori(0, B) as b:
                sp.wait_ge(s_x4, b + 2)
                sp.dma_start(out[:, :, tok(b)], xT[:, :, tok(b)]).then_inc(s_out, 16)
            sp.wait_ge(s_out, 16 * B)
            sp.wait_ge(s_dbg, 16 * len(dbg))

        @block.tensor
        def _(pe):
            for started in (s_kx_mm, s_ln_var, s_ao_mm, s_out_mm, s_c2_mm, s_i2_mm, s_i1_mm, s_z_tr, s_wo_mm, s_h_mm, s_ngb_mm, s_pv):
                pe.sem_inc(started, 1)
            pe.wait_ge(s_early, 16)
            for j, name in enumerate(("k_aff", "o_aff", "c2_aff")):
                for c in range(C):
                    last = pe.matmul(ps[:, 0, (j * C + c) * B:(j * C + c + 1) * B],
                                     w[name][:, c * P:(c + 1) * P], w["condT"], start=True, stop=True)
            last.then_inc(s_style_mm, 1)
            pe.wait_ge(s_sq, 1)
            for b in range(B):
                for c in range(C):
                    pe.matmul(ps[:, 1 + b // 2, (b % 2) * D:(b % 2 + 1) * D],
                              style2[:, 0, c, b:b + 1].to_broadcast([P, P]), w2k[:, c, :],
                              start=(c == 0), stop=(c == C - 1))
            for o in range(C):
                for c in range(C):
                    last = pe.matmul(ps[:, 3, o * B:(o + 1) * B], w2o[:, c, o * P:(o + 1) * P],
                                     style2[:, 1, c, :], start=(c == 0), stop=(c == C - 1))
            last.then_inc(s_dem_mm, 1)
            pe.wait_ge(s_kw, 1)

            def kx_products(b, t):
                m = b * TILES + t
                if t == 0:
                    pe.wait_ge(s_xb, b * 16 + 16)
                pe.wait_ge(s_kx, m + 1)
                for c in range(C):
                    pe.matmul(ps[:, t % 2, 0:D], xb[:, c, t * P:(t + 1) * P],
                              kw_mod[:, bass.ds(b, 1), c, :], start=(c == 0), stop=False)
                pe.matmul(ps[:, t % 2, 0:D], ones[0:1, :], w["k_b"][0:1, :],
                          start=False, stop=True).then_inc(s_kx_mm, 1)

            def mix_products(b, t, first):
                n = b * TILES + t
                pe.wait_ge(s_mixv, n + 2)
                pe.wait_ge(s_mixp, n + 2)
                if not first or t >= 2:
                    pe.wait_ge(s_ao, n - 1)
                for c in range(C):
                    for s in range(H):
                        last = pe.matmul(ps[:, 4 + t % 2, c * P:(c + 1) * P],
                                         mix[:, t % 2, s, c * P:(c + 1) * P], ident,
                                         start=(s == 0), stop=(s == H - 1))
                last.then_inc(s_ao_mm, 1)

            def project(b):
                pe.wait_ge(s_ao, (b + 1) * TILES)
                pe.wait_ge(s_h0, b + 1)
                for o in range(C):
                    for c in range(C):
                        last = pe.matmul(ps[:, 6 + o, :], o_w[:, c, o * P:(o + 1) * P], aoT[:, c, tok(b)],
                                         start=(c == 0), stop=(c == C - 1))
                last.then_inc(s_o_mm, 1)

            def first_attention(b, first, final):
                for t in range(TILES):
                    if not (final and t >= 2):
                        kx_products(b + (t + 2) // TILES, (t + 2) % TILES)
                    mix_products(b, t, first)
                    if t == 2 and not first:
                        project(b - 1)

            kx_products(0, 0)
            kx_products(0, 1)
            first_attention(0, True, False)
            with pe.Fori(1, B - 1) as b:
                first_attention(b, False, False)
            first_attention(B - 1, False, True)
            project(B - 1)

            pe.wait_ge(s_h0, B + 1)
            pe.wait_ge(s_dec, 32)
            for b in range(B):
                ln_tensor(pe, hT[:, :, tok(b)], b)
                for i in range(b * (D + 1) // B, (b + 1) * (D + 1) // B):
                    last = pe.matmul(ps[0:KU, i // P, (i % P) * B:(i % P + 1) * B], dec_w[:, i * KU:(i + 1) * KU],
                                     w["condT"], start=True, stop=True)
            last.then_inc(s_dec_mm, 1)
            pe.wait_ge(s_u_t, 1)
            with pe.Fori(0, B) as b:
                pe.wait_ge(s_ln_out, b + 2)
                for m in range(M):
                    pe.wait_ge(s_up, b * M + m + 1)
                    for c in range(C):
                        last = pe.matmul(ps[:, m, :], w_u[:, c, m * P:(m + 1) * P],
                                         xn[:, bass.ds(b, 1), c, TAPS - 1:TAPS - 1 + S],
                                         start=(c == 0), stop=(c == C - 1))
                    last.then_inc(s_u_mm, 1)
            with pe.Fori(0, B) as b:
                pe.wait_ge(s_u2, (b + 2) * M)
                pe.wait_ge(s_dbl, b + 1)
                for m in range(M):
                    last = pe.matmul(ps[0:48, 4, :], w_x[:, m, :], u2[:, m, tok(b)],
                                     start=(m == 0), stop=(m == M - 1))
                last.then_inc(s_x_mm, 1)
                pe.wait_ge(s_dbl, b + 2)
                pe.wait_ge(s_up, (B + 1) * M)
                pe.wait_ge(s_soft, b + 1)
                for m in range(M):
                    last = pe.matmul(ps[:, m, :], wm["w_dt"][0:RANK, m * P:(m + 1) * P], dbl[0:RANK, tok(b)],
                                     start=True, stop=True)
                last.then_inc(s_dt_mm, 1)
            pe.wait_ge(s_soft, B + 1)

            def z_products(b, y):
                pe.wait_ge(s_x1, b)
                for m in range(M):
                    for c in range(C):
                        last = pe.matmul(ps[:, y + m, :], w_z[:, c, m * P:(m + 1) * P],
                                         xn[:, bass.ds(b, 1), c, TAPS - 1:TAPS - 1 + S],
                                         start=(c == 0), stop=(c == C - 1))
                last.then_inc(s_z_mm, 1)

            def d_term(b, y):
                pe.wait_ge(s_sz, b + 2)
                for m in range(M):
                    last = pe.matmul(ps[:, y + m, :], diag[:, m, :], u2[:, m, tok(b)], start=True, stop=False)
                last.then_inc(s_dterm, 1)

            def mamba_out(b, y, turn):
                pe.wait_ge(s_yz, b + 2)
                for o in range(C):
                    for m in range(M):
                        last = pe.matmul(ps[:, y + o, :], w_out[:, m, o * P:(o + 1) * P], sz[:, turn, m, :],
                                         start=(m == 0), stop=(m == M - 1))
                last.then_inc(s_out_mm, 1)

            def sum_states(b, turn, first, final):
                y, other = 4 * turn, 4 - 4 * turn
                for n in range(NS):
                    pe.wait_ge(s_hc, b * NS + n + 1 + 2 * G)
                    for m in range(M):
                        last = pe.matmul(ps[:, y + m, :], ident, state[:, (n + turn) % 3, m, :],
                                         start=False, stop=(n == NS - 1))
                    last.then_inc(s_y, 1)
                    if n == 1 and not first:
                        mamba_out(b - 1, other, 1 - turn)
                    if n == 6 and not final:
                        z_products(b + 1, other)
                    if n == 9 and not final:
                        d_term(b + 1, other)

            z_products(0, 0)
            d_term(0, 0)
            sum_states(0, 0, True, False)
            with pe.Fori(0, B // 2 - 1) as i:
                sum_states(2 * i + 1, 1, False, False)
                sum_states(2 * i + 2, 0, False, False)
            sum_states(B - 1, 1, False, True)
            mamba_out(B - 1, 4, 1)

            pe.wait_ge(s_x1, B + 1)
            pe.wait_ge(s_prep, 1)
            for o in range(C):
                for c in range(C):
                    pe.matmul(ps[:, 3, o * B:(o + 1) * B], w2c[:, c, o * P:(o + 1) * P],
                              style2[:, 2, c, :], start=(c == 0), stop=(c == C - 1))
            for j, rows_in in enumerate((128, 64, 32)):
                for o in range(C):
                    last = pe.matmul(ps[:, 4, (j * C + o) * B:(j * C + o + 1) * B],
                                     cut("v_w1", 3, D)[0:rows_in, j, o * P:(o + 1) * P],
                                     cut("v_in", 3, B)[0:rows_in, j, :], start=True, stop=True)
            last.then_inc(s_prep_mm, 1)
            pe.wait_ge(s_prep_act, 1)
            for j in range(3):
                for o in range(C):
                    for c in range(C):
                        last = pe.matmul(ps[:, 5, (j * C + o) * B:(j * C + o + 1) * B],
                                         cut("v_w2", 3, C, D)[:, j, c, o * P:(o + 1) * P], vh[:, j, c, :],
                                         start=(c == 0), stop=(c == C - 1))
            last.then_inc(s_prep_mm, 1)
            for k, x in enumerate((vz, vsq)):
                pe.wait_ge(s_prep, k + 2)
                for j in range(3):
                    for c in range(C):
                        last = pe.matmul(ps[:, 6 + k, j * B:(j + 1) * B], mean, x[:, j, c, :],
                                         start=(c == 0), stop=(c == C - 1))
                last.then_inc(s_prep_mm, 1)
            pe.wait_ge(s_prep, 4)
            for o in range(C):
                for j in range(3):
                    for c in range(C):
                        last = pe.matmul(ps[:, 5, o * B:(o + 1) * B], i_w1[:, 2 + j, c, o * P:(o + 1) * P],
                                         vz[:, j, c, :], start=(j + c == 0), stop=(j == 2 and c == C - 1))
            last.then_inc(s_prep_mm, 1)

            pe.wait_ge(s_prep, 5)
            with pe.Fori(0, B) as b:
                pe.wait_ge(s_xm, b + 1)
                pe.wait_ge(s_yq, b + 1)
                for o in range(C):
                    for c in range(C):
                        last = pe.matmul(ps[:, o, :], c2_w[:, c, o * P:(o + 1) * P], xm[:, c, :],
                                         start=(c == 0), stop=(c == C - 1))
                last.then_inc(s_c2_mm, 1)
                pe.wait_ge(s_yq, b + 2)
                pe.wait_ge(s_f16, b + 1)
                for o in range(C):
                    for c in range(C):
                        last = pe.matmul(ps[:, 2 + o, :], wq8[:, c, o * P:(o + 1) * P], yq[:, c, :],
                                         start=(c == 0), stop=(c == C - 1))
                last.then_inc(s_ffn_mm, 1)

            def gather(b, i, table, onehot, parts):
                pe.wait_ge(s_g_used, b * 5 + i + 1)
                for j in range(2):
                    for c in range(C):
                        for k in range(parts):
                            last = pe.matmul(ps[:, 2 * j + c, :], table(k, j, c), onehot(k),
                                             start=(k == 0), stop=(k == parts - 1))
                last.then_inc(s_g_mm, 1)

            pe.wait_ge(s_x2, B + 1)
            with pe.Fori(0, B) as b:
                ln_tensor(pe, xT[:, :, tok(b)], B + 3 * b)
                pe.wait_ge(s_oh, b + 2)
                gather(b, 0, lambda k, j, c: pw_t[:, k, j, c, :], lambda k: oh_pw[:, k, :], 2)
                pe.wait_ge(s_h1, b + 1)
                ln_tensor(pe, hh, B + 3 * b + 1)
                gather(b, 1, lambda k, j, c: cp_t[:, 0, j, c, :], lambda k: oh_cp, 1)
                gather(b, 2, lambda k, j, c: cp_t[:, 1, j, c, :], lambda k: oh_cp, 1)
                gather(b, 3, lambda k, j, c: ms_t[:, j, c, :], lambda k: oh_ms, 1)
                pe.wait_ge(s_g_used, b * 5 + 5)
                pe.wait_ge(s_i1, b + 1)
                for o in range(C):
                    src = [(i_w1[:, 0], hh), (i_w1[:, 1], tt), (i_w1[:, 5], ss), (wx, xT[:, :, tok(b)])]
                    for i, (wt, x) in enumerate(src):
                        for c in range(C):
                            last = pe.matmul(ps[:, 4 + o, :], wt[:, c, o * P:(o + 1) * P], x[:, c, :],
                                             start=(i + c == 0), stop=(i == 3 and c == C - 1))
                last.then_inc(s_i1_mm, 1)
                pe.wait_ge(s_i1, b + 2)
                for o in range(C):
                    for c in range(C):
                        last = pe.matmul(ps[:, o, :], i_w2[:, c, o * P:(o + 1) * P], i1[:, c, :],
                                         start=(c == 0), stop=(c == C - 1))
                last.then_inc(s_i2_mm, 1)
                pe.wait_ge(s_i2, b + 1)
                ln_tensor(pe, y3, B + 3 * b + 2)
                pe.wait_ge(s_y3, b + 1)
                for bank, wt, done in ((0, w_q, s_q_mm), (2, w_k, s_k_mm)):
                    for g in range(C):
                        for c in range(C):
                            last = pe.matmul(ps[:, bank + g, :], wt[:, c, g * P:(g + 1) * P], y3[:, c, :],
                                             start=(c == 0), stop=(c == C - 1))
                    last.then_inc(done, 1)
                for t in range(TILES):
                    for c in range(C):
                        last = pe.matmul(ps[:, 4 + t // 2, (t % 2) * D:(t % 2 + 1) * D], y3[:, c, t * P:(t + 1) * P],
                                         w_v[:, c, :], start=(c == 0), stop=(c == C - 1))
                last.then_inc(s_v_mm, 1)
                pe.wait_ge(s_qf, b + 2)
                pe.wait_ge(s_kf, b + 2)
                pe.wait_ge(s_vs, b + 2)

            pe.matmul(ps[:, 5, 0:2 * B], ones, sums[:, :, :], start=True, stop=True).then_inc(s_rho_mm, 1)

            def scores(b, hg, s):
                i, qc = s % HG, s // HG
                if s == 0:
                    pe.wait_ge(s_heads[hg], (b + 1) * 2 * len(Q_PARTS) * 16)
                pe.wait_ge(s_max, (b * HG + hg) * 16 + s + 1)
                pe.matmul(ps[:, s % 2, :], qstack[0:STACK, hg, i, qc * P:(qc + 1) * P], kstack[0:STACK, hg, i, :],
                          start=True, stop=True).then_inc(s_s_mm, 1)

            def max_rows(b, hg):
                g = b * HG + hg
                pe.wait_ge(s_max, g * 16 + 18)
                for t in range(TILES):
                    last = pe.transpose(ps[0:HG, 7, t * P:(t + 1) * P], mxs[:, hg % 2, t, :], ident)
                last.then_inc(s_m_tr, 1)

            def values(b, hg, kc):
                g = b * HG + hg
                pe.wait_ge(s_pt, g * 8 + 2 * kc + 4)
                if kc == 0:
                    pe.wait_ge(s_zt, g + 1)
                    pe.wait_ge(s_va, g + 1)
                for i in range(HG):
                    h = hg * HG + i
                    last = pe.matmul(ps[i * SLOT:(i + 1) * SLOT, 6, :], va[:, kc, h * SLOT:(h + 1) * SLOT],
                                     pt[:, (2 * kc + i // 2) % 4, i % 2, :], start=(kc == 0), stop=(kc == TILES - 1))
                last.then_inc(s_pv, 1)

            def z_rows(b, hg):
                g = b * HG + hg
                pe.wait_ge(s_zt, g + 2)
                for t in range(TILES):
                    last = pe.transpose(ps[:, 7, t * P:(t + 1) * P], zt[:, t * P:(t + 1) * P], ident)
                last.then_inc(s_z_tr, 1)

            def zn_columns(b, c):
                pe.wait_ge(s_zn, (b + 1) * HG + 1)
                if c:
                    pe.wait_ge(s_znt, b * C + c + 1)
                for t in range(TILES):
                    last = pe.transpose(ps[:, 7, t * P:(t + 1) * P], zn[:, t, c * P:(c + 1) * P], ident)
                last.then_inc(s_zn_tr, 1)

            def attention_out(b, o):
                pe.wait_ge(s_znt, (b + 1) * C + 1)
                pe.wait_ge(s_x3, b * C + o + 1)
                for c in range(C):
                    last = pe.matmul(ps[:, 7, :], w_o[:, c, o * P:(o + 1) * P], zn_t[:, c, :],
                                     start=(c == 0), stop=(c == C - 1))
                last.then_inc(s_wo_mm, 1)

            def attend(b, first, final):
                for hg in range(HG):
                    g = b * HG + hg
                    ahead = (b + (hg + 2) // HG, (hg + 2) % HG)
                    pe.wait_ge(s_mrow_in, 16 * (g + 1) + 1)
                    for j in range(8):
                        kc, pair = j // 2, j % 2
                        pe.wait_ge(s_pt, g * 8 + j + 1)
                        for i in (2 * pair, 2 * pair + 1):
                            last = pe.matmul(ps[:, 2 + 2 * pair + i % 2, :], kstack[:, hg, i, kc * P:(kc + 1) * P],
                                             qstack[:, hg, i, :], start=True, stop=True)
                        last.then_inc(s_t_mm, 1)
                        if not (final and hg >= 2):
                            scores(*ahead, 2 * j)
                            scores(*ahead, 2 * j + 1)
                        if j % 2 == 0 and j:
                            values(b, hg, kc - 1)
                        if j < 2 and hg == 1 and not first:
                            zn_columns(b - 1, j)
                        if j == 2 and not (final and hg == HG - 1):
                            if hg == 1 and not first:
                                pe.wait_ge(s_znt, b * C + 1)
                            elif not (first and hg == 0):
                                pe.wait_ge(s_zn, g)
                            max_rows(b + (hg + 1) // HG, (hg + 1) % HG)
                        if j in (3, 4) and hg == 1 and not first:
                            pe.wait_ge(s_mrow, g + 3)
                            attention_out(b - 1, j - 3)
                        if j == 5 and not (first and hg == 0):
                            if not (final and hg == HG - 1):
                                pe.wait_ge(s_mrow, g + 3)
                            else:
                                pe.wait_ge(s_zn, g)
                            if hg == 1:
                                pe.wait_ge(s_x3, b * C + 1)
                            z_rows(*((b, hg - 1) if hg else (b - 1, HG - 1)))
                    values(b, hg, TILES - 1)

            pe.wait_ge(s_fw, 16)
            pe.wait_ge(s_rho_sum, 1)
            pe.wait_ge(s_ones, 1)
            for hg in range(2):
                for s in range(16):
                    scores(0, hg, s)
                if hg == 0:
                    max_rows(0, 0)
            pe.wait_ge(s_mrow, 2)
            attend(0, True, False)
            with pe.Fori(1, B - 1) as b:
                attend(b, False, False)
            attend(B - 1, False, True)
            pe.wait_ge(s_zn, B * HG)
            z_rows(B - 1, HG - 1)
            for c in range(C):
                zn_columns(B - 1, c)
            for o in range(C):
                attention_out(B - 1, o)

            pe.wait_ge(s_ew, 16)
            pe.wait_ge(s_x3, B * C + 1)
            for b in range(B):
                for c in range(C):
                    pe.matmul(ps[:, b, c * D:(c + 1) * D], u_t[:, b, c * P:(c + 1) * P], wf["v_dec"][0:KU, :],
                              start=True, stop=True)
            for o in range(C):
                last = pe.matmul(ps[:, 4, o * B:(o + 1) * B], wf["v_dec"][0:KU, o * P:(o + 1) * P], u_t[:, :, D],
                                 start=True, stop=True)
            last.then_inc(s_wgt_mm, 1)

            def hidden(n, f):
                pe.wait_ge(s_hid, n * FM + f + 1)
                for c in range(C):
                    last = pe.matmul(ps[:, 2 + f % 4, :], w1[:, c, f * P:(f + 1) * P], y4[:, c, :],
                                     start=(c == 0), stop=(c == C - 1))
                last.then_inc(s_h_mm, 1)

            with pe.Fori(0, B) as b:
                pe.wait_ge(s_wgt, b + 1)
                pe.wait_ge(s_x4, b + 1)
                for o in range(C):
                    for c in range(C):
                        last = pe.matmul(ps[:, o, :], wgt[:, c, o * P:(o + 1) * P], xT[:, c, tok(b)],
                                         start=(c == 0), stop=(c == C - 1))
                last.then_inc(s_y4_mm, 1)
                pe.wait_ge(s_y4, b + 2)
                for t in range(TILES):
                    for c in range(C):
                        last = pe.matmul(ps[:, 6, t * E:(t + 1) * E], y4[:, c, t * P:(t + 1) * P], gate_w[:, c, :],
                                         start=(c == 0), stop=(c == C - 1))
                last.then_inc(s_gate_mm, 1)
                for f in range(FM + 2):
                    if f < FM:
                        hidden(b, f)
                    if f >= 2:
                        pe.wait_ge(s_hid, b * FM + f - 2 + 5)
                        for o in range(C):
                            last = pe.matmul(ps[:, o, :], w2[:, f - 2, o * P:(o + 1) * P], hid[:, (f - 2) % 4, :],
                                             start=(f == 2), stop=(f == FM + 1))
                        last.then_inc(s_e_mm, 1)
                    if f == FM // 2:
                        pe.wait_ge(s_ng, b + 1)
                        for t in range(TILES):
                            last = pe.matmul(ps[:, 7, t * P:(t + 1) * P], gs[:, 3, t:t + 1].to_broadcast([P, P]),
                                             ident, start=True, stop=True)
                        last.then_inc(s_ngb_mm, 1)


        @block.scalar
        def _(act):
            for started in (s_h0, s_ln_rstd, s_dbl, s_soft, s_sz, s_f16, s_i1, s_zt, s_y4, s_vs, s_znt, s_qf, s_kf, s_mrow):
                act.sem_inc(started, 1)
            act.preload_act_table_set("natural_log_exp_and_others")
            act.sem_inc(s_kx, 2)
            act.wait_ge(s_dem_mm, 1)
            act.activation(demk, ps[:, 1:3, :], ACT.Ln, bias=eps[:, 0:1])
            act.activation(dem[:, 0], ps[:, 3, 0:C * B], ACT.Ln, bias=eps[:, 0:1])
            act.drain()
            act.activation(dem[:, 0], dem[:, 0], ACT.Exp, scale=-0.5)
            act.activation(demk, demk, ACT.Exp, scale=-0.5).then_inc(s_dem_ln, 1)

            def kx_copies(b, t, first):
                m = b * TILES + t
                act.wait_ge(s_kx_mm, m + 2)
                if not first:
                    act.wait_ge(s_mixv, m - 2)
                    act.wait_ge(s_mixp, m - 2)
                act.activation(kx[:, t, 0:D], ps[:, t % 2, 0:D], ACT.Copy)
                act.activation(kx[:, t, D:2 * D], ps[:, t % 2, 0:D], ACT.Copy).then_inc(s_kx, 1)

            def other_half(b, t):
                act.wait_ge(s_red, b * TILES + t + 1)
                act.activation(view(full[:, t % 2], [[2 * H, H - HALF], [1, H]], 2 * H + H),
                               view(full[:, t % 2], [[2 * H, H - HALF], [1, H]], 2 * H), ACT.Copy)
                act.drain()
                act.activation(view(full[:, t % 2], [[2 * H, H - HALF], [1, H]], HALF * 2 * H),
                               view(full[:, t % 2], [[1 - 2 * H, H - HALF], [1, H]], (H - HALF) * 2 * H + HALF),
                               ACT.Copy).then_inc(s_full, 1)

            def gathered(b, t):
                n = b * TILES + t
                act.wait_ge(s_ao_mm, n + 2)
                apart(act)
                for c in range(C):
                    last = act.activation(aoT[:, c, bass.ds(n * P, P)], ps[:, 4 + t % 2, c * P:(c + 1) * P],
                                          ACT.Copy, scale=style[:, 1, c, bass.ds(b, 1)])
                last.then_inc(s_ao, 1)

            def h0_out(b):
                act.wait_ge(s_o_mm, b + 1)
                apart(act)
                for o in range(C):
                    last = act.activation(hT[:, o, tok(b)], ps[:, 6 + o, :], ACT.Identity,
                                          bias=w["o_b"][:, o:o + 1], scale=dem[:, 0, o, bass.ds(b, 1)])
                last.then_inc(s_h0, 1)

            def first_attention(b, first, final):
                for t in range(TILES):
                    act.wait_ge(s_diff, b * TILES + t + 1)
                    act.activation(att[:, t % 2, :], diff[:, t % 2, :], ACT.Exp, scale=0.25).then_inc(s_exp, 1)
                    if not (final and t >= 2):
                        kx_copies(b + (t + 2) // TILES, (t + 2) % TILES, first and t < 2)
                    if not (final and t == TILES - 1):
                        other_half(b + (t + 1) // TILES, (t + 1) % TILES)
                    if not first or t >= 2:
                        gathered(b - 1 + (t + 2) // TILES, (t + 2) % TILES)
                    if t == 2 and not first:
                        h0_out(b - 1)

            kx_copies(0, 0, True)
            kx_copies(0, 1, True)
            other_half(0, 0)
            first_attention(0, True, False)
            with act.Fori(1, B - 1) as b:
                first_attention(b, False, False)
            first_attention(B - 1, False, True)
            gathered(B - 1, 2)
            gathered(B - 1, 3)
            h0_out(B - 1)

            act.wait_ge(s_mam, 16)
            act.activation(a_neg, a_neg, ACT.Exp).then_inc(s_a, 1)
            with act.Fori(0, B) as b:
                ln_scalar(act, b)
            act.sem_inc(s_up, M)
            act.sem_inc(s_u2, M)
            act.wait_ge(s_pad, 1)
            with act.Fori(0, B) as b:
                for m in range(M):
                    act.wait_ge(s_u_mm, b * M + m + 1)
                    act.wait_ge(s_cv, b * M + m + 1)
                    act.activation(up[:, m, TAPS - 1:], ps[:, m, :], ACT.Copy).then_inc(s_up, 1)
                for m in range(M):
                    act.wait_ge(s_cv, (b + 1) * M + m + 1)
                    apart(act)
                    act.activation(u2[:, m, tok(b)], uc[:, m, :], ACT.Silu,
                                   bias=wm["conv_b"][:, m:m + 1]).then_inc(s_u2, 1)
            act.preload_act_table_set("natural_log_exp_and_others")
            with act.Fori(0, B) as b:
                act.wait_ge(s_x_mm, b + 1)
                apart(act)
                act.activation(dbl[0:48, tok(b)], ps[0:48, 4, :], ACT.Copy).then_inc(s_dbl, 1)
                act.wait_ge(s_dt_mm, b + 1)
                act.wait_ge(s_dt, b + 1)
                apart(act)
                for m in range(M):
                    act.activation(soft_e[:, m, :], ps[:, m, :], ACT.Abs, bias=wm["b_dt"][:, m:m + 1])
                    act.activation(dt[:, m, tok(b)], ps[:, m, :], ACT.Relu, bias=wm["b_dt"][:, m:m + 1])
                act.drain()
                act.activation(soft_e, soft_e, ACT.Exp, scale=-1.0)
                act.drain()
                act.activation(soft_l, soft_e, ACT.Ln, bias=one[:, 0:1]).then_inc(s_soft, 1)
            act.sem_inc(s_scan, 2)
            act.wait_ge(s_dt, B + 1)
            act.drain()
            act.wait_ge(s_xh0, 1)

            def gate_z(b, turn):
                act.wait_ge(s_z_mm, b + 1)
                act.wait_ge(s_out_mm, b)
                act.activation(sz[:, turn], ps[:, 4 * turn:4 * turn + 4, :], ACT.Silu).then_inc(s_sz, 1)

            def decays(b, turn, final):
                for n in range(NS):
                    act.wait_ge(s_scan, b * NS + n + 1)
                    apart(act)
                    for m in range(M):
                        last = act.activation(decay[:, n % 2, m, 1:S], dt[:, m, bass.ds(b * S + 1, S - 1)],
                                              ACT.Exp, scale=a_neg[:, m * NS + n:m * NS + n + 1])
                    last.then_inc(s_decay, 1)
                    if n == 9 and not final:
                        gate_z(b + 1, 1 - turn)

            gate_z(0, 0)
            decays(0, 0, False)
            with act.Fori(0, B // 2 - 1) as i:
                decays(2 * i + 1, 1, False)
                decays(2 * i + 2, 0, False)
            decays(B - 1, 1, True)

            act.wait_ge(s_prep_mm, 1)
            for j in range(3):
                for c in range(C):
                    last = act.activation(vh[:, j, c, :], ps[:, 4, (j * C + c) * B:(j * C + c + 1) * B], ACT.Silu,
                                          bias=cut("v_b1", 3, C)[:, j, c:c + 1])
            last.then_inc(s_prep_act, 1)
            act.preload_act_table_set("natural_log_exp_and_others")
            act.activation(dem[:, 1], ps[:, 3, 0:C * B], ACT.Ln, bias=eps[:, 0:1])
            act.drain()
            act.activation(dem[:, 1], dem[:, 1], ACT.Exp, scale=-0.5).then_inc(s_prep_act, 1)
            act.wait_ge(s_prep, 1)
            act.activation(awn[:, 0:6], awn[:, 0:6], ACT.Exp).then_inc(s_prep_act, 1)
            act.wait_ge(s_prep_mm, 4)
            act.activation(vr[:, :, :], ps[:, 7, 0:3 * B], ACT.Ln, bias=eps[:, 1:2])
            act.drain()
            act.activation(vr[:, :, :], vr[:, :, :], ACT.Exp, scale=-0.5).then_inc(s_prep_act, 1)
            with act.Fori(0, B) as b:
                act.wait_ge(s_x1, B + 1)
                act.wait_ge(s_c2_mm, b + 1)
                apart(act)
                for c in range(C):
                    last = act.activation(xm[:, c, :], xT[:, c, tok(b)], ACT.Copy, scale=style[:, 2, c, bass.ds(b, 1)])
                last.then_inc(s_xm, 1)
                act.wait_ge(s_ffn_mm, b + 1)
                act.wait_ge(s_x2, b + 1)
                act.activation(f16, ps[:, 2:4, :], ACT.Copy).then_inc(s_f16, 1)
            with act.Fori(0, B) as b:
                act.preload_act_table_set("natural_log_exp_and_others")
                ln_scalar(act, B + 3 * b)
                ln_scalar(act, B + 3 * b + 1)
                act.wait_ge(s_i1_mm, b + 2)
                act.wait_ge(s_i2_mm, b + 1)
                apart(act)
                for o in range(C):
                    last = act.activation(i1[:, o, :], ps[:, 4 + o, :], ACT.Silu, bias=cvec[:, o, bass.ds(b, 1)])
                last.then_inc(s_i1, 1)
                act.preload_act_table_set("natural_log_exp_and_others")
                ln_scalar(act, B + 3 * b + 2)
                act.wait_ge(s_q_mm, b + 1)
                act.wait_ge(s_qp, b + 1)
                apart(act)
                act.activation(qf, ps[:, 0:2, :], ACT.Square, accum_out=sums[:, 0, bass.ds(b, 1)])
                act.drain()
                act.activation(qf, ps[:, 0:2, :], ACT.Copy, scale=sqk[:, 0:1]).then_inc(s_qf, 1)
                act.wait_ge(s_k_mm, b + 1)
                act.wait_ge(s_kp, b + 1)
                apart(act)
                act.activation(kf, ps[:, 2:4, :], ACT.Square, accum_out=sums[:, 1, bass.ds(b, 1)])
                act.drain()
                act.activation(kf, ps[:, 2:4, :], ACT.Copy).then_inc(s_kf, 1)
                act.wait_ge(s_v_mm, b + 1)
                apart(act)
                act.activation(v_all[:, bass.ds(b, 1)], ps[:, 4:6, :], ACT.Copy).then_inc(s_vs, 1)
            act.wait_ge(s_rho_sum, 1)
            act.activation(rho[:, :], ssq[:, :], ACT.Ln, scale=1.0 / (N * D))
            act.drain()
            act.activation(rho[:, :], rho[:, :], ACT.Exp, scale=0.5).then_inc(s_rho_root, 1)
            act.sem_inc(s_pt, 2)
            act.wait_ge(s_rho, 1)

            def max_row(g, parity):
                act.wait_ge(s_m_tr, g + 1)
                act.wait_ge(s_mrow_in, 16 * g - 15)
                act.activation(mrow[:, parity, :], ps[0:HG, 7, :], ACT.Copy).then_inc(s_mrow, 1)

            def weigh(b, first, final):
                for hg in range(HG):
                    g = b * HG + hg
                    for j in range(8):
                        n = g * 8 + j
                        act.wait_ge(s_t_mm, n + 1)
                        act.wait_ge(s_pv, g * TILES + j // 2)
                        act.activation(pt[:, j % 4], ps[:, 2 + 2 * (j % 2):4 + 2 * (j % 2), :], ACT.Exp,
                                       scale=rho[:, 0:1]).then_inc(s_pt, 1)
                        if hg == 1 and j in (1, 2) and not first:
                            act.wait_ge(s_zn_tr, (b - 1) * C + j)
                            act.wait_ge(s_wo_mm, (b - 1) * C + 1)
                            act.activation(zn_t[:, j - 1, :], ps[:, 7, :], ACT.Copy).then_inc(s_znt, 1)
                        if j == 3 and not (final and hg == HG - 1):
                            max_row(g + 1, (hg + 1) % 2)
                    act.wait_ge(s_pv, g * TILES + TILES + 1)
                    act.wait_ge(s_z_tr, g + 1)
                    act.activation(zt, ps[:, 6, :], ACT.Copy).then_inc(s_zt, 1)

            act.wait_ge(s_m_tr, 1)
            act.activation(mrow[:, 0, :], ps[0:HG, 7, :], ACT.Copy).then_inc(s_mrow, 1)
            weigh(0, True, False)
            with act.Fori(1, B - 1) as b:
                weigh(b, False, False)
            weigh(B - 1, False, True)
            for c in range(C):
                act.wait_ge(s_zn_tr, (B - 1) * C + c + 1)
                act.wait_ge(s_wo_mm, (B - 1) * C + 1)
                act.activation(zn_t[:, c, :], ps[:, 7, :], ACT.Copy).then_inc(s_znt, 1)
            act.sem_inc(s_hid, 4)
            with act.Fori(0, B) as b:
                act.wait_ge(s_y4_mm, b + 1)
                act.wait_ge(s_h_mm, b * FM + 1)
                apart(act)
                for o in range(C):
                    last = act.activation(y4[:, o, :], ps[:, o, :], ACT.Identity, bias=dbias[:, o, bass.ds(b, 1)])
                last.then_inc(s_y4, 1)
                act.wait_ge(s_gate_sq, b + 1)
                act.activation(gs[:, 1, :], gs[:, 0, :], ACT.Ln, scale=1.0 / E, bias=eps32[:, 0:1])
                act.drain()
                act.activation(gs[:, 1, :], gs[:, 1, :], ACT.Exp, scale=-0.5).then_inc(s_gate_r, 1)
                act.wait_ge(s_gate_d, b + 1)
                act.activation(lg[:, :, :], lg[:, :, :], ACT.Exp, scale=2.0).then_inc(s_gate_e, 1)
                for f in range(FM):
                    n = b * FM + f
                    act.wait_ge(s_h_mm, n + 2)
                    act.wait_ge(s_e_mm, n + 1)
                    act.activation(hid[:, f % 4, :], ps[:, 2 + f % 4, :], ACT.Gelu,
                                   bias=wf["b1"][:, f:f + 1]).then_inc(s_hid, 1)
                act.preload_act_table_set("natural_log_exp_and_others")
                act.wait_ge(s_ngb_mm, b + 2)
                act.wait_ge(s_x4, b + 1)
                act.activation(ngb, ps[:, 7, :], ACT.Copy).then_inc(s_ngb, 1)


        @block.vector
        def _(dve):
            for started in (s_ln_xc, s_ln_out, s_x1, s_yz, s_yq, s_g_used, s_x3, s_x4, s_dt, s_x2, s_mixv, s_zn, s_oh):
                dve.sem_inc(started, 1)
            for j, v in enumerate((1e-8, 1e-5, 1e-6)):
                dve.memset(eps[:, j:j + 1], v)
            dve.wait_ge(s_early, 16)
            dve.tensor_tensor(w2k, k_w, k_w, ALU.mult)
            dve.tensor_tensor(w2o, o_w, o_w, ALU.mult)
            dve.wait_ge(s_style_mm, 1)
            for j, (name, gain) in enumerate((("k_affb", 1.0), ("o_affb", 1.0), ("c2_affb", float(P) ** -0.5))):
                for c in range(C):
                    dve.tensor_scalar(style[:, j, c, :], ps[:, 0, (j * C + c) * B:(j * C + c + 1) * B],
                                      gain, w[name][:, c:c + 1], ALU.mult, ALU.add)
            dve.drain()
            dve.tensor_tensor(style2[:, :, :, :], style[:, :, :, :], style[:, :, :, :], ALU.mult).then_inc(s_sq, 1)
            dve.wait_ge(s_dem_ln, 1)
            for b in range(B):
                for c in range(C):
                    last = dve.scalar_tensor_tensor(kw_mod[:, b, c, :], k_w[:, c, :], style[:, 0, c, b:b + 1],
                                                    demk[:, b, :], ALU.mult, ALU.mult)
            last.then_inc(s_kw, 1)

            def half_scores(b, t):
                dve.wait_ge(s_kx, b * TILES + t + 3)
                k = kx[:, t, :]
                dve.tensor_tensor(prod, view(k, [[0, HALF], [DH, H], [1, DH]]),
                                  view(k, [[DH, HALF], [DH, H], [1, DH]]), ALU.mult)
                dve.drain()
                dve.tensor_reduce(view(full[:, t % 2], [[2 * H, HALF], [1, H]]), prod, AX, ALU.add).then_inc(s_red, 1)

            def first_attention(b, first, final):
                for t in range(TILES):
                    n = b * TILES + t
                    u = t % 2
                    k = kx[:, t, :]
                    dve.wait_ge(s_full, n + 1)
                    dve.tensor_reduce(mx[:, u, :], view(full[:, u], [[1, H], [2 * H, H]]), AX, ALU.max)
                    dve.drain()
                    dve.tensor_tensor(view(diff[:, u], [[H, H], [1, H]]), view(full[:, u], [[2 * H, H], [1, H]]),
                                      view(mx[:, u], [[0, H], [1, H]]), ALU.subtract).then_inc(s_diff, 1)
                    if not (final and t == TILES - 1):
                        half_scores(b + (t + 1) // TILES, (t + 1) % TILES)
                    dve.wait_ge(s_exp, n + 1)
                    dve.tensor_reduce(ssum[:, u, :], view(att[:, u], [[1, H], [H, H]]), AX, ALU.add)
                    dve.drain()
                    dve.reciprocal(ssum[:, u, :], ssum[:, u, :])
                    dve.drain()
                    if not first or t >= 2:
                        dve.wait_ge(s_mixp, n)
                        dve.wait_ge(s_ao_mm, n)
                    dve.tensor_tensor(view(att_p[:, u], [[H, H], [1, H]]), view(att[:, u], [[H, H], [1, H]]),
                                      view(ssum[:, u], [[0, H], [1, H]]), ALU.mult).then_inc(s_att, 1)
                    dve.drain()
                    dve.tensor_tensor(view(mix[:, u, POOL_SH], [[D, H - POOL_SH], [DH, H], [1, DH]]),
                                      view(att_p[:, u], [[H, H - POOL_SH], [1, H], [0, DH]], POOL_SH * H),
                                      view(k, [[DH, H - POOL_SH], [DH, H], [1, DH]], POOL_SH * DH),
                                      ALU.mult).then_inc(s_mixv, 1)

            half_scores(0, 0)
            first_attention(0, True, False)
            with dve.Fori(1, B - 1) as b:
                first_attention(b, False, False)
            first_attention(B - 1, False, True)

            dve.memset(one[:, :], 1.0)
            dve.wait_ge(s_h0, B + 1)
            dve.wait_ge(s_mam, 16)
            dve.wait_ge(s_a, 1)
            dve.tensor_scalar(a_neg, a_neg, -1.0, None, ALU.mult)
            for m in range(M):
                dve.tensor_scalar(diag[:, m, :], ident, wm["d"][:, m:m + 1], None, ALU.mult)
            for b in range(B):
                dve.memset(xn[:, b, :, 0:TAPS - 1], 0.0)
            with dve.Fori(0, B) as b:
                ln_vector(dve, hT[:, :, tok(b)], b)
                for c in range(C):
                    dve.scalar_tensor_tensor(ln_xc[:, c, :], ln_xc[:, c, :], wm["gamma"][:, c:c + 1], ln_rstd,
                                             ALU.mult, ALU.mult)
                dve.drain()
                for c in range(C):
                    last = dve.tensor_scalar(xn[:, bass.ds(b, 1), c, TAPS - 1:TAPS - 1 + S], ln_xc[:, c, :],
                                             wm["beta"][:, c:c + 1], None, ALU.add)
                last.then_inc(s_ln_out, 1)
            dve.wait_ge(s_dec_mm, 1)
            for i, n in ((0, P), (1, P), (2, 1)):
                last = dve.tensor_tensor(view(u_t[:, 0, i * P:i * P + n], [[D + 1, B], [1, n]]),
                                         view(ps[0:KU, i, :], [[1, B], [B, n]]),
                                         view(dec_b[0:KU, i * P:i * P + n], [[0, B], [1, n]]), ALU.add)
            last.then_inc(s_u_t, 1)
            dve.sem_inc(s_cv, M)
            dve.drain()
            for m in range(M):
                last = dve.memset(up[:, m, 0:TAPS - 1], 0.0)
            last.then_inc(s_pad, 1)
            with dve.Fori(0, B) as b:
                for m in range(0, M, 2):
                    for i in (m, m + 1):
                        dve.wait_ge(s_up, (b + 1) * M + i + 1)
                        dve.wait_ge(s_u2, b * M + i + 1)
                        dve.tensor_scalar(uc[:, i, :], up[:, i, 0:S], conv[:, i, 0:1], None, ALU.mult)
                    for k in range(1, TAPS):
                        dve.drain()
                        for i in (m, m + 1):
                            last = dve.scalar_tensor_tensor(uc[:, i, :], up[:, i, k:k + S], conv[:, i, k:k + 1],
                                                            uc[:, i, :], ALU.mult, ALU.add)
                            if k == TAPS - 1:
                                last.then_inc(s_cv, 1)
            with dve.Fori(0, B) as b:
                dve.wait_ge(s_soft, b + 2)
                dve.wait_ge(s_dt, b + 1)
                dve.tensor_scalar(rest, soft_e, 1.0, -1.0, ALU.add, ALU.add)
                dve.drain()
                dve.tensor_tensor(rest, soft_e, rest, ALU.subtract)
                dve.drain()
                dve.tensor_tensor(rest, soft_l, rest, ALU.add)
                dve.drain()
                dve.tensor_tensor(dt[:, :, tok(b)], dt[:, :, tok(b)], rest, ALU.add).then_inc(s_dt, 1)
            dve.sem_inc(s_hc, 2 * G)
            dve.sem_inc(s_y, 3)
            dve.drain()
            dve.memset(view(decay[:, 0], [[S, 2 * M]]), 0.0)

            def spread(b):
                dve.wait_ge(s_dterm, b + 1)
                dve.tensor_tensor(u2[:, :, tok(b)], u2[:, :, tok(b)], dt[:, :, tok(b)], ALU.mult).then_inc(s_du, 1)

            def gate_y(b, turn):
                dve.wait_ge(s_y, (b + 1) * NS + 3)
                dve.tensor_tensor(sz[:, turn], ps[:, 4 * turn:4 * turn + 4, :], sz[:, turn], ALU.mult).then_inc(s_yz, 1)

            def residual(b, turn):
                dve.wait_ge(s_out_mm, b + 2)
                dve.tensor_tensor(xT[:, :, tok(b)], ps[:, 4 * turn:4 * turn + 2, :], xT[:, :, tok(b)],
                                  ALU.add).then_inc(s_x1, 1)

            def scans(b, turn, first, final):
                for n in range(NS):
                    g = n // G
                    flat = view(state[:, (n + turn) % 3], [[1, M * S]])
                    dve.wait_ge(s_decay, b * NS + n + 1)
                    dve.wait_ge(s_dbu, b * NS + n + 1)
                    dve.tensor_tensor_scan(flat, view(decay[:, n % 2], [[1, M * S]]), flat, 0.0,
                                           ALU.mult, ALU.add).then_inc(s_scan, 1)
                    dve.drain()
                    dve.wait_ge(s_bcl[g % 2], (b * (NS // G // 2) + g // 2 + 1) * 16)
                    dve.tensor_tensor(state[:, (n + turn) % 3], state[:, (n + turn) % 3],
                                      view(bc[:, g % 2, 1, n % G, :], [[0, M], [1, S]]),
                                      ALU.mult).then_inc(s_hc, 1)
                    if n == 0 and not first:
                        gate_y(b - 1, 1 - turn)
                    if n == 4 and not first:
                        residual(b - 1, 1 - turn)
                    if n == 12 and not final:
                        spread(b + 1)

            spread(0)
            scans(0, 0, True, False)
            with dve.Fori(0, B // 2 - 1) as i:
                scans(2 * i + 1, 1, False, False)
                scans(2 * i + 2, 0, False, False)
            scans(B - 1, 1, False, True)
            gate_y(B - 1, 1)
            dve.wait_ge(s_out_mm, B + 1)
            dve.tensor_tensor(xT[:, :, tok(B - 1)], ps[:, 4:6, :], xT[:, :, tok(B - 1)], ALU.add).then_inc(s_x1, 1)

            dve.wait_ge(s_cond, 16)
            dve.tensor_tensor(w2c, c2_w, c2_w, ALU.mult)
            dve.tensor_tensor(sqk[:, :], wc["s_q"], wc["s_k"], ALU.mult)
            dve.tensor_reduce(awn[:, 6:7], wc["aw"], AX, ALU.max)
            wbig, wsml = xm[:, :, 0:D], xh[:, :, 0:D]
            dve.tensor_scalar(wbig, ffn_w, 448.0, -448.0, ALU.min, ALU.max)
            dve.tensor_scalar(wsml, ffn_w, 1.0, -1.0, ALU.min, ALU.max)
            dve.drain()
            dve.tensor_scalar(q8[:, :, 0:D], wbig, 0.5, None, ALU.mult, saturate=False)
            dve.tensor_scalar(q8b, wsml, 1.0, None, ALU.mult, saturate=False)
            dve.tensor_scalar(q8c, wsml, 0.5, None, ALU.mult, saturate=False)
            dve.drain()
            dve.scalar_tensor_tensor(wbig, q8[:, :, 0:D], 2.0, q8b, ALU.mult, ALU.add)
            dve.drain()
            dve.scalar_tensor_tensor(wq8, q8c, -2.0, wbig, ALU.mult, ALU.add)
            dve.tensor_scalar(awn[:, 0:6], wc["aw"], awn[:, 6:7], None, ALU.subtract)
            dve.drain()
            dve.engine_nop().then_inc(s_prep, 1)
            dve.wait_ge(s_prep_act, 3)
            dve.tensor_reduce(awn[:, 6:7], awn[:, 0:6], AX, ALU.add)
            dve.drain()
            dve.reciprocal(awn[:, 7:8], awn[:, 6:7])
            dve.drain()
            dve.tensor_scalar(awn[:, 0:6], awn[:, 0:6], awn[:, 7:8], None, ALU.mult)
            dve.drain()
            for j in range(6):
                dve.tensor_scalar(i_w1[:, j], i_w1[:, j], awn[:, j:j + 1], None, ALU.mult)
            dve.drain()
            dve.tensor_tensor(wx, i_w1[:, 2], i_w1[:, 3], ALU.add)
            dve.drain()
            dve.tensor_tensor(wx, wx, i_w1[:, 4], ALU.add)
            dve.wait_ge(s_prep_mm, 2)
            dve.tensor_tensor(view(vz[:, 0, 0, :], [[B, 3 * C], [1, B]]), view(ps[:, 5, :], [[B, 3 * C], [1, B]]),
                              view(wc["v_b2"], [[1, 3 * C], [0, B]]), ALU.add).then_inc(s_prep, 1)
            dve.wait_ge(s_prep_mm, 3)
            dve.drain()
            dve.tensor_tensor(vz[:, :, :, :], vz[:, :, :, :], view(ps[:, 6, :], [[B, 3], [0, C], [1, B]]), ALU.subtract)
            dve.drain()
            dve.tensor_tensor(vsq[:, :, :, :], vz[:, :, :, :], vz[:, :, :, :], ALU.mult).then_inc(s_prep, 1)
            dve.wait_ge(s_prep_act, 4)
            dve.tensor_tensor(vz[:, :, :, :], vz[:, :, :, :], view(vr[:, 0, :], [[B, 3], [0, C], [1, B]]), ALU.mult)
            dve.drain()
            dve.tensor_tensor(view(vz[:, 0, 0, :], [[B, 3 * C], [1, B]]), view(vz[:, 0, 0, :], [[B, 3 * C], [1, B]]),
                              view(wc["v_g"], [[1, 3 * C], [0, B]]), ALU.mult)
            dve.drain()
            dve.tensor_tensor(view(vz[:, 0, 0, :], [[B, 3 * C], [1, B]]), view(vz[:, 0, 0, :], [[B, 3 * C], [1, B]]),
                              view(wc["v_be"], [[1, 3 * C], [0, B]]), ALU.add).then_inc(s_prep, 1)
            dve.wait_ge(s_prep_mm, 5)
            dve.tensor_tensor(cvec[:, :, :], view(ps[:, 5, :], [[B, C], [1, B]]),
                              view(wc["i_b1"], [[1, C], [0, B]]), ALU.add).then_inc(s_prep, 1)
            dve.wait_ge(s_prep_act, 4)
            with dve.Fori(0, B) as b:
                dve.wait_ge(s_c2_mm, b + 2)
                dve.wait_ge(s_x2, b + 1)
                y2 = tt
                for o in range(C):
                    dve.tensor_scalar(y2[:, o, :], ps[:, o, :], dem[:, 1, o, bass.ds(b, 1)], wc["c2_b"][:, o:o + 1],
                                      ALU.mult, ALU.add)
                dve.drain()
                dve.tensor_scalar(y2, y2, 256.0, -256.0, ALU.min, ALU.max)
                dve.drain()
                dve.tensor_scalar(q8, y2, 240.0, -240.0, ALU.min, ALU.max, saturate=False)
                dve.tensor_scalar(low, y2, -248.0, None, ALU.is_le)
                dve.drain()
                dve.scalar_tensor_tensor(low, y2, 248.0, low, ALU.is_ge, ALU.subtract)
                dve.drain()
                dve.scalar_tensor_tensor(yq, low, 16.0, q8, ALU.mult, ALU.add).then_inc(s_yq, 1)
                dve.wait_ge(s_f16, b + 2)
                for o in range(C):
                    last = dve.scalar_tensor_tensor(xT[:, o, tok(b)], f16[:, o, :], wc["ffn_b"][:, o:o + 1],
                                                    xT[:, o, tok(b)], ALU.add, ALU.add)
                last.then_inc(s_x2, 1)

            def embed(b, i, out, x):
                dve.wait_ge(s_g_mm, b * 4 + i + 1)
                dve.tensor_tensor(out, x, ps[:, 0:2, :], ALU.mult)
                dve.drain()
                last = dve.tensor_tensor(out, out, ps[:, 2:4, :], ALU.add)
                last.then_inc(s_g_used, 1)

            with dve.Fori(0, B) as b:
                dve.wait_ge(s_ids, 16 * (b + 1))
                dve.wait_ge(s_i1_mm, b + 1)
                for k in range(2):
                    dve.tensor_scalar(oh_pw[:, k, :], ids[:, 0, :], wc["rows"][:, k:k + 1], None, ALU.is_equal)
                dve.tensor_scalar(oh_cp, ids[:, 1, :], wc["rows"][:, 0:1], None, ALU.is_equal)
                dve.tensor_scalar(oh_ms, ids[:, 2, :], wc["rows"][:, 0:1], None,
                                  ALU.is_equal).then_inc(s_oh, 1)
                ln_vector(dve, xT[:, :, tok(b)], B + 3 * b)
                rstd2 = view(ln_rstd, [[0, C], [1, S]])
                dve.tensor_tensor(xh, ln_xc, rstd2, ALU.mult).then_inc(s_ln_out, 1)
                dve.drain()
                embed(b, 0, hh, xh)
                dve.drain()
                dve.engine_nop().then_inc(s_h1, 1)
                ln_vector(dve, hh, B + 3 * b + 1)
                dve.tensor_tensor(hh, ln_xc, rstd2, ALU.mult).then_inc(s_ln_out, 1)
                dve.drain()
                embed(b, 1, hh, hh)
                embed(b, 2, tt, xh)
                embed(b, 3, ss, xh)
                dve.wait_ge(s_i2_mm, b + 2)
                for o in range(C):
                    last = dve.tensor_scalar(y3[:, o, :], ps[:, o, :], wc["i_b2"][:, o:o + 1], None, ALU.add)
                last.then_inc(s_i2, 1)
                dve.engine_nop().then_inc(s_g_used, 1)
                dve.drain()
                ln_vector(dve, y3, B + 3 * b + 2)
                for c in range(C):
                    dve.scalar_tensor_tensor(y3[:, c, :], ln_xc[:, c, :], wc["i_g"][:, c:c + 1], ln_rstd,
                                             ALU.mult, ALU.mult)
                dve.drain()
                for c in range(C):
                    last = dve.tensor_scalar(y3[:, c, :], y3[:, c, :], wc["i_be"][:, c:c + 1], None, ALU.add)
                last.then_inc(s_ln_out, 1)
                dve.drain()
                dve.engine_nop().then_inc(s_y3, 1)
            dve.wait_ge(s_rho_mm, 1)
            dve.tensor_reduce(ssq[:, :], view(ps[:, 5, :], [[B, 2], [1, B]]), AX, ALU.add).then_inc(s_rho_sum, 1)
            dve.wait_ge(s_rho_root, 1)
            dve.tensor_scalar(rho[:, :], rho[:, :], 1e-6, None, ALU.add)
            dve.drain()
            dve.tensor_tensor(rho[:, 0:1], rho[:, 0:1], rho[:, 1:2], ALU.mult)
            dve.drain()
            dve.reciprocal(rho[:, 0:1], rho[:, 0:1]).then_inc(s_rho, 1)
            dve.sem_inc(s_max, 2)
            dve.wait_ge(s_k_out, 16 * B + 1)
            dve.wait_ge(s_vs, B + 1)
            dve.memset(kstack[STACK:P], 0.0)
            dve.memset(qstack[STACK:P], 0.0)
            dve.drain()
            dve.memset(kstack[STACK:STACK + 1], -1.0).then_inc(s_ones, 1)

            def maximum(hg, n, s):
                i, qc = s % HG, s // HG
                dve.wait_ge(s_s_mm, n + s + 1)
                dve.tensor_reduce(mxs[:, hg % 2, qc, i:i + 1], ps[:, s % 2, :], AX, ALU.max).then_inc(s_max, 1)

            def normalise(g, hg):
                dve.wait_ge(s_z_tr, g + 2)
                dve.reciprocal(zrec[:, :, :], view(ps[:, 7, DH:], [[P, TILES], [SLOT, HG]]))
                dve.drain()
                dve.tensor_tensor(view(zn, [[D, TILES], [DH, HG], [1, DH]], hg * HG * DH),
                                  view(ps[:, 7, :], [[P, TILES], [SLOT, HG], [1, DH]]),
                                  view(zrec[:, :, :], [[HG, TILES], [1, HG], [0, DH]]), ALU.mult).then_inc(s_zn, 1)

            def attention_add(b, o):
                dve.wait_ge(s_wo_mm, b * C + o + 2)
                dve.tensor_tensor(xT[:, o, tok(b)], ps[:, 7, :], xT[:, o, tok(b)], ALU.add).then_inc(s_x3, 1)

            def follow(b, first, final):
                for hg in range(HG):
                    g = b * HG + hg
                    for s in range(16):
                        if s == 0:
                            dve.wait_ge(s_m_tr, g + 1)
                        if not (final and hg >= 2):
                            maximum(hg, (g + 2) * 16, s)
                        if s in (7, 9) and hg == 1 and not first:
                            attention_add(b - 1, (s - 7) // 2)
                        if s == 11 and not (first and hg == 0):
                            normalise(g - 1, (hg - 1) % HG)

            for hg in range(2):
                for s in range(16):
                    maximum(hg, hg * 16, s)
            follow(0, True, False)
            with dve.Fori(1, B - 1) as b:
                follow(b, False, False)
            follow(B - 1, False, True)
            normalise(B * HG - 1, HG - 1)
            for o in range(C):
                attention_add(B - 1, o)

            dve.memset(eps32[:, :], float(np.finfo(np.float32).eps))
            dve.sem_inc(s_e_mm, 4)
            dve.wait_ge(s_ew, 16)
            if "x3" in dbg:
                dve.wait_ge(s_dbg, 16 * len(dbg))
            dve.tensor_reduce(b2s[:, :], fcut("b2", C, E), AX, ALU.add)
            dve.wait_ge(s_wgt_mm, 1)
            dve.tensor_copy(view(wgt_all, [[C * D, B], [1, C * D]]), ps[:, 0:B, :])
            dve.tensor_copy(dbias[:, :, :], ps[:, 4, 0:C * B]).then_inc(s_wgt_all, 1)
            with dve.Fori(0, B) as b:
                dve.wait_ge(s_gate_mm, b + 1)
                dve.tensor_tensor(lg[:, :, :], view(ps[:, 6, :], [[E, TILES], [1, E]]),
                                  view(wf["gate_b"], [[0, TILES], [1, E]]), ALU.add)
                dve.drain()
                dve.tensor_tensor(lg2[:, :, :], lg[:, :, :], lg[:, :, :], ALU.mult)
                dve.drain()
                dve.tensor_reduce(gs[:, 0, :], lg2[:, :, :], AX, ALU.add).then_inc(s_gate_sq, 1)
                dve.drain()
                dve.tensor_tensor(lg2[:, :, :], lg[:, :, :], view(wf["rms_w"], [[0, TILES], [1, E]]), ALU.mult)
                dve.drain()
                dve.wait_ge(s_gate_r, b + 1)
                dve.tensor_tensor(lg2[:, :, :], lg2[:, :, :], view(gs[:, 1, :], [[1, TILES], [0, E]]), ALU.mult)
                dve.drain()
                dve.tensor_reduce(gs[:, 2, :], lg2[:, :, :], AX, ALU.max)
                dve.drain()
                dve.tensor_tensor(lg[:, :, :], lg2[:, :, :], view(gs[:, 2, :], [[1, TILES], [0, E]]),
                                  ALU.subtract).then_inc(s_gate_d, 1)
                dve.wait_ge(s_gate_e, b + 1)
                dve.tensor_reduce(gs[:, 0, :], lg[:, :, :], AX, ALU.add)
                dve.drain()
                dve.reciprocal(gs[:, 2, :], gs[:, 0, :])
                dve.drain()
                dve.tensor_scalar(gs[:, 1, :], gs[:, 2, :], 1e-6, None, ALU.add)
                dve.drain()
                dve.reciprocal(gs[:, 0, :], gs[:, 1, :])
                dve.drain()
                dve.wait_ge(s_ngb_mm, b + 1)
                dve.tensor_tensor(gs[:, 3, :], gs[:, 2, :], gs[:, 0, :], ALU.mult).then_inc(s_ng, 1)
                dve.wait_ge(s_ngb, b + 1)
                dve.wait_ge(s_e_mm, (b + 1) * FM + 4)
                for o in range(C):
                    dve.scalar_tensor_tensor(moe[:, o, :], ps[:, o, :], b2s[:, o:o + 1], ngb, ALU.add, ALU.mult)
                dve.drain()
                dve.tensor_tensor(xT[:, :, tok(b)], xT[:, :, tok(b)], moe, ALU.add).then_inc(s_x4, 1)


        @block.gpsimd
        def _(pool):
            for started in (s_mixp, s_qp, s_kp):
                pool.sem_inc(started, 1)
            with pool.Fori(0, B) as b:
                for t in range(TILES):
                    n = b * TILES + t
                    u = t % 2
                    pool.wait_ge(s_att, n + 1)
                    pool.tensor_tensor(view(mix[:, u], [[D, POOL_SH], [DH, H], [1, DH]]),
                                       view(att_p[:, u], [[H, POOL_SH], [1, H], [0, DH]]),
                                       view(kx[:, t, :], [[DH, POOL_SH], [DH, H], [1, DH]]),
                                       ALU.mult).then_inc(s_mixp, 1)

            pool.wait_ge(s_h0, B + 1)
            pool.wait_ge(s_x, 32 if "h0" in dbg else 16)
            pool.wait_ge(s_ln_xc, B + 1)
            pool.tensor_tensor(xT[:, :, :], xT[:, :, :], hT[:, :, :], ALU.add).then_inc(s_xh0, 1)

            def inputs(b, turn):
                pool.wait_ge(s_du, b + 1)
                for n in range(NS):
                    g = n // G
                    pool.wait_ge(s_bcl[g % 2], (b * (NS // G // 2) + g // 2 + 1) * 16)
                    pool.wait_ge(s_y, b * NS + (min(n + 2, 3) if turn == 0 and n < 2 else n + 1))
                    apart(pool)
                    pool.tensor_tensor(state[:, (n + turn) % 3], u2[:, :, tok(b)],
                                       view(bc[:, g % 2, 0, n % G, :], [[0, M], [1, S]]),
                                       ALU.mult).then_inc(s_dbu, 1)

            with pool.Fori(0, B // 2) as i:
                inputs(2 * i, 0)
                inputs(2 * i + 1, 1)
            with pool.Fori(0, B) as b:
                for full, parts, ready, written, split in ((qf, qp, s_qf, s_q_out, s_qp), (kf, kp, s_kf, s_k_out, s_kp)):
                    pool.wait_ge(ready, b + 2)
                    pool.wait_ge(written, 16 * b + 1)
                    apart(pool)
                    pool.tensor_copy(parts[:, 0], full)
                    pool.drain()
                    pool.tensor_tensor(rest_q, full, parts[:, 0], ALU.subtract)
                    pool.drain()
                    pool.tensor_copy(parts[:, 1], rest_q)
                    pool.drain()
                    pool.tensor_tensor(parts[:, 2], rest_q, parts[:, 1], ALU.subtract).then_inc(split, 1)
                    pool.drain()
            pool.wait_ge(s_k_out, 16 * B + 1)
            pool.wait_ge(s_vs, B + 1)
            pool.memset(va, 0.0)
            pool.drain()
            pool.memset(view(va, [[SLOT, TILES * H]], DH), 1.0)

            def fill_slots(src, hg):
                pool.tensor_copy(view(va, [[H * SLOT, TILES], [SLOT, HG], [1, DH]], hg * HG * SLOT),
                                 view(src, [[D, TILES], [DH, HG], [1, DH]], hg * HG * DH)).then_inc(s_va, 1)

            for hg in range(HG):
                fill_slots(v_all[:, 0], hg)
            with pool.Fori(1, B) as b:
                for hg in range(HG):
                    pool.wait_ge(s_pv, (b * HG + hg) * TILES + 1 - (HG - 1) * TILES)
                    apart(pool)
                    fill_slots(v_all[:, bass.ds(b, 1)], hg)
            pool.wait_ge(s_wgt_all, 1)
            with pool.Fori(0, B) as b:
                pool.wait_ge(s_y4, b + 1)
                apart(pool)
                pool.tensor_copy(wgt, wgt_all[:, bass.ds(b, 1)]).then_inc(s_wgt, 1)


ARENA = 36000


def chunked(a):
    a = np.asarray(a)
    k = a.shape[0] // P
    return a.reshape(k, P, -1).transpose(1, 0, 2).reshape(P, -1)


def rows(a):
    a = np.asarray(a, np.float32)
    out = np.zeros((P, a.shape[1]), np.float32)
    out[:a.shape[0]] = a
    return out


def pack(spec, width, parts):
    out = np.zeros((P, width), np.float32)
    for name, (at, n) in spec.items():
        a = parts[name]
        assert a.shape == (P, n), (name, a.shape, n)
        out[:, at:at + n] = a
    return out


def host_arrays(i):
    col = lambda v: chunked(np.asarray(v).reshape(-1, 1))
    wide = lambda v: np.broadcast_to(np.asarray(v).reshape(1, -1), (P, np.asarray(v).size))
    x = np.asarray(i["x"]).reshape(N, D).T
    early = pack(EARLY, EARLY_W, dict(
        condT=np.asarray(i["cond_512"]).T, k_aff=np.asarray(i["L0_cond_k_aff_w"]).T,
        o_aff=np.asarray(i["L0_cond_o_aff_w"]).T, c2_aff=np.asarray(i["L0_cond2_affine_w"]).T,
        k_affb=col(i["L0_cond_k_aff_b"]), o_affb=col(i["L0_cond_o_aff_b"]), c2_affb=col(i["L0_cond2_affine_b"]),
        k_w=chunked(np.asarray(i["L0_cond_k_w"]).T), o_w=chunked(np.asarray(i["L0_cond_o_w"]).T),
        ident=np.eye(P, dtype=np.float32), mean=np.full((P, P), 1.0 / D, np.float32),
        ones=np.ones((P, P), np.float32), k_b=wide(i["L0_cond_k_b"]), o_b=col(i["L0_cond_o_b"])))
    w_in = np.asarray(i["L0_attn_W_in"])
    mamba = pack(MAMBA, MAMBA_W, dict(
        gamma=col(i["L0_attn_gamma"]), beta=col(i["L0_attn_beta"]), w_u=chunked(w_in[:, :DI]),
        conv=chunked(i["L0_attn_conv_w"]), w_z=chunked(w_in[:, DI:]), conv_b=col(i["L0_attn_conv_b"]),
        w_x=chunked(i["L0_attn_W_x"]), w_dt=rows(i["L0_attn_W_dt"]), b_dt=col(i["L0_attn_b_dt"]),
        a_log=chunked(i["L0_attn_A_log"]), d=col(i["L0_attn_D"]), w_out=chunked(i["L0_attn_W_out"])))
    table = lambda g, b: np.concatenate([np.asarray(i[g]), np.asarray(i[b])], axis=1)
    pw = table("L1_cond_pw_g", "L1_cond_pw_b")
    three = lambda f: np.concatenate([f(x) for x in ("mem", "noi", "res")], axis=1)
    wqkv = np.asarray(i["L1_attn_Wqkv"])
    cond = pack(COND, COND_W, dict(
        c2_w=chunked(np.asarray(i["L0_cond2_weight"]).T), c2_b=col(i["L0_cond2_bias"]),
        ffn_w=chunked(np.asarray(i["L0_ffn_weight"]).T), ffn_b=col(i["L0_ffn_bias"]),
        pw=np.concatenate([rows(pw[:PWK]), rows(pw[PWK:])], axis=1),
        cp=rows(np.concatenate([table("L1_cond_cp_g", "L1_cond_cp_b"), table("L1_cond_tm_g", "L1_cond_tm_b")], axis=1)),
        ms=rows(table("L1_cond_ms_g", "L1_cond_ms_b")),
        rows=np.stack([np.arange(P), np.arange(P) + PWK], axis=1).astype(np.float32), aw=wide(i["L1_cond_aw"]),
        v_in=np.concatenate([rows(np.asarray(i[x]).T) for x in ("cond_512", "cond_64", "fside_Bx32_0")], axis=1),
        v_w1=three(lambda x: rows(i[f"L1_cond_{x}_W1"])), v_w2=three(lambda x: chunked(i[f"L1_cond_{x}_W2"])),
        v_b1=three(lambda x: col(i[f"L1_cond_{x}_b1"])), v_b2=three(lambda x: col(i[f"L1_cond_{x}_b2"])),
        v_g=three(lambda x: col(i[f"L1_cond_{x}_g"])), v_be=three(lambda x: col(i[f"L1_cond_{x}_be"])),
        i_w1=chunked(i["L1_cond_int_W1"]), i_w2=chunked(i["L1_cond_int_W2"]), i_b1=col(i["L1_cond_int_b1"]),
        i_b2=col(i["L1_cond_int_b2"]), i_g=col(i["L1_cond_int_g"]), i_be=col(i["L1_cond_int_be"]),
        w_q=chunked(wqkv[:, :D]), w_k=chunked(wqkv[:, D:2 * D]), w_v=chunked(wqkv[:, 2 * D:]),
        s_q=np.tile(np.asarray(i["L1_attn_scale_q"]), P // DH).reshape(P, 1),
        s_k=np.tile(np.asarray(i["L1_attn_scale_k"]), P // DH).reshape(P, 1)))
    ids = np.stack([np.asarray(i[k]).reshape(-1) for k in ("itok_BxS_0_999", "itok_BxS_0_4", "mask_BxS_ik0")])
    per = lambda a: np.asarray(a).transpose(1, 0, 2).reshape(np.asarray(a).shape[1], -1)
    ffn = pack(FFN, FFN_W, dict(
        w_o=chunked(i["L1_attn_Wo"]), v_dec=rows(i["L1_cond2_V"]), gate_w=chunked(np.asarray(i["L1_ffn_gate_w"]).T),
        gate_b=wide(i["L1_ffn_gate_b"]), rms_w=wide(i["L1_ffn_rms_w"]),
        b1=np.asarray(i["L1_ffn_b1"]).reshape(FM, P).T, b2=chunked(np.asarray(i["L1_ffn_b2"]).T),
        w1=chunked(per(i["L1_ffn_w1"])), w2=chunked(np.asarray(i["L1_ffn_w2"]).reshape(E * FH, D))))
    return {
        "cond": cond, "ffn": ffn, "ids": ids.astype(np.int32), "dec_w": np.asarray(i["L1_cond2_W_dec"]),
        "dec_b": np.ascontiguousarray(np.asarray(i["L1_cond2_b_dec"]).reshape(D + 1, KU).T),
        "mamba": mamba,
        "xT": np.ascontiguousarray(x.reshape(C, P, N).transpose(1, 0, 2)),
        "early": early,
    }


def kernel(**inputs):
    import concourse.bacc as bacc
    from concourse.bass_utils import run_bass_kernel_spmd
    arrays = host_arrays(inputs)
    nc = bacc.Bacc("TRN2", target_bir_lowering=False, num_devices=1)
    t_in = {k: nc.dram_tensor(f"in_{k}", a.shape, mybir.dt.from_np(a.dtype), kind="ExternalInput").ap()
            for k, a in arrays.items()}
    out = nc.dram_tensor("out", (P, C, N), F32, kind="ExternalOutput").ap()
    program(nc, t_in, out)
    r = run_bass_kernel_spmd(nc, [{f"in_{k}": a for k, a in arrays.items()}], core_ids=[0])
    got = r.results[0]["out"]
    return np.ascontiguousarray(got.transpose(1, 0, 2).reshape(D, N).T).reshape(B, S, D)
```

```python
from contextlib import ExitStack

import numpy as np

import concourse.bass as bass
from concourse import mybir

F32 = mybir.dt.float32
BF16 = mybir.dt.bfloat16
F16 = mybir.dt.float16
FP8 = mybir.dt.float8e4
I32 = mybir.dt.int32
ALU = mybir.AluOpType
ACT = mybir.ActivationFunctionType
AX = mybir.AxisListType.X

P = 128
B, S, D = 4, 512, 256
N = B * S
C = D // P
H, DH = 16, 16
TILES = S // P
DI, NS, RANK, TAPS = 512, 16, 16, 4
M = DI // P
G = 2
PW, CP, MS = 250, 5, 3
PWK = PW // 2
KU = 30
E, FH = 8, 512
FM = E * FH // P
SLOT = 32
Q_PARTS = (0, 0, 1, 0, 2, 1)
K_PARTS = (0, 1, 0, 2, 0, 1)
STATS, LAYER = 32, 64
PARTS = 3
GAP = 32
STACK = len(Q_PARTS) * DH
HG = P // SLOT
HALF = H // 2 + 1


def layout(fields):
    at, out = 0, {}
    for name, width in fields:
        out[name] = (at, width)
        at += width
    return out, at


EARLY, EARLY_W = layout([
    ("condT", B), ("k_aff", D), ("o_aff", D), ("c2_aff", D), ("k_affb", C), ("o_affb", C), ("c2_affb", C),
    ("k_w", C * D), ("ident", P), ("mean", P), ("k_b", D), ("ones", P), ("o_w", C * D), ("o_b", C)])
MAMBA, MAMBA_W = layout([
    ("gamma", C), ("beta", C), ("w_u", C * DI), ("spare", 2 * C), ("conv", M * TAPS), ("w_z", C * DI), ("conv_b", M),
    ("w_x", M * 48), ("w_dt", DI), ("b_dt", M), ("a_log", M * NS), ("d", M), ("w_out", M * D)])
LINEAR, LINEAR_W = layout([("c2_w", C * D), ("c2_b", C), ("ffn_w", C * D), ("ffn_b", C)])
COND, COND_W = layout([
    ("pw", 2 * 2 * D), ("cp", 4 * D), ("ms", 2 * D), ("rows", 3), ("aw", 6),
    ("v_in", 3 * B), ("v_w1", 3 * D), ("v_w2", 3 * C * D), ("v_b1", 3 * C), ("v_b2", 3 * C),
    ("v_g", 3 * C), ("v_be", 3 * C),
    ("i_w1", 6 * C * D), ("i_w2", C * D), ("i_b1", C), ("i_b2", C), ("i_g", C), ("i_be", C),
    ("w_q", C * D), ("w_k", C * D), ("w_v", C * D), ("s_q", 1), ("s_k", 1)])
FFN, FFN_W = layout([
    ("w_o", C * D), ("v_dec", D), ("gate_w", C * E), ("gate_b", E), ("rms_w", E), ("b1", FM), ("b2", C * E),
    ("w1", C * E * FH), ("w2", FM * D)])
UD = (D + 1) * KU


class Norm:
    def __init__(self, mean, var, buffers, sems):
        self.mean, self.var = mean, var
        self.xc, self.sq, self.rstd = buffers
        self.s_mu, self.s_xc, self.s_sq, self.s_var, self.s_rstd, self.s_out = sems


def view(ap, dims, off=0):
    return bass.AP(ap.tensor, ap.offset + off, [list(ap.ap[0])] + [list(d) for d in dims])


def tok(b, n=S):
    return bass.ds(b * n, n)


def program(nc, t_in, out, dbg=()):
    ctx = ExitStack()
    with ctx:
        def sb(name, shape, dt=F32):
            return ctx.enter_context(nc.sbuf_tensor(name, shape, dt))

        def sem(name):
            return ctx.enter_context(nc.semaphore(name))

        ps = ctx.enter_context(nc.psum_tensor("ps", [P, 8, 512], F32))

        early = sb("early", [P, EARLY_W])
        xT = sb("xT", [P, C, N])
        hT = sb("hT", [P, C, N])
        arena = sb("arena", [P, ARENA])

        def fields(tensor, spec, base=0):
            return {k: tensor[:, base + a:base + a + w] for k, (a, w) in spec.items()}

        w = fields(early, EARLY)
        k_w = w["k_w"].rearrange("p (c o) -> p c o", c=C)
        o_w = w["o_w"].rearrange("p (c o) -> p c o", c=C)
        ident, ones, mean = w["ident"], w["ones"], w["mean"]

        def carve(at, *shape):
            n = int(np.prod(shape))
            assert at + n <= ARENA, (at + n, ARENA)
            flat = arena[:, at:at + n]
            dims, st = [], n
            for s in shape:
                st //= s
                dims.append([st, s])
            return view(flat, dims), at + n

        style = sb("style", [P, 3, C, B])
        style2 = sb("style2", [P, 3, C, B])
        dem = sb("dem", [P, 2, C, B])
        eps = sb("eps", [P, 3])
        at = 0
        w2k, at = carve(at, C, D)
        w2o, at = carve(at, C, D)
        demk, at = carve(at, B, D)
        kw_mod, at = carve(at, B, C, D)
        xb, at = carve(at, TILES, C, P)
        kx, at = carve(at, TILES, 2 * D)
        prod, at = carve(at, HALF, H, DH)
        full, at = carve(at, 2, H, 2 * H)
        diff, at = carve(at, 2, D)
        att, at = carve(at, 2, D)
        att_p, at = carve(at, 2, D)
        mx, at = carve(at, 2, H)
        ssum, at = carve(at, 2, H)
        mix, at = carve(at, 2, H, D)
        aoT, at = carve(at, C, N)
        stage1_end = at

        s_early = sem("early_loaded")
        s_x = sem("x_loaded")
        s_style_mm = sem("style_products")
        s_style = sem("style_ready")
        s_sq = sem("squares_ready")
        s_dem_mm = sem("demod_products")
        s_dem_ln = sem("demod_ready")
        s_kw = sem("kw_ready")
        s_xb = [sem(f"xb_loaded{i}") for i in range(TILES)]
        s_kx_mm = sem("kx_products")
        s_kx = sem("kx_ready")
        s_red = sem("half_scores_ready")
        s_full = sem("scores_ready")
        s_diff = sem("diff_ready")
        s_exp = sem("exp_ready")
        s_att = sem("att_ready")
        s_mixv = sem("mix_by_vector")
        s_mixp = sem("mix_by_pool")
        s_ao_mm = sem("ao_products")
        s_ao = sem("ao_ready")
        s_o_mm = sem("o_products")
        s_h0 = sem("h0_ready")
        s_dbg = sem("dbg_out")

        POOL_SH = 12

        s_apart = sem("kept_apart")

        def apart(eng):
            eng.sem_inc(s_apart, 1)


        mam = sb("mam", [P, MAMBA_W])
        wm = fields(mam, MAMBA)
        w_u = wm["w_u"].rearrange("p (c o) -> p c o", c=C)
        w_z = wm["w_z"].rearrange("p (c o) -> p c o", c=C)
        w_x = wm["w_x"].rearrange("p (m o) -> p m o", m=M)
        w_out = wm["w_out"].rearrange("p (m o) -> p m o", m=M)
        a_neg = wm["a_log"]
        conv = wm["conv"].rearrange("p (m k) -> p m k", m=M)
        hflat = hT[:, :, :].rearrange("p c n -> p (c n)")
        sz = view(hflat, [[M * S, 2], [S, M], [1, S]])
        diag = sb("diag", [P, M, P])
        one = sb("one", [P, 1])
        at = 0
        u2, at = carve(at, M, N)
        dt, at = carve(at, M, N)
        xn, at = carve(at, B, C, S)
        head_at = at
        dbl, _ = carve(at, N)
        up, conv_end = carve(head_at + N, M, S + TAPS - 1)
        uc, conv_end = carve(conv_end, M, S)
        soft_r, _ = carve(head_at + N, 2, 2, S)
        soft_e, soft_l = (view(hflat, [[2 * S, 2], [S, 2], [1, S]], j * 4 * S) for j in range(2))
        lo_xc, lo_end = carve(head_at, C, S)
        lo_sq, lo_end = carve(lo_end, C, S)
        lo_rstd, lo_end = carve(lo_end, S)
        ln_xc, at = carve(head_at + 2 * M * S, C, S)
        ln_sq, at = carve(at, C, S)
        ln_rstd, at = carve(at, S)
        ln_end = at
        assert conv_end <= ln_end and lo_end <= head_at + 2 * M * S
        dec_w, at = carve(ln_end, UD)
        dec_b, at = carve(at, D + 1)
        at = head_at
        decay, at = carve(at, 2, M, S)
        state, at = carve(at, 3, M, S)
        bc, at = carve(at, 2, 2, G, S)
        bc_dram = nc.dram_tensor("bc_scratch", (B, 2 * NS, S), F32, kind="Internal").ap()

        s_mam = sem("mamba_loaded")
        s_a = sem("a_exponent_ready")
        s_ln_mu = sem("ln_mean_product")
        s_ln_xc = sem("ln_centred")
        s_ln_sq = sem("ln_squared")
        s_ln_var = sem("ln_var_product")
        s_ln_rstd = sem("ln_rstd_ready")
        s_ln_out = sem("ln_scaled")
        s_lo_mu, s_lo_xc, s_lo_sq, s_lo_var, s_lo_rstd, s_lo_out = (sem(f"other_ln_{x}") for x in (
            "mean_product", "centred", "squared", "var_product", "rstd_ready", "scaled"))
        norm = Norm(6, 7, (ln_xc, ln_sq, ln_rstd), (s_ln_mu, s_ln_xc, s_ln_sq, s_ln_var, s_ln_rstd, s_ln_out))
        lo_sems = (s_lo_mu, s_lo_xc, s_lo_sq, s_lo_var, s_lo_rstd, s_lo_out)
        other = Norm(4, 5, (lo_xc, lo_sq, lo_rstd), lo_sems)
        s_up = sem("u_copied")
        s_cv = sem("convolved")
        s_pad = sem("pads_ready")
        s_xh0 = sem("residual_took_h0")
        s_u_mm = sem("u_products")
        s_u2 = sem("u2_ready")
        s_x_mm = sem("x_products")
        s_dbl = sem("dbl_ready")
        s_bc = sem("bc_written")
        s_dt_mm = sem("dt_products")
        s_soft = sem("softplus_parts")
        s_rest = sem("softplus_rest_ready")
        s_dt = sem("dt_ready")
        s_z_mm = sem("z_products")
        s_sz = sem("sz_ready")
        s_dterm = sem("d_term_product")
        s_du = sem("du_ready")
        s_bcl = [sem(f"bc_loaded{i}") for i in range(2)]
        s_decay = sem("decay_ready")
        s_dbu = sem("dbu_ready")
        s_scan = sem("scan_done")
        s_hc = sem("state_times_c")
        s_y = sem("y_accumulated")
        s_yz = sem("yz_ready")
        s_out_mm = sem("out_products")
        s_x1 = sem("x1_ready")


        u_t = sb("u_t", [KU, B, D + 1])
        s_dec = sem("decoder_loaded")
        s_dec_mm = sem("decoder_products")
        s_u_t = sem("u_t_ready")

        at = 0
        cw, at = carve(at, COND_W)
        wc = {k: view(cw, [[1, n]], a) for k, (a, n) in COND.items()}
        cut = lambda name, *dims: view(wc[name], [[int(np.prod(dims[j + 1:])), d] for j, d in enumerate(dims)])
        lw = mam[:, MAMBA["w_u"][0]:MAMBA["w_u"][0] + LINEAR_W]
        assert LINEAR_W == MAMBA["w_u"][1] + MAMBA["spare"][1]
        wl = {k: view(lw, [[1, n]], a) for k, (a, n) in LINEAR.items()}
        c2_w, ffn_w = (view(wl[x], [[D, C], [1, D]]) for x in ("c2_w", "ffn_w"))
        pw_p, at = carve(at, PARTS * 2 * D)
        pw_p = pw_p.bitcast(BF16)
        small_p, at = carve(at, PARTS * D)
        small_p = small_p.bitcast(BF16)
        pw_t = view(pw_p, [[4 * D, PARTS], [2 * D, 2], [D, 2], [P, C], [1, P]])
        cp_t = view(small_p, [[2 * D, 2], [D, 2], [P, C], [1, P]])
        ms_t = view(small_p, [[D, 2], [P, C], [1, P]], 4 * D)
        i_w1, i_w2 = cut("i_w1", 6, C, D), cut("i_w2", C, D)
        w_q, w_k, w_v = (cut(x, C, D) for x in ("w_q", "w_k", "w_v"))
        xm, at = carve(at, C, S)
        xh, at = carve(at, C, S)
        hh, at = carve(at, C, S)
        tt, at = carve(at, C, S)
        ss, at = carve(at, C, S)
        y3, at = carve(at, C, S)
        i1, at = carve(at, C, S)
        qf, at = carve(at, C, S)
        kf, at = carve(at, C, S)
        w2c, at = carve(at, C, D)
        rest_q, at = carve(at, C, S)
        oh_pw, oh_cp, oh_ms = (cw[:, COND["pw"][0] + a * S // 2:COND["pw"][0] + b * S // 2].bitcast(BF16)
                               for a, b in ((0, 2), (2, 3), (3, 4)))
        oh_pw = oh_pw.rearrange("p (k s) -> p k s", k=2)
        wx, at = carve(at, C, D)
        assert at <= head_at + 2 * M * S, at
        qp, kp = (arena[:, ln_end + j * 3 * C * S // 2:ln_end + (j + 1) * 3 * C * S // 2]
                  .bitcast(BF16).rearrange("p (k c s) -> p k c s", k=3, c=C) for j in range(2))
        v_all, _ = carve(ARENA - B * TILES * D, B, TILES * D)
        assert MAMBA["spare"][0] + 2 * C + 3 * S <= MAMBA_W
        ids = mam[:, MAMBA["spare"][0] + 2 * C:MAMBA["spare"][0] + 2 * C + 3 * S].bitcast(I32).rearrange("p (k s) -> p k s", k=3)

        def narrow(at, dtype, n):
            width = C * n * mybir.dt.size(dtype) // 4
            return arena[:, at:at + width].bitcast(dtype).rearrange("p (c s) -> p c s", c=C), at + width

        at3 = ln_end
        q8, at3 = narrow(at3, FP8, S)
        q8b, at3 = narrow(at3, FP8, D)
        q8c, at3 = narrow(at3, FP8, D)
        low, at3 = narrow(at3, BF16, S)
        yq, at3 = narrow(at3, BF16, S)
        wq8, at3 = narrow(at3, BF16, D)
        f16, at3 = narrow(at3, F16, S)
        lo_xc, lo_sq, lo_rstd = (view(hflat, dims, off) for dims, off in (
            ([[S, C], [1, S]], 0), ([[S, C], [1, S]], C * S), ([[1, S]], 2 * C * S)))
        final_norm = Norm(4, 5, (lo_xc, lo_sq, lo_rstd), lo_sems)
        awn = sb("awn", [P, 8])
        vh = sb("vh", [P, 3, C, B])
        vz = sb("vz", [P, 3, C, B])
        vsq = sb("vsq", [P, 3, C, B])
        vr = sb("vr", [P, 3, B])
        cvec = sb("cvec", [P, C, B])
        sums = sb("sums", [P, 2, B])
        sqk = sb("sqk", [P, 1])
        rho = sb("rho", [P, 2])
        q_dram = nc.dram_tensor("q_scratch", (B, P, 3 * C * S), BF16, kind="Internal").ap()
        k_dram = nc.dram_tensor("k_scratch", (B, P, 3 * C * S), BF16, kind="Internal").ap()

        s_cond = sem("linear_weights_loaded")
        s_cond2 = sem("embedding_weights_loaded")
        s_prep = sem("prep_by_vector")
        s_prep_mm = sem("prep_products")
        s_prep_act = sem("prep_by_scalar")
        s_xm = sem("xm_ready")
        s_c2_mm = sem("c2_products")
        s_y2 = sem("y2_read")
        s_yq = sem("yq_ready")
        s_ffn_mm = sem("ffn_products")
        s_f16 = sem("f16_ready")
        s_x2 = sem("x2_ready")
        s_ids = sem("ids_loaded")
        s_tables = sem("table_parts_ready")
        s_oh = sem("onehot_ready")
        s_xh = sem("xh_ready")
        s_g_mm = sem("gathered")
        s_g_used = sem("gathered_used")
        s_h1 = sem("h1_ready")
        s_i1_mm = sem("i1_products")
        s_i1 = sem("i1_ready")
        s_i2_mm = sem("i2_products")
        s_i2 = sem("i2_ready")
        s_q_mm = sem("q_products")
        s_k_mm = sem("k_products")
        s_v_mm = sem("v_products")
        s_qf = sem("q_ready")
        s_kf = sem("k_ready")
        s_qp = sem("q_parts_ready")
        s_kp = sem("k_parts_ready")
        s_vs = sem("v_ready")
        s_q_out = sem("q_written")
        s_k_out = sem("k_written")

        at = 0
        fw, at = carve(at, FFN_W)
        wf = {k: view(fw, [[1, n]], a) for k, (a, n) in FFN.items()}
        fcut = lambda name, *dims: view(wf[name], [[int(np.prod(dims[j + 1:])), d] for j, d in enumerate(dims)])
        w_o = fcut("w_o", C, D)
        stack_at = at
        qstack, kstack = (arena[:, stack_at + j * H * S // 2:stack_at + (j + 1) * H * S // 2].bitcast(BF16)
                   .rearrange("p (g i s) -> p g i s", g=HG, i=HG) for j in range(2))
        at += H * S
        va, at = carve(at, TILES, H * SLOT)
        pt, at = carve(at, 4, 2, S)
        zn, zn_t, zt = (view(hflat, dims, off) for dims, off in (
            ([[D, TILES], [1, D]], 0), ([[S, C], [1, S]], TILES * D), ([[1, S]], TILES * D + C * S)))
        assert at <= ARENA - B * TILES * D, at
        mxs = sb("mxs", [P, 2, TILES, HG])
        mrow = sb("mrow", [HG, 2, S], BF16)
        zrec = sb("zrec", [P, TILES, HG])
        ssq = sb("ssq", [P, 2])
        s_fw = sem("w_o_loaded")
        s_ew = sem("expert_weights_loaded")
        s_rho_mm = sem("rho_product")
        s_rho_sum = sem("rho_mean_ready")
        s_rho_root = sem("rho_root_ready")
        s_rho = sem("rho_ready")
        s_heads = [sem(f"qk_stack_loaded{i}") for i in range(HG)]
        s_ones = sem("constant_rows_ready")
        s_va = sem("v_slots_ready")
        s_mrow = sem("max_row_ready")
        s_mrow_in = sem("max_row_in_stack")
        s_s_mm = sem("score_products")
        s_max = sem("max_ready")
        s_m_tr = sem("max_transposed")
        s_t_mm = sem("scoreT_products")
        s_pt = sem("exp_scores_ready")
        s_pv = sem("value_products")
        s_zt = sem("z_copied")
        s_z_tr = sem("z_transposed")
        s_zn = sem("z_normalised")
        s_zn_tr = sem("zn_transposed")
        s_znt = sem("zn_copied")
        s_wo_mm = sem("attention_out_products")
        s_x3 = sem("x3_ready")

        at = FFN_W
        assert FFN_W + 11 * C * S <= ARENA
        gate_w, w1, w2 = fcut("gate_w", C, E), fcut("w1", C, E * FH), fcut("w2", FM, D)
        wgt_all, at = carve(at, B, C, D)
        y4, at = carve(at, B, C, S)
        hid, at = carve(at, 4, S)
        ngb, at = carve(at, N)
        moe, at = carve(at, C, S)
        dbias = sb("dbias", [P, C, B])
        b2s = sb("b2s", [P, C])
        lg = sb("lg", [P, B * TILES, E])
        lg2 = sb("lg2", [P, B * TILES, E])
        gs = sb("gs", [P, 4, B * TILES])
        eps32 = sb("eps32", [P, 1])
        s_wgt_mm = sem("decoded_products")
        s_wgt_all = sem("decoded_ready")
        s_y4_mm = sem("y4_products")
        s_y4 = sem("y4_ready")
        s_gate_mm = sem("gate_products")
        s_gate_sq = sem("gate_squares")
        s_gate_r = sem("gate_rstd")
        s_gate_d = sem("gate_less_max")
        s_gate_e = sem("gate_exp")
        s_ng = sem("gate_factor")
        s_ngb_mm = sem("gate_factor_product")
        s_ngb = sem("gate_factor_spread")
        s_h_mm = sem("hidden_products")
        s_hid = sem("hidden_ready")
        s_e_mm = sem("expert_products")
        s_x4 = sem("x4_ready")
        s_out = sem("out_written")

        def ln_mean(pe, L, x, k):
            pe.wait_ge(L.s_xc, k + 1)
            for c in range(C):
                done = pe.matmul(ps[:, L.mean, :], mean, x[:, c, :], start=(c == 0), stop=(c == C - 1))
            done.then_inc(L.s_mu, 1)

        def ln_var(pe, L, k):
            pe.wait_ge(L.s_sq, k + 1)
            pe.wait_ge(L.s_rstd, k + 1)
            for c in range(C):
                done = pe.matmul(ps[:, L.var, :], mean, L.sq[:, c, :], start=(c == 0), stop=(c == C - 1))
            done.then_inc(L.s_var, 1)

        def ln_square(act, L, k):
            act.wait_ge(L.s_xc, k + 2)
            act.wait_ge(L.s_var, k + 1)
            act.activation(L.sq, L.xc, ACT.Square).then_inc(L.s_sq, 1)

        def ln_root(act, L, k):
            act.wait_ge(L.s_var, k + 2)
            act.wait_ge(L.s_out, k + 1)
            act.activation(L.rstd, ps[:, L.var, :], ACT.Ln, bias=eps[:, 1:2])
            act.drain()
            act.activation(L.rstd, L.rstd, ACT.Exp, scale=-0.5).then_inc(L.s_rstd, 1)

        def ln_centre(dve, L, x, k):
            dve.wait_ge(L.s_mu, k + 1)
            dve.wait_ge(L.s_out, k + 1)
            mu = view(ps[:, L.mean, :], [[0, C], [1, S]])
            dve.tensor_tensor(L.xc, x, mu, ALU.subtract).then_inc(L.s_xc, 1)

        block = ctx.enter_context(nc.Block())

        def debug_out(sp, name, ap):
            if name in dbg:
                sp.dma_start(dbg[name], ap).then_inc(s_dbg, 16)

        def split_parts(engine, b, full, parts, rest, ready, written, split):
            engine.wait_ge(ready, b + 2)
            engine.wait_ge(written, 16 * b + 1)
            if engine is nc.gpsimd:
                apart(engine)
            engine.tensor_copy(parts[:, 0], full)
            engine.drain()
            engine.tensor_tensor(rest, full, parts[:, 0], ALU.subtract)
            engine.drain()
            engine.tensor_copy(parts[:, 1], rest)
            engine.drain()
            engine.tensor_tensor(parts[:, 2], rest, parts[:, 1], ALU.subtract).then_inc(split, 1)
            engine.drain()

        Q_STACK, K_STACK = (q_dram, qstack, Q_PARTS), (k_dram, kstack, K_PARTS)

        def load_heads(queue, b, hg, *stacks):
            for dram, stack, parts in stacks:
                for j, part in enumerate(parts):
                    src = dram[bass.ds(b, 1)] if not isinstance(b, int) else dram[b]
                    row = 3 * C * S
                    off = (hg % 2) * HG * DH * row + part * C * S + (hg // 2) * S
                    queue.dma_start(stack[j * DH:(j + 1) * DH, hg],
                                    bass.AP(src.tensor, src.offset + off, [[row, DH], [DH * row, HG], [1, S]])
                                    ).then_inc(s_heads[hg], 16)

        @block.sync
        def _(sp):
            for started in (s_q_out, s_k_out, s_mrow_in):
                sp.sem_inc(started, 1)
            sp.dma_start(early[:, :], t_in["early"]).then_inc(s_early, 16)
            x_dram = t_in["xT"]
            for t in range(TILES):
                sp.dma_start(xb[:, t], x_dram[:, :, t * P:(t + 1) * P]).then_inc(s_xb[t], 16)
            sp.dma_start(mam[:, :], t_in["mamba"]).then_inc(s_mam, 16)
            sp.dma_start(dec_w, t_in["dec_w"]).then_inc(s_dec, 16)
            sp.dma_start(dec_b[0:KU, :], t_in["dec_b"]).then_inc(s_dec, 16)
            sp.dma_start(xT[:, :, :], x_dram).then_inc(s_x, 16)
            with sp.Fori(1, B) as b:
                for t in range(TILES):
                    sp.wait_ge(s_kx_mm, b * TILES + t + 2 - TILES)
                    sp.dma_start(xb[:, t], x_dram[:, :, bass.ds(b * S + t * P, P)]).then_inc(s_xb[t], 16)
            sp.wait_ge(s_h0, B + 1)
            with sp.Fori(0, B) as b:
                sp.wait_ge(s_dbl, b + 2)
                sp.dma_start(bc_dram[bass.ds(b, 1)].rearrange("b r s -> r (b s)"),
                             dbl[RANK:RANK + 2 * NS, tok(b)]).then_inc(s_bc, 16)
            sp.wait_ge(s_bc, 16 * B)
            sp.dma_start(lw, t_in["linear"]).then_inc(s_cond, 16)
            with sp.Fori(0, B) as b:
                for g in range(NS // G):
                    sp.wait_ge(s_hc, b * NS + G * (g + 1))
                    if g == 0:
                        sp.wait_ge(s_dt, 2 * B + 2)
                    src = bc_dram[bass.ds(b, 1)]
                    src = bass.AP(src.tensor, src.offset + g * G * S, [[0, P], [NS * S, 2], [S, G], [1, S]])
                    sp.dma_start(bc[:, g % 2], src).then_inc(s_bcl[g % 2], 16)
            sp.wait_ge(s_x1, B + 1)
            debug_out(sp, "x1", xT[:, :, :])
            if "x1" in dbg:
                sp.wait_ge(s_dbg, 16)
            sp.dma_start(cw, t_in["cond"]).then_inc(s_cond2, 16)

            def load_ids(b):
                src = t_in["ids"][:, tok(b)]
                sp.dma_start(ids, bass.AP(src.tensor, src.offset, [[0, P], [N, 3], [1, S]])).then_inc(s_ids, 16)

            def store_parts(b):
                for stack, dram, ready, stored in ((qp, q_dram, s_qp, s_q_out), (kp, k_dram, s_kp, s_k_out)):
                    sp.wait_ge(ready, b + 2)
                    dst = dram[b] if isinstance(b, int) else dram[bass.ds(b, 1)].rearrange("b p n -> p (b n)")
                    sp.dma_start(dst, view(stack, [[1, 3 * C * S]])).then_inc(stored, 16)

            load_ids(0)
            sp.wait_ge(s_oh, 2)
            load_ids(1)
            with sp.Fori(0, B - 2) as b:
                sp.wait_ge(s_oh, b + 3)
                load_ids(b + 2)
                store_parts(b)
            for b in (B - 2, B - 1):
                store_parts(b)
            debug_out(sp, "x2", xT[:, :, :])
            sp.wait_ge(s_vs, B + 1)
            cut_at = FFN["w1"][0]
            sp.dma_start(fw[:, 0:cut_at], t_in["ffn"][:, 0:cut_at]).then_inc(s_fw, 16)

            for hg in range(HG):
                load_heads(sp, 0, hg, Q_STACK)
            sp.wait_ge(s_q_out, 16 * B + 1)
            sp.wait_ge(s_k_out, 16 * B + 1)
            sp.wait_ge(s_mrow, 2)
            sp.dma_start(qstack[STACK:STACK + 1, 0], mrow[0:HG, 0, :]).then_inc(s_mrow_in, 16)
            sp.dma_start(fw[:, cut_at:], t_in["ffn"][:, cut_at:]).then_inc(s_ew, 16)

            def feed(b, last):
                for hg in range(HG):
                    g = b * HG + hg
                    nxt = (hg + 1) % HG
                    if not (last and hg == HG - 1):
                        sp.wait_ge(s_mrow, g + 3)
                        sp.dma_start(qstack[STACK:STACK + 1, nxt], mrow[0:HG, nxt % 2, :]).then_inc(s_mrow_in, 16)
                    if not last:
                        sp.wait_ge(s_t_mm, g * 8 + 8)
                        load_heads(sp, b + 1, hg, Q_STACK, K_STACK)

            with sp.Fori(0, B - 1) as b:
                feed(b, False)
            feed(B - 1, True)
            if "x3" in dbg:
                sp.wait_ge(s_x3, B * C + 1)
                debug_out(sp, "x3", xT[:, :, :])
            with sp.Fori(0, B) as b:
                sp.wait_ge(s_x4, b + 3)
                sp.dma_start(out[:, :, tok(b)], xT[:, :, tok(b)]).then_inc(s_out, 16)
            sp.wait_ge(s_out, 16 * B)
            sp.wait_ge(s_dbg, 16 * len(dbg))

        @block.tensor
        def _(pe):
            for started in (s_kx_mm, s_ln_var, s_lo_var, s_ao_mm, s_out_mm, s_c2_mm, s_i2_mm, s_i1_mm, s_z_tr, s_wo_mm, s_h_mm, s_pv, s_v_mm):
                pe.sem_inc(started, 1)
            pe.wait_ge(s_early, 16)
            for j, name in enumerate(("k_aff", "o_aff", "c2_aff")):
                for c in range(C):
                    last = pe.matmul(ps[:, 0, (j * C + c) * B:(j * C + c + 1) * B],
                                     w[name][:, c * P:(c + 1) * P], w["condT"], start=True, stop=True)
            last.then_inc(s_style_mm, 1)
            pe.wait_ge(s_sq, 1)
            for b in range(B):
                for c in range(C):
                    pe.matmul(ps[:, 1 + b // 2, (b % 2) * D:(b % 2 + 1) * D],
                              style2[:, 0, c, b:b + 1].to_broadcast([P, P]), w2k[:, c, :],
                              start=(c == 0), stop=(c == C - 1))
            for o in range(C):
                for c in range(C):
                    last = pe.matmul(ps[:, 3, o * B:(o + 1) * B], w2o[:, c, o * P:(o + 1) * P],
                                     style2[:, 1, c, :], start=(c == 0), stop=(c == C - 1))
            last.then_inc(s_dem_mm, 1)
            pe.wait_ge(s_kw, 1)

            def kx_products(b, t):
                m = b * TILES + t
                pe.wait_ge(s_xb[t], b * 16 + 16)
                pe.wait_ge(s_kx, m + 1)
                for c in range(C):
                    pe.matmul(ps[:, t % 2, 0:D], xb[:, t, c, :],
                              kw_mod[:, bass.ds(b, 1), c, :], start=(c == 0), stop=False)
                pe.matmul(ps[:, t % 2, 0:D], ones[0:1, :], w["k_b"][0:1, :],
                          start=False, stop=True).then_inc(s_kx_mm, 1)

            def mix_products(b, t, first):
                n = b * TILES + t
                pe.wait_ge(s_mixv, n + 2)
                pe.wait_ge(s_mixp, n + 2)
                if not first or t >= 2:
                    pe.wait_ge(s_ao, n - 1)
                for c in range(C):
                    for s in range(H):
                        last = pe.matmul(ps[:, 4 + t % 2, c * P:(c + 1) * P],
                                         mix[:, t % 2, s, c * P:(c + 1) * P], ident,
                                         start=(s == 0), stop=(s == H - 1))
                last.then_inc(s_ao_mm, 1)

            def project(b):
                pe.wait_ge(s_ao, (b + 1) * TILES)
                pe.wait_ge(s_h0, b + 1)
                for o in range(C):
                    for c in range(C):
                        last = pe.matmul(ps[:, 6 + o, :], o_w[:, c, o * P:(o + 1) * P], aoT[:, c, tok(b)],
                                         start=(c == 0), stop=(c == C - 1))
                last.then_inc(s_o_mm, 1)

            def first_attention(b, first, final):
                for t in range(TILES):
                    if not (final and t >= 1):
                        kx_products(b + (t + 3) // TILES, (t + 3) % TILES)
                    mix_products(b, t, first)
                    if t == 2 and not first:
                        project(b - 1)

            kx_products(0, 0)
            kx_products(0, 1)
            kx_products(0, 2)
            first_attention(0, True, False)
            with pe.Fori(1, B - 1) as b:
                first_attention(b, False, False)
            first_attention(B - 1, False, True)
            project(B - 1)

            pe.wait_ge(s_h0, B + 1)
            norms = [(norm, b // 2) if b % 2 == 0 else (other, b // 2) for b in range(B)]
            for b in range(B + 2):
                if b >= 2:
                    ln_var(pe, *norms[b - 2])
                if b < B:
                    ln_mean(pe, norms[b][0], hT[:, :, tok(b)], norms[b][1])
            pe.wait_ge(s_ln_out, B // 2 + 1)
            pe.wait_ge(s_lo_out, B // 2 + 1)
            with pe.Fori(0, B) as b:
                for m in range(M):
                    pe.wait_ge(s_up, b * M + m + 1)
                    for c in range(C):
                        last = pe.matmul(ps[:, m, :], w_u[:, c, m * P:(m + 1) * P], xn[:, bass.ds(b, 1), c, :],
                                         start=(c == 0), stop=(c == C - 1))
                    last.then_inc(s_u_mm, 1)
            pe.wait_ge(s_pad, 1)
            pe.wait_ge(s_dec, 32)
            for b in range(B):
                pe.wait_ge(s_u2, (b + 2) * M)
                pe.wait_ge(s_dbl, b + 1)
                for m in range(M):
                    last = pe.matmul(ps[0:48, 4, :], w_x[:, m, :], u2[:, m, tok(b)],
                                     start=(m == 0), stop=(m == M - 1))
                last.then_inc(s_x_mm, 1)
                for i in range(b * (D + 1) // B, (b + 1) * (D + 1) // B):
                    last = pe.matmul(ps[0:KU, 5 + i // P, (i % P) * B:(i % P + 1) * B], dec_w[:, i * KU:(i + 1) * KU],
                                     w["condT"], start=True, stop=True)
                if b == B - 1:
                    last.then_inc(s_dec_mm, 1)
                pe.wait_ge(s_dbl, b + 2)
                pe.wait_ge(s_up, (B + 1) * M)
                for h in range(2):
                    if b:
                        pe.wait_ge(s_soft, 2 * b + h)
                        pe.wait_ge(s_rest, 2 * b + h - 1)
                    for m in (2 * h, 2 * h + 1):
                        last = pe.matmul(ps[:, m, :], wm["w_dt"][:, m * P:(m + 1) * P], dbl[:, tok(b)],
                                         start=True, stop=True)
                    last.then_inc(s_dt_mm, 1)
            pe.wait_ge(s_u_t, 1)
            pe.wait_ge(s_soft, 2 * B + 1)
            pe.wait_ge(s_rest, 2 * B)

            def z_products(b, y):
                pe.wait_ge(s_x1, b)
                for m in range(M):
                    for c in range(C):
                        last = pe.matmul(ps[:, y + m, :], w_z[:, c, m * P:(m + 1) * P],
                                         xn[:, bass.ds(b, 1), c, :],
                                         start=(c == 0), stop=(c == C - 1))
                last.then_inc(s_z_mm, 1)

            def d_term(b, y):
                pe.wait_ge(s_sz, b + 2)
                for m in range(M):
                    last = pe.matmul(ps[:, y + m, :], diag[:, m, :], u2[:, m, tok(b)], start=True, stop=False)
                last.then_inc(s_dterm, 1)

            def mamba_out(b, y, turn):
                pe.wait_ge(s_yz, b + 2)
                for o in range(C):
                    for m in range(M):
                        last = pe.matmul(ps[:, y + o, :], w_out[:, m, o * P:(o + 1) * P], sz[:, turn, m, :],
                                         start=(m == 0), stop=(m == M - 1))
                last.then_inc(s_out_mm, 1)

            def sum_states(b, turn, first, final):
                y, other = 4 * turn, 4 - 4 * turn
                for n in range(NS):
                    pe.wait_ge(s_hc, b * NS + n + 1 + 2 * G)
                    for m in range(M):
                        last = pe.matmul(ps[:, y + m, :], ident, state[:, (n + turn) % 3, m, :],
                                         start=False, stop=(n == NS - 1))
                    last.then_inc(s_y, 1)
                    if n == 1 and not first:
                        mamba_out(b - 1, other, 1 - turn)
                    if n == 6 and not final:
                        z_products(b + 1, other)
                    if n == 9 and not final:
                        d_term(b + 1, other)

            z_products(0, 0)
            d_term(0, 0)
            sum_states(0, 0, True, False)
            with pe.Fori(0, B // 2 - 1) as i:
                sum_states(2 * i + 1, 1, False, False)
                sum_states(2 * i + 2, 0, False, False)
            sum_states(B - 1, 1, False, True)
            mamba_out(B - 1, 4, 1)

            pe.wait_ge(s_prep, 1)
            for o in range(C):
                for c in range(C):
                    last = pe.matmul(ps[:, 3, o * B:(o + 1) * B], w2c[:, c, o * P:(o + 1) * P],
                                     style2[:, 2, c, :], start=(c == 0), stop=(c == C - 1))
            last.then_inc(s_prep_mm, 1)

            def modulated(b):
                pe.wait_ge(s_xm, b + 1)
                pe.wait_ge(s_y2, b + 1)
                for o in range(C):
                    for c in range(C):
                        last = pe.matmul(ps[:, o, :], c2_w[:, c, o * P:(o + 1) * P], xm[:, c, :],
                                         start=(c == 0), stop=(c == C - 1))
                last.then_inc(s_c2_mm, 1)

            def fp8_linear(b):
                pe.wait_ge(s_yq, b + 2)
                pe.wait_ge(s_f16, b + 1)
                for o in range(C):
                    for c in range(C):
                        last = pe.matmul(ps[:, 2 + o, :], wq8[:, c, o * P:(o + 1) * P], yq[:, c, :],
                                         start=(c == 0), stop=(c == C - 1))
                last.then_inc(s_ffn_mm, 1)

            modulated(0)
            pe.wait_ge(s_prep_act, 1)
            with pe.Fori(0, B - 1) as b:
                modulated(b + 1)
                fp8_linear(b)
            fp8_linear(B - 1)

            pe.wait_ge(s_cond2, 16)
            for j, rows_in in enumerate((128, 64, 32)):
                for o in range(C):
                    last = pe.matmul(ps[:, 4, (j * C + o) * B:(j * C + o + 1) * B],
                                     cut("v_w1", 3, D)[0:rows_in, j, o * P:(o + 1) * P],
                                     cut("v_in", 3, B)[0:rows_in, j, :], start=True, stop=True)
            last.then_inc(s_prep_mm, 1)
            pe.wait_ge(s_x2, B + 1)

            def gather(a, i, table, onehot, parts):
                if i == 0:
                    pe.wait_ge(s_oh, a + 2)
                pe.wait_ge(s_g_used, a * 4 + i + 1)
                for j in range(2):
                    for c in range(C):
                        for k in range(parts):
                            last = pe.matmul(ps[:, 2 * j + c, :], table(k, j, c), onehot(k),
                                             start=(k == 0), stop=(k == parts - 1))
                last.then_inc(s_g_mm, 1)

            def vectors(step):
                if step == 0:
                    pe.wait_ge(s_prep_act, 2)
                    for j in range(3):
                        for o in range(C):
                            for c in range(C):
                                last = pe.matmul(ps[:, 5, (j * C + o) * B:(j * C + o + 1) * B],
                                                 cut("v_w2", 3, C, D)[:, j, c, o * P:(o + 1) * P], vh[:, j, c, :],
                                                 start=(c == 0), stop=(c == C - 1))
                elif step < 3:
                    pe.wait_ge(s_prep, step + 2)
                    for j in range(3):
                        for c in range(C):
                            last = pe.matmul(ps[:, 3 + step, STATS + j * B:STATS + (j + 1) * B], mean,
                                             (vz, vsq)[step - 1][:, j, c, :], start=(c == 0), stop=(c == C - 1))
                else:
                    pe.wait_ge(s_prep, 5)
                    for o in range(C):
                        for j in range(3):
                            for c in range(C):
                                last = pe.matmul(ps[:, 4, LAYER + o * B:LAYER + (o + 1) * B],
                                                 i_w1[:, 2 + j, c, o * P:(o + 1) * P], vz[:, j, c, :],
                                                 start=(j + c == 0), stop=(j == 2 and c == C - 1))
                last.then_inc(s_prep_mm, 1)

            def embed_step(b, back, front):
                a = b + 1
                if front:
                    ln_mean(pe, norm, xT[:, :, tok(a)], B // 2 + 2 * a)
                    if not back:
                        vectors(0)
                if back:
                    pe.wait_ge(s_g_used, a * 4 + 1)
                    pe.wait_ge(s_vs, b + 1)
                    for o in range(C):
                        src = [(i_w1[:, 0], hh), (i_w1[:, 1], tt), (i_w1[:, 5], ss), (wx, xT[:, :, tok(b)])]
                        for i, (wt, x) in enumerate(src):
                            for c in range(C):
                                last = pe.matmul(ps[:, 4 + o, :], wt[:, c, o * P:(o + 1) * P], x[:, c, :],
                                                 start=(i + c == 0), stop=(i == 3 and c == C - 1))
                    last.then_inc(s_i1_mm, 1)
                if front:
                    ln_var(pe, norm, B // 2 + 2 * a)
                    if back:
                        pe.wait_ge(s_kf, a)
                    gather(a, 0, lambda k, j, c: pw_t[:, k // 2, k % 2, j, c, :], lambda k: oh_pw[:, k % 2, :], 2 * PARTS)
                    if not back:
                        vectors(1)
                if back:
                    pe.wait_ge(s_i1, b + 2)
                    for o in range(C):
                        for c in range(C):
                            last = pe.matmul(ps[:, 4 + o, :], i_w2[:, c, o * P:(o + 1) * P], i1[:, c, :],
                                             start=(c == 0), stop=(c == C - 1))
                    last.then_inc(s_i2_mm, 1)
                if front:
                    pe.wait_ge(s_h1, a + 1)
                    ln_mean(pe, norm, hh, B // 2 + 2 * a + 1)
                    gather(a, 1, lambda k, j, c: cp_t[0:PARTS * GAP, 1, j, c, :], lambda k: oh_cp[0:PARTS * GAP], 1)
                    if not back:
                        vectors(2)
                if back:
                    pe.wait_ge(s_i2, b + 1)
                    ln_mean(pe, final_norm, y3, B // 2 + b)
                if front:
                    ln_var(pe, norm, B // 2 + 2 * a + 1)
                    gather(a, 2, lambda k, j, c: ms_t[0:PARTS * GAP, j, c, :], lambda k: oh_ms[0:PARTS * GAP], 1)
                    if not back:
                        vectors(3)
                if back:
                    ln_var(pe, final_norm, B // 2 + b)
                if front:
                    gather(a, 3, lambda k, j, c: cp_t[0:PARTS * GAP, 0, j, c, :], lambda k: oh_cp[0:PARTS * GAP], 1)
                if back:
                    pe.wait_ge(s_lo_out, B // 2 + b + 2)
                    for wt, done, bank in ((w_q, s_q_mm, 4), (w_k, s_k_mm, 0)):
                        if bank == 0 and front:
                            pe.wait_ge(s_g_used, a * 4 + 5)
                        for g in range(C):
                            for c in range(C):
                                last = pe.matmul(ps[:, bank + g, :], wt[:, c, g * P:(g + 1) * P], y3[:, c, :],
                                                 start=(c == 0), stop=(c == C - 1))
                        last.then_inc(done, 1)
                    pe.wait_ge(s_qf, b + 2)
                    for t in range(TILES):
                        for c in range(C):
                            last = pe.matmul(ps[:, 4 + t // 2, (t % 2) * D:(t % 2 + 1) * D],
                                             y3[:, c, t * P:(t + 1) * P], w_v[:, c, :], start=(c == 0), stop=(c == C - 1))
                    last.then_inc(s_v_mm, 1)

            embed_step(-1, False, True)
            pe.wait_ge(s_prep, 6)
            with pe.Fori(0, B - 1) as b:
                embed_step(b, True, True)
            embed_step(B - 1, True, False)
            pe.wait_ge(s_vs, B + 1)

            pe.matmul(ps[:, 5, 0:2 * B], ones, sums[:, :, :], start=True, stop=True).then_inc(s_rho_mm, 1)

            def scores(b, hg, s):
                i, qc = s % HG, s // HG
                if s == 0:
                    pe.wait_ge(s_heads[hg], (b + 1) * 2 * len(Q_PARTS) * 16)
                pe.wait_ge(s_max, (b * HG + hg) * 16 + s + 1)
                pe.matmul(ps[:, s % 2, :], qstack[0:STACK, hg, i, qc * P:(qc + 1) * P], kstack[0:STACK, hg, i, :],
                          start=True, stop=True).then_inc(s_s_mm, 1)

            def max_rows(b, hg):
                g = b * HG + hg
                pe.wait_ge(s_max, g * 16 + 18)
                for t in range(TILES):
                    last = pe.transpose(ps[0:HG, 7, t * P:(t + 1) * P], mxs[:, hg % 2, t, :], ident)
                last.then_inc(s_m_tr, 1)

            def values(b, hg, kc):
                g = b * HG + hg
                pe.wait_ge(s_pt, g * 8 + 2 * kc + 4)
                if kc == 0:
                    pe.wait_ge(s_zt, g + 1)
                    pe.wait_ge(s_va, g + 1)
                for i in range(HG):
                    h = hg * HG + i
                    last = pe.matmul(ps[i * SLOT:(i + 1) * SLOT, 6, :], va[:, kc, h * SLOT:(h + 1) * SLOT],
                                     pt[:, (2 * kc + i // 2) % 4, i % 2, :], start=(kc == 0), stop=(kc == TILES - 1))
                last.then_inc(s_pv, 1)

            def z_rows(b, hg):
                g = b * HG + hg
                pe.wait_ge(s_zt, g + 2)
                for t in range(TILES):
                    last = pe.transpose(ps[:, 7, t * P:(t + 1) * P], zt[:, t * P:(t + 1) * P], ident)
                last.then_inc(s_z_tr, 1)

            def zn_columns(b, c):
                pe.wait_ge(s_zn, b * HG + 2 * c + 3)
                if c:
                    pe.wait_ge(s_znt, b * C + c + 1)
                for t in range(TILES):
                    last = pe.transpose(ps[:, 7, t * P:(t + 1) * P], zn[:, t, c * P:(c + 1) * P], ident)
                last.then_inc(s_zn_tr, 1)

            def attention_out(b, o):
                pe.wait_ge(s_znt, (b + 1) * C + 1)
                pe.wait_ge(s_x3, b * C + o + 1)
                for c in range(C):
                    last = pe.matmul(ps[:, 7, :], w_o[:, c, o * P:(o + 1) * P], zn_t[:, c, :],
                                     start=(c == 0), stop=(c == C - 1))
                last.then_inc(s_wo_mm, 1)

            def attend(b, first, final):
                for hg in range(HG):
                    g = b * HG + hg
                    ahead = (b + (hg + 2) // HG, (hg + 2) % HG)
                    pe.wait_ge(s_mrow_in, 16 * (g + 1) + 1)
                    for j in range(8):
                        kc, pair = j // 2, j % 2
                        pe.wait_ge(s_pt, g * 8 + j + 1)
                        for i in (2 * pair, 2 * pair + 1):
                            last = pe.matmul(ps[:, 2 + 2 * pair + i % 2, :], kstack[0:STACK + 1, hg, i, kc * P:(kc + 1) * P],
                                             qstack[0:STACK + 1, hg, i, :], start=True, stop=True)
                        last.then_inc(s_t_mm, 1)
                        if not (final and hg >= 2):
                            scores(*ahead, 2 * j)
                            scores(*ahead, 2 * j + 1)
                        if j % 2 == 0 and j:
                            values(b, hg, kc - 1)
                        if j < 2 and hg == 1 and not first:
                            zn_columns(b - 1, j)
                        if j == 2 and final and hg == HG - 1:
                            zn_columns(b, 0)
                        elif j == 2:
                            if hg == 1 and not first:
                                pe.wait_ge(s_znt, b * C + 1)
                            elif not (first and hg == 0):
                                pe.wait_ge(s_zn, g)
                            max_rows(b + (hg + 1) // HG, (hg + 1) % HG)
                        if j in (3, 4) and hg == 1 and not first:
                            pe.wait_ge(s_mrow, g + 3)
                            attention_out(b - 1, j - 3)
                        if j == 5 and not (first and hg == 0):
                            if not (final and hg == HG - 1):
                                pe.wait_ge(s_mrow, g + 3)
                            else:
                                pe.wait_ge(s_znt, b * C + 2)
                            if hg == 1:
                                pe.wait_ge(s_x3, b * C + 1)
                            z_rows(*((b, hg - 1) if hg else (b - 1, HG - 1)))
                    values(b, hg, TILES - 1)

            pe.wait_ge(s_fw, 16)
            pe.wait_ge(s_rho_sum, 1)
            for hg in range(2):
                for s in range(16):
                    scores(0, hg, s)
                if hg == 0:
                    max_rows(0, 0)
            pe.wait_ge(s_mrow, 2)
            pe.wait_ge(s_ones, 1)
            attend(0, True, False)
            with pe.Fori(1, B - 1) as b:
                attend(b, False, False)
            attend(B - 1, False, True)
            def decoded(b):
                for c in range(C):
                    last = pe.matmul(ps[:, b, c * D:(c + 1) * D], u_t[:, b, c * P:(c + 1) * P], wf["v_dec"][0:KU, :],
                                     start=True, stop=True)
                last.then_inc(s_wgt_mm, 1)

            pe.wait_ge(s_ew, 16)
            pe.wait_ge(s_pt, B * HG * 8 + 2)
            for o in range(C):
                pe.matmul(ps[:, 4, o * B:(o + 1) * B], wf["v_dec"][0:KU, o * P:(o + 1) * P], u_t[:, :, D],
                          start=True, stop=True)
            decoded(0)
            pe.wait_ge(s_zn, B * HG)
            z_rows(B - 1, HG - 1)
            decoded(1)
            zn_columns(B - 1, 1)
            decoded(2)
            attention_out(B - 1, 0)
            decoded(3)
            attention_out(B - 1, 1)

            for b in range(B):
                pe.wait_ge(s_wgt_all, min(2 * b + 2, B))
                if b == B - 1:
                    pe.wait_ge(s_x3, B * C + 1)
                for o in range(C):
                    for c in range(C):
                        last = pe.matmul(ps[:, 2 * b + o, :], wgt_all[:, b, c, o * P:(o + 1) * P], xT[:, c, tok(b)],
                                         start=(c == 0), stop=(c == C - 1))
                last.then_inc(s_y4_mm, 1)
            pe.wait_ge(s_y4, B + 1)
            for b in range(B):
                for t in range(TILES):
                    for c in range(C):
                        last = pe.matmul(ps[:, 6, (b * TILES + t) * E:(b * TILES + t + 1) * E],
                                         y4[:, b, c, t * P:(t + 1) * P], gate_w[:, c, :],
                                         start=(c == 0), stop=(c == C - 1))
            last.then_inc(s_gate_mm, 1)

            def hidden(b, f):
                pe.wait_ge(s_hid, b * FM + f + 1)
                for c in range(C):
                    last = pe.matmul(ps[:, 2 + f % 4, :], w1[:, c, f * P:(f + 1) * P],
                                     y4[:, b if isinstance(b, int) else bass.ds(b, 1), c, :],
                                     start=(c == 0), stop=(c == C - 1))
                last.then_inc(s_h_mm, 1)

            def experts(b, turn, first):
                for f in range(FM + 2):
                    if f < FM:
                        hidden(b, f)
                    if f == 2:
                        pe.wait_ge(s_x4, b + 1)
                    if f >= 2:
                        pe.wait_ge(s_hid, b * FM + f - 2 + 5)
                        for o in range(C):
                            last = pe.matmul(ps[:, 6 * turn + o, :], w2[:, f - 2, o * P:(o + 1) * P],
                                             hid[:, (f - 2) % 4, :], start=(f == 2), stop=(f == FM + 1))
                        last.then_inc(s_e_mm, 1)
                    if first and f >= FM // 2 and f % 4 == 0 and f < FM:
                        i = (f - FM // 2) // 4
                        pe.wait_ge(s_ng, 1)
                        pe.wait_ge(s_ngb, i)
                        for t in range(TILES):
                            col = i * TILES + t
                            last = pe.matmul(ps[:, 7, t * P:(t + 1) * P], gs[:, 3, col:col + 1].to_broadcast([P, P]),
                                             ident, start=True, stop=True)
                        last.then_inc(s_ngb_mm, 1)

            pe.sem_inc(s_e_mm, 4)
            experts(0, 0, True)
            pe.wait_ge(s_ngb, B)
            experts(1, 1, False)
            with pe.Fori(1, B // 2) as i:
                experts(2 * i, 0, False)
                experts(2 * i + 1, 1, False)


        @block.scalar
        def _(act):
            for started in (s_h0, s_ln_rstd, s_lo_rstd, s_dbl, s_soft, s_sz, s_f16, s_i1, s_zt, s_y4, s_vs, s_znt, s_qf, s_kf, s_mrow):
                act.sem_inc(started, 1)
            act.preload_act_table_set("natural_log_exp_and_others")
            act.sem_inc(s_kx, 2)
            act.wait_ge(s_dem_mm, 1)
            act.activation(demk, ps[:, 1:3, :], ACT.Ln, bias=eps[:, 0:1])
            act.activation(dem[:, 0], ps[:, 3, 0:C * B], ACT.Ln, bias=eps[:, 0:1])
            act.drain()
            act.activation(dem[:, 0], dem[:, 0], ACT.Exp, scale=-0.5)
            act.activation(demk, demk, ACT.Exp, scale=-0.5).then_inc(s_dem_ln, 1)

            def kx_copies(b, t, first):
                m = b * TILES + t
                act.wait_ge(s_kx_mm, m + 2)
                if not first:
                    act.wait_ge(s_mixv, m - 2)
                    act.wait_ge(s_mixp, m - 2)
                act.activation(kx[:, t, 0:D], ps[:, t % 2, 0:D], ACT.Copy)
                act.activation(kx[:, t, D:2 * D], ps[:, t % 2, 0:D], ACT.Copy).then_inc(s_kx, 1)

            def other_half(b, t):
                act.wait_ge(s_red, b * TILES + t + 1)
                act.activation(view(full[:, t % 2], [[2 * H, H - HALF], [1, H]], 2 * H + H),
                               view(full[:, t % 2], [[2 * H, H - HALF], [1, H]], 2 * H), ACT.Copy)
                act.drain()
                act.activation(view(full[:, t % 2], [[2 * H, H - HALF], [1, H]], HALF * 2 * H),
                               view(full[:, t % 2], [[1 - 2 * H, H - HALF], [1, H]], (H - HALF) * 2 * H + HALF),
                               ACT.Copy).then_inc(s_full, 1)

            def gathered(b, t):
                n = b * TILES + t
                act.wait_ge(s_ao_mm, n + 2)
                apart(act)
                for c in range(C):
                    last = act.activation(aoT[:, c, bass.ds(n * P, P)], ps[:, 4 + t % 2, c * P:(c + 1) * P],
                                          ACT.Copy, scale=style[:, 1, c, bass.ds(b, 1)])
                last.then_inc(s_ao, 1)

            def h0_out(b):
                act.wait_ge(s_o_mm, b + 1)
                apart(act)
                for o in range(C):
                    last = act.activation(hT[:, o, tok(b)], ps[:, 6 + o, :], ACT.Identity,
                                          bias=w["o_b"][:, o:o + 1], scale=dem[:, 0, o, bass.ds(b, 1)])
                last.then_inc(s_h0, 1)

            def first_attention(b, first, final):
                for t in range(TILES):
                    act.wait_ge(s_diff, b * TILES + t + 1)
                    act.activation(att[:, t % 2, :], diff[:, t % 2, :], ACT.Exp, scale=0.25).then_inc(s_exp, 1)
                    if not (final and t == TILES - 1):
                        other_half(b + (t + 1) // TILES, (t + 1) % TILES)
                    if not (final and t >= 1):
                        kx_copies(b + (t + 3) // TILES, (t + 3) % TILES, first and t < 1)
                    if not first or t >= 2:
                        gathered(b - 1 + (t + 2) // TILES, (t + 2) % TILES)
                    if t == 3 and not first:
                        h0_out(b - 1)

            kx_copies(0, 0, True)
            kx_copies(0, 1, True)
            kx_copies(0, 2, True)
            other_half(0, 0)
            first_attention(0, True, False)
            with act.Fori(1, B - 1) as b:
                first_attention(b, False, False)
            first_attention(B - 1, False, True)
            gathered(B - 1, 2)
            gathered(B - 1, 3)
            h0_out(B - 1)

            act.wait_ge(s_mam, 16)
            act.activation(a_neg, a_neg, ACT.Exp).then_inc(s_a, 1)
            for b in range(B + 2):
                L, k = (norm, other)[b % 2], b // 2
                if b >= 2:
                    ln_root(act, L, k - 1)
                if b < B:
                    ln_square(act, L, k)
            act.sem_inc(s_up, M)
            act.sem_inc(s_u2, M)
            act.wait_ge(s_pad, 1)
            act.preload_act_table_set("silu_and_others")

            def tap_in(b, chunks):
                act.drain()
                for m in chunks:
                    act.wait_ge(s_u_mm, b * M + m + 1)
                    act.wait_ge(s_cv, b * M + m + 1)
                    act.activation(uc[:, m, :], ps[:, m, :], ACT.Copy, scale=conv[:, m, TAPS - 1:TAPS])
                    act.activation(up[:, m, TAPS - 1:], ps[:, m, :], ACT.Copy).then_inc(s_up, 1)

            def silu_out(b, chunks):
                for m in chunks:
                    act.wait_ge(s_cv, (b + 1) * M + m + 1)
                    apart(act)
                    act.activation(u2[:, m, tok(b)], uc[:, m, :], ACT.Silu,
                                   bias=wm["conv_b"][:, m:m + 1]).then_inc(s_u2, 1)

            halves = range(M // 2), range(M // 2, M)
            tap_in(0, halves[0])
            with act.Fori(0, B - 1) as b:
                tap_in(b, halves[1])
                silu_out(b, halves[0])
                tap_in(b + 1, halves[0])
                silu_out(b, halves[1])
            tap_in(B - 1, halves[1])
            for half in halves:
                silu_out(B - 1, half)
            act.wait_ge(s_xh0, 1)
            act.preload_act_table_set("natural_log_exp_and_others")
            with act.Fori(0, B) as b:
                act.wait_ge(s_x_mm, b + 1)
                apart(act)
                act.activation(dbl[0:48, tok(b)], ps[0:48, 4, :], ACT.Copy).then_inc(s_dbl, 1)
                for h in range(2):
                    act.wait_ge(s_dt_mm, 2 * b + h + 1)
                    act.wait_ge(s_dt, 2 * b + h + 1)
                    apart(act)
                    for i in range(2):
                        m = 2 * h + i
                        act.activation(soft_e[:, h, i, :], ps[:, m, :], ACT.Abs, bias=wm["b_dt"][:, m:m + 1])
                    act.drain()
                    act.activation(soft_e[:, h], soft_e[:, h], ACT.Exp, scale=-1.0)
                    act.drain()
                    act.activation(soft_l[:, h], soft_e[:, h], ACT.Ln, bias=one[:, 0:1]).then_inc(s_soft, 1)
            act.sem_inc(s_scan, 2)
            act.wait_ge(s_dt, 2 * B + 2)
            act.wait_ge(s_bc, 16 * B)
            act.drain()

            def gate_z(b, turn):
                act.wait_ge(s_z_mm, b + 1)
                act.wait_ge(s_out_mm, b)
                act.activation(sz[:, turn], ps[:, 4 * turn:4 * turn + 4, :], ACT.Silu).then_inc(s_sz, 1)

            def decays(b, turn, final):
                for n in range(NS):
                    act.wait_ge(s_scan, b * NS + n + 1)
                    apart(act)
                    for m in range(M):
                        last = act.activation(decay[:, n % 2, m, 1:S], dt[:, m, bass.ds(b * S + 1, S - 1)],
                                              ACT.Exp, scale=a_neg[:, m * NS + n:m * NS + n + 1])
                    last.then_inc(s_decay, 1)
                    if n == 9 and not final:
                        gate_z(b + 1, 1 - turn)

            gate_z(0, 0)
            decays(0, 0, False)
            with act.Fori(0, B // 2 - 1) as i:
                decays(2 * i + 1, 1, False)
                decays(2 * i + 2, 0, False)
            decays(B - 1, 1, True)

            def styled(b):
                act.wait_ge(s_c2_mm, b + 1)
                apart(act)
                for c in range(C):
                    last = act.activation(xm[:, c, :], xT[:, c, tok(b)], ACT.Copy, scale=style[:, 2, c, bass.ds(b, 1)])
                last.then_inc(s_xm, 1)

            def to_half(b):
                act.wait_ge(s_ffn_mm, b + 1)
                act.wait_ge(s_x2, b + 1)
                act.activation(f16, ps[:, 2:4, :], ACT.Copy).then_inc(s_f16, 1)

            act.wait_ge(s_prep, 1)
            styled(0)
            act.wait_ge(s_prep_mm, 1)
            act.preload_act_table_set("natural_log_exp_and_others")
            act.activation(dem[:, 1], ps[:, 3, 0:C * B], ACT.Ln, bias=eps[:, 0:1])
            act.drain()
            act.activation(dem[:, 1], dem[:, 1], ACT.Exp, scale=-0.5).then_inc(s_prep_act, 1)
            with act.Fori(0, B - 1) as b:
                styled(b + 1)
                to_half(b)
            to_half(B - 1)

            act.wait_ge(s_prep_mm, 2)
            for j in range(3):
                for c in range(C):
                    last = act.activation(vh[:, j, c, :], ps[:, 4, (j * C + c) * B:(j * C + c + 1) * B], ACT.Silu,
                                          bias=cut("v_b1", 3, C)[:, j, c:c + 1])
            last.then_inc(s_prep_act, 1)
            act.preload_act_table_set("natural_log_exp_and_others")
            act.wait_ge(s_prep, 2)
            act.activation(awn[:, 0:6], awn[:, 0:6], ACT.Exp).then_inc(s_prep_act, 1)

            def embed_step(b, back, front):
                a = b + 1
                if front:
                    ln_square(act, norm, B // 2 + 2 * a)
                if back:
                    act.wait_ge(s_i1_mm, b + 2)
                    apart(act)
                    for o in range(C):
                        last = act.activation(i1[:, o, :], ps[:, 4 + o, :], ACT.Silu, bias=cvec[:, o, bass.ds(b, 1)])
                    last.then_inc(s_i1, 1)
                    act.preload_act_table_set("natural_log_exp_and_others")
                if front:
                    ln_root(act, norm, B // 2 + 2 * a)
                if back:
                    act.wait_ge(s_i2_mm, b + 2)
                    act.wait_ge(s_v_mm, b + 1)
                    for o in range(C):
                        last = act.activation(y3[:, o, :], ps[:, 4 + o, :], ACT.Identity, bias=wc["i_b2"][:, o:o + 1])
                    last.then_inc(s_i2, 1)
                if front:
                    ln_square(act, norm, B // 2 + 2 * a + 1)
                if back:
                    ln_square(act, final_norm, B // 2 + b)
                if front:
                    if not back:
                        act.wait_ge(s_prep_mm, 5)
                        act.activation(vr[:, :, :], ps[:, 5, STATS:STATS + 3 * B], ACT.Ln, bias=eps[:, 1:2])
                        act.drain()
                        act.activation(vr[:, :, :], vr[:, :, :], ACT.Exp, scale=-0.5).then_inc(s_prep_act, 1)
                    ln_root(act, norm, B // 2 + 2 * a + 1)
                if back:
                    ln_root(act, final_norm, B // 2 + b)
                    for i, (full, made, split, ready, scale, bank) in enumerate((
                            (qf, s_q_mm, s_qp, s_qf, sqk[:, 0:1], 4), (kf, s_k_mm, s_kp, s_kf, 1.0, 0))):
                        act.wait_ge(made, b + 1)
                        act.wait_ge(split, b + 1)
                        apart(act)
                        act.activation(full, ps[:, bank:bank + C, :], ACT.Square, accum_out=sums[:, i, bass.ds(b, 1)])
                        act.drain()
                        act.activation(full, ps[:, bank:bank + C, :], ACT.Copy, scale=scale).then_inc(ready, 1)
                    act.wait_ge(s_v_mm, b + 2)
                    apart(act)
                    act.activation(v_all[:, bass.ds(b, 1)], ps[:, 4:6, :], ACT.Copy).then_inc(s_vs, 1)

            embed_step(-1, False, True)
            with act.Fori(0, B - 1) as b:
                embed_step(b, True, True)
            embed_step(B - 1, True, False)
            act.wait_ge(s_rho_sum, 1)
            act.activation(rho[:, :], ssq[:, :], ACT.Ln, scale=1.0 / (N * D))
            act.drain()
            act.activation(rho[:, :], rho[:, :], ACT.Exp, scale=0.5).then_inc(s_rho_root, 1)
            act.sem_inc(s_pt, 2)
            act.wait_ge(s_kp, B + 1)
            act.wait_ge(s_k_out, 17)
            for hg in range(HG):
                load_heads(nc.scalar, 0, hg, K_STACK)
            act.wait_ge(s_k_out, 16 * B + 1)
            act.wait_ge(s_rho, 1)

            def max_row(g, parity):
                act.wait_ge(s_m_tr, g + 1)
                act.wait_ge(s_mrow_in, 16 * g - 15)
                act.activation(mrow[:, parity, :], ps[0:HG, 7, :], ACT.Copy).then_inc(s_mrow, 1)

            def weigh(b, first, final):
                for hg in range(HG):
                    g = b * HG + hg
                    for j in range(8):
                        n = g * 8 + j
                        act.wait_ge(s_t_mm, n + 1)
                        act.wait_ge(s_pv, g * TILES + j // 2)
                        act.activation(pt[:, j % 4], ps[:, 2 + 2 * (j % 2):4 + 2 * (j % 2), :], ACT.Exp,
                                       scale=rho[:, 0:1]).then_inc(s_pt, 1)
                        if hg == 1 and j in (1, 2) and not first:
                            act.wait_ge(s_zn_tr, (b - 1) * C + j)
                            act.wait_ge(s_wo_mm, (b - 1) * C + 1)
                            act.activation(zn_t[:, j - 1, :], ps[:, 7, :], ACT.Copy).then_inc(s_znt, 1)
                        if j == 3 and final and hg == HG - 1:
                            act.wait_ge(s_zn_tr, b * C + 1)
                            act.wait_ge(s_wo_mm, b * C + 1)
                            act.activation(zn_t[:, 0, :], ps[:, 7, :], ACT.Copy).then_inc(s_znt, 1)
                        elif j == 3:
                            max_row(g + 1, (hg + 1) % 2)
                    act.wait_ge(s_pv, g * TILES + TILES + 1)
                    act.wait_ge(s_z_tr, g + 1)
                    act.activation(zt, ps[:, 6, :], ACT.Copy).then_inc(s_zt, 1)

            act.wait_ge(s_m_tr, 1)
            act.activation(mrow[:, 0, :], ps[0:HG, 7, :], ACT.Copy).then_inc(s_mrow, 1)
            weigh(0, True, False)
            with act.Fori(1, B - 1) as b:
                weigh(b, False, False)
            weigh(B - 1, False, True)
            act.wait_ge(s_zn_tr, B * C)
            act.activation(zn_t[:, 1, :], ps[:, 7, :], ACT.Copy).then_inc(s_znt, 1)
            act.sem_inc(s_hid, 4)
            for b in range(B):
                act.wait_ge(s_y4_mm, b + 1)
                for o in range(C):
                    last = act.activation(y4[:, b, o, :], ps[:, 2 * b + o, :], ACT.Identity, bias=dbias[:, o, b:b + 1])
                last.then_inc(s_y4, 1)
            act.wait_ge(s_gate_sq, 1)
            act.activation(gs[:, 1, :], gs[:, 0, :], ACT.Ln, scale=1.0 / E, bias=eps32[:, 0:1])
            act.drain()
            act.activation(gs[:, 1, :], gs[:, 1, :], ACT.Exp, scale=-0.5).then_inc(s_gate_r, 1)
            act.wait_ge(s_gate_d, 1)
            act.activation(lg[:, :, :], lg[:, :, :], ACT.Exp, scale=2.0).then_inc(s_gate_e, 1)
            act.preload_act_table_set("gelu_and_others")
            with act.Fori(0, B) as b:
                for f in range(FM):
                    n = b * FM + f
                    act.wait_ge(s_h_mm, n + 2)
                    act.wait_ge(s_e_mm, n + 1)
                    act.activation(hid[:, f % 4, :], ps[:, 2 + f % 4, :], ACT.Gelu,
                                   bias=wf["b1"][:, f:f + 1]).then_inc(s_hid, 1)


        @block.vector
        def _(dve):
            for started in (s_ln_xc, s_ln_out, s_lo_xc, s_lo_out, s_x1, s_yz, s_yq, s_y2, s_g_used, s_x3, s_x4, s_x2, s_mixv, s_zn, s_oh):
                dve.sem_inc(started, 1)
            for j, v in enumerate((1e-8, 1e-5, 1e-6)):
                dve.memset(eps[:, j:j + 1], v)
            dve.wait_ge(s_early, 16)
            dve.tensor_tensor(w2k, k_w, k_w, ALU.mult)
            dve.tensor_tensor(w2o, o_w, o_w, ALU.mult)
            dve.wait_ge(s_style_mm, 1)
            for j, (name, gain) in enumerate((("k_affb", 1.0), ("o_affb", 1.0), ("c2_affb", float(P) ** -0.5))):
                for c in range(C):
                    dve.tensor_scalar(style[:, j, c, :], ps[:, 0, (j * C + c) * B:(j * C + c + 1) * B],
                                      gain, w[name][:, c:c + 1], ALU.mult, ALU.add)
            dve.drain()
            dve.tensor_tensor(style2[:, :, :, :], style[:, :, :, :], style[:, :, :, :], ALU.mult).then_inc(s_sq, 1)
            dve.wait_ge(s_dem_ln, 1)
            for b in range(B):
                for c in range(C):
                    last = dve.scalar_tensor_tensor(kw_mod[:, b, c, :], k_w[:, c, :], style[:, 0, c, b:b + 1],
                                                    demk[:, b, :], ALU.mult, ALU.mult)
            last.then_inc(s_kw, 1)

            def half_scores(b, t):
                dve.wait_ge(s_kx, b * TILES + t + 3)
                k = kx[:, t, :]
                dve.tensor_tensor(prod, view(k, [[0, HALF], [DH, H], [1, DH]]),
                                  view(k, [[DH, HALF], [DH, H], [1, DH]]), ALU.mult)
                dve.drain()
                dve.tensor_reduce(view(full[:, t % 2], [[2 * H, HALF], [1, H]]), prod, AX, ALU.add).then_inc(s_red, 1)

            def first_attention(b, first, final):
                for t in range(TILES):
                    n = b * TILES + t
                    u = t % 2
                    k = kx[:, t, :]
                    dve.wait_ge(s_full, n + 1)
                    dve.tensor_reduce(mx[:, u, :], view(full[:, u], [[1, H], [2 * H, H]]), AX, ALU.max)
                    dve.drain()
                    dve.tensor_tensor(view(diff[:, u], [[H, H], [1, H]]), view(full[:, u], [[2 * H, H], [1, H]]),
                                      view(mx[:, u], [[0, H], [1, H]]), ALU.subtract).then_inc(s_diff, 1)
                    if not (final and t == TILES - 1):
                        half_scores(b + (t + 1) // TILES, (t + 1) % TILES)
                    dve.wait_ge(s_exp, n + 1)
                    dve.tensor_reduce(ssum[:, u, :], view(att[:, u], [[1, H], [H, H]]), AX, ALU.add)
                    dve.drain()
                    dve.reciprocal(ssum[:, u, :], ssum[:, u, :])
                    dve.drain()
                    if not first or t >= 2:
                        dve.wait_ge(s_mixp, n)
                        dve.wait_ge(s_ao_mm, n)
                    dve.tensor_tensor(view(att_p[:, u], [[H, H], [1, H]]), view(att[:, u], [[H, H], [1, H]]),
                                      view(ssum[:, u], [[0, H], [1, H]]), ALU.mult).then_inc(s_att, 1)
                    dve.drain()
                    dve.tensor_tensor(view(mix[:, u, POOL_SH], [[D, H - POOL_SH], [DH, H], [1, DH]]),
                                      view(att_p[:, u], [[H, H - POOL_SH], [1, H], [0, DH]], POOL_SH * H),
                                      view(k, [[DH, H - POOL_SH], [DH, H], [1, DH]], POOL_SH * DH),
                                      ALU.mult).then_inc(s_mixv, 1)

            half_scores(0, 0)
            first_attention(0, True, False)
            with dve.Fori(1, B - 1) as b:
                first_attention(b, False, False)
            first_attention(B - 1, False, True)

            dve.memset(one[:, :], 1.0)
            dve.wait_ge(s_h0, B + 1)
            dve.wait_ge(s_mam, 16)
            dve.wait_ge(s_a, 1)
            dve.tensor_scalar(a_neg, a_neg, -1.0, None, ALU.mult)
            for m in range(M):
                dve.tensor_scalar(diag[:, m, :], ident, wm["d"][:, m:m + 1], None, ALU.mult)
            for b in range(B + 1):
                if b < B:
                    ln_centre(dve, (norm, other)[b % 2], hT[:, :, tok(b)], b // 2)
                if b:
                    L, k = (norm, other)[(b - 1) % 2], (b - 1) // 2
                    dve.wait_ge(L.s_rstd, k + 2)
                    for c in range(C):
                        dve.scalar_tensor_tensor(L.xc[:, c, :], L.xc[:, c, :], wm["gamma"][:, c:c + 1], L.rstd,
                                                 ALU.mult, ALU.mult)
                    dve.drain()
                    for c in range(C):
                        last = dve.tensor_scalar(xn[:, b - 1, c, :], L.xc[:, c, :],
                                                 wm["beta"][:, c:c + 1], None, ALU.add)
                    last.then_inc(L.s_out, 1)
            dve.drain()
            dve.memset(dbl, 0.0)
            dve.sem_inc(s_cv, M)
            dve.drain()
            for m in range(M):
                last = dve.memset(up[:, m, 0:TAPS - 1], 0.0)
            last.then_inc(s_pad, 1)
            with dve.Fori(0, B) as b:
                for m in range(0, M, 2):
                    for k in range(TAPS - 1):
                        dve.drain()
                        for i in (m, m + 1):
                            if k == 0:
                                dve.wait_ge(s_up, (b + 1) * M + i + 1)
                            last = dve.scalar_tensor_tensor(uc[:, i, :], up[:, i, k:k + S], conv[:, i, k:k + 1],
                                                            uc[:, i, :], ALU.mult, ALU.add)
                            if k == TAPS - 2:
                                last.then_inc(s_cv, 1)
            with dve.Fori(0, B) as b:
                for h in range(2):
                    dve.wait_ge(s_soft, 2 * b + h + 2)
                    dve.wait_ge(s_dt, 2 * b + h + 1)
                    apart(dve)
                    for m in (2 * h, 2 * h + 1):
                        dve.tensor_scalar(dt[:, m, tok(b)], ps[:, m, :], wm["b_dt"][:, m:m + 1], 0.0, ALU.add, ALU.max)
                    dve.tensor_scalar(soft_r[:, h], soft_e[:, h], 1.0, -1.0, ALU.add, ALU.add)
                    dve.drain()
                    dve.tensor_tensor(soft_r[:, h], soft_e[:, h], soft_r[:, h], ALU.subtract).then_inc(s_rest, 1)
            dve.wait_ge(s_dec_mm, 1)
            for i, n in ((0, P), (1, P), (2, 1)):
                last = dve.tensor_tensor(view(u_t[:, 0, i * P:i * P + n], [[D + 1, B], [1, n]]),
                                         view(ps[0:KU, 5 + i, :], [[1, B], [B, n]]),
                                         view(dec_b[0:KU, i * P:i * P + n], [[0, B], [1, n]]), ALU.add)
            last.then_inc(s_u_t, 1)
            dve.wait_ge(s_dt, 2 * B + 2)
            dve.wait_ge(s_bc, 16 * B)
            dve.sem_inc(s_hc, 2 * G)
            dve.sem_inc(s_y, 3)
            dve.drain()
            dve.memset(view(decay[:, 0], [[S, 2 * M]]), 0.0)

            def spread(b):
                dve.wait_ge(s_dterm, b + 1)
                dve.tensor_tensor(u2[:, :, tok(b)], u2[:, :, tok(b)], dt[:, :, tok(b)], ALU.mult).then_inc(s_du, 1)

            def gate_y(b, turn):
                dve.wait_ge(s_y, (b + 1) * NS + 3)
                dve.tensor_tensor(sz[:, turn], ps[:, 4 * turn:4 * turn + 4, :], sz[:, turn], ALU.mult).then_inc(s_yz, 1)

            def residual(b, turn):
                dve.wait_ge(s_out_mm, b + 2)
                dve.tensor_tensor(xT[:, :, tok(b)], ps[:, 4 * turn:4 * turn + 2, :], xT[:, :, tok(b)],
                                  ALU.add).then_inc(s_x1, 1)

            def scans(b, turn, first, final):
                for n in range(NS):
                    g = n // G
                    flat = view(state[:, (n + turn) % 3], [[1, M * S]])
                    dve.wait_ge(s_decay, b * NS + n + 1)
                    dve.wait_ge(s_dbu, b * NS + n + 1)
                    dve.tensor_tensor_scan(flat, view(decay[:, n % 2], [[1, M * S]]), flat, 0.0,
                                           ALU.mult, ALU.add).then_inc(s_scan, 1)
                    dve.drain()
                    dve.wait_ge(s_bcl[g % 2], (b * (NS // G // 2) + g // 2 + 1) * 16)
                    dve.tensor_tensor(state[:, (n + turn) % 3], state[:, (n + turn) % 3],
                                      view(bc[:, g % 2, 1, n % G, :], [[0, M], [1, S]]),
                                      ALU.mult).then_inc(s_hc, 1)
                    if n == 0 and not first:
                        gate_y(b - 1, 1 - turn)
                    if n == 4 and not first:
                        residual(b - 1, 1 - turn)
                    if n == 12 and not final:
                        spread(b + 1)

            spread(0)
            scans(0, 0, True, False)
            with dve.Fori(0, B // 2 - 1) as i:
                scans(2 * i + 1, 1, False, False)
                scans(2 * i + 2, 0, False, False)
            scans(B - 1, 1, False, True)
            gate_y(B - 1, 1)
            dve.wait_ge(s_cond, 16)
            dve.tensor_tensor(w2c, c2_w, c2_w, ALU.mult)
            wbig, wsml = xm[:, :, 0:D], xh[:, :, 0:D]
            dve.tensor_scalar(wbig, ffn_w, 448.0, -448.0, ALU.min, ALU.max)
            dve.tensor_scalar(wsml, ffn_w, 1.0, -1.0, ALU.min, ALU.max)
            dve.drain()
            dve.tensor_scalar(q8[:, :, 0:D], wbig, 0.5, None, ALU.mult, saturate=False)
            dve.tensor_scalar(q8b, wsml, 1.0, None, ALU.mult, saturate=False)
            dve.tensor_scalar(q8c, wsml, 0.5, None, ALU.mult, saturate=False)
            dve.drain()
            dve.scalar_tensor_tensor(wbig, q8[:, :, 0:D], 2.0, q8b, ALU.mult, ALU.add)
            dve.drain()
            dve.scalar_tensor_tensor(wq8, q8c, -2.0, wbig, ALU.mult, ALU.add)
            dve.drain()
            dve.engine_nop().then_inc(s_prep, 1)
            dve.wait_ge(s_out_mm, B + 1)
            dve.tensor_tensor(xT[:, :, tok(B - 1)], ps[:, 4:6, :], xT[:, :, tok(B - 1)], ALU.add).then_inc(s_x1, 1)
            dve.wait_ge(s_prep_act, 1)
            y2 = tt

            def take(b):
                dve.wait_ge(s_f16, b + 2)
                for o in range(C):
                    last = dve.scalar_tensor_tensor(xT[:, o, tok(b)], f16[:, o, :], wl["ffn_b"][:, o:o + 1],
                                                    xT[:, o, tok(b)], ALU.add, ALU.add)
                last.then_inc(s_x2, 1)

            def quantise(b, first):
                dve.wait_ge(s_c2_mm, b + 2)
                for o in range(C):
                    last = dve.tensor_scalar(y2[:, o, :], ps[:, o, :], dem[:, 1, o, bass.ds(b, 1)],
                                             wl["c2_b"][:, o:o + 1], ALU.mult, ALU.add)
                last.then_inc(s_y2, 1)
                dve.drain()
                dve.tensor_scalar(y2, y2, 256.0, -256.0, ALU.min, ALU.max)
                dve.drain()
                dve.tensor_scalar(q8, y2, 240.0, -240.0, ALU.min, ALU.max, saturate=False)
                dve.tensor_scalar(low, y2, -248.0, None, ALU.is_le)
                dve.drain()
                dve.scalar_tensor_tensor(low, y2, 248.0, low, ALU.is_ge, ALU.subtract)
                if not first:
                    take(b - 1)
                dve.drain()
                dve.scalar_tensor_tensor(yq, low, 16.0, q8, ALU.mult, ALU.add).then_inc(s_yq, 1)
                dve.drain()

            quantise(0, True)
            with dve.Fori(1, B) as b:
                quantise(b, False)
            take(B - 1)
            dve.wait_ge(s_cond2, 16)
            dve.tensor_tensor(sqk[:, :], wc["s_q"], wc["s_k"], ALU.mult)
            dve.tensor_reduce(awn[:, 6:7], wc["aw"], AX, ALU.max)
            dve.drain()
            dve.tensor_scalar(awn[:, 0:6], wc["aw"], awn[:, 6:7], None, ALU.subtract).then_inc(s_prep, 1)
            def vectors(step):
                if step == 0:
                    dve.wait_ge(s_prep_act, 3)
                    dve.tensor_reduce(awn[:, 6:7], awn[:, 0:6], AX, ALU.add)
                    dve.drain()
                    dve.reciprocal(awn[:, 7:8], awn[:, 6:7])
                    dve.drain()
                    dve.tensor_scalar(awn[:, 0:6], awn[:, 0:6], awn[:, 7:8], None, ALU.mult)
                    dve.drain()
                    for j in range(6):
                        dve.tensor_scalar(i_w1[:, j], i_w1[:, j], awn[:, j:j + 1], None, ALU.mult)
                    dve.drain()
                    dve.tensor_tensor(wx, i_w1[:, 2], i_w1[:, 3], ALU.add)
                    dve.drain()
                    dve.tensor_tensor(wx, wx, i_w1[:, 4], ALU.add)
                    dve.wait_ge(s_prep_mm, 3)
                    dve.tensor_tensor(view(vz[:, 0, 0, :], [[B, 3 * C], [1, B]]), view(ps[:, 5, :], [[B, 3 * C], [1, B]]),
                                      view(wc["v_b2"], [[1, 3 * C], [0, B]]), ALU.add).then_inc(s_prep, 1)
                if step == 1:
                    dve.wait_ge(s_prep_mm, 4)
                    dve.drain()
                    dve.tensor_tensor(vz[:, :, :, :], vz[:, :, :, :], view(ps[:, 4, :], [[B, 3], [0, C], [1, B]], STATS), ALU.subtract)
                    dve.drain()
                    dve.tensor_tensor(vsq[:, :, :, :], vz[:, :, :, :], vz[:, :, :, :], ALU.mult).then_inc(s_prep, 1)
                if step == 2:
                    dve.wait_ge(s_prep_act, 4)
                    dve.tensor_tensor(vz[:, :, :, :], vz[:, :, :, :], view(vr[:, 0, :], [[B, 3], [0, C], [1, B]]), ALU.mult)
                    dve.drain()
                    dve.tensor_tensor(view(vz[:, 0, 0, :], [[B, 3 * C], [1, B]]), view(vz[:, 0, 0, :], [[B, 3 * C], [1, B]]),
                                      view(wc["v_g"], [[1, 3 * C], [0, B]]), ALU.mult)
                    dve.drain()
                    dve.tensor_tensor(view(vz[:, 0, 0, :], [[B, 3 * C], [1, B]]), view(vz[:, 0, 0, :], [[B, 3 * C], [1, B]]),
                                      view(wc["v_be"], [[1, 3 * C], [0, B]]), ALU.add).then_inc(s_prep, 1)
                if step == 3:
                    dve.wait_ge(s_prep_mm, 6)
                    dve.tensor_tensor(cvec[:, :, :], view(ps[:, 4, :], [[B, C], [1, B]], LAYER),
                                      view(wc["i_b1"], [[1, C], [0, B]]), ALU.add).then_inc(s_prep, 1)

            def embed(a, i, out, x):
                dve.wait_ge(s_g_mm, a * 4 + i + 1)
                dve.tensor_tensor(out, x, ps[:, 0:2, :], ALU.mult)
                dve.drain()
                dve.tensor_tensor(out, out, ps[:, 2:4, :], ALU.add).then_inc(s_g_used, 1)

            def embed_step(b, back, front):
                a = b + 1
                rstd2 = view(ln_rstd, [[0, C], [1, S]])
                if front:
                    dve.wait_ge(s_ids, 16 * (a + 1))
                    if back:
                        dve.wait_ge(s_g_mm, a * 4)
                    for k in range(2):
                        dve.tensor_scalar(oh_pw[:, k, :], ids[:, 0, :], wc["rows"][:, k:k + 1], None, ALU.is_equal)
                    dve.tensor_scalar(oh_cp, ids[:, 1, :], wc["rows"][:, 2:3], None, ALU.is_equal)
                    dve.tensor_scalar(oh_ms, ids[:, 2, :], wc["rows"][:, 2:3], None, ALU.is_equal).then_inc(s_oh, 1)
                    ln_centre(dve, norm, xT[:, :, tok(a)], B // 2 + 2 * a)
                    if not back:
                        vectors(0)
                    dve.wait_ge(s_ln_rstd, B // 2 + 2 * a + 2)
                    dve.tensor_tensor(xh, ln_xc, rstd2, ALU.mult).then_inc(s_ln_out, 1)
                    dve.drain()
                    if back:
                        dve.wait_ge(s_i1_mm, a + 1)
                    embed(a, 0, hh, xh)
                    dve.drain()
                    dve.engine_nop().then_inc(s_h1, 1)
                    if not back:
                        vectors(1)
                    ln_centre(dve, norm, hh, B // 2 + 2 * a + 1)
                    embed(a, 1, tt, xh)
                    if not back:
                        vectors(2)
                if back:
                    ln_centre(dve, final_norm, y3, B // 2 + b)
                if front:
                    dve.wait_ge(s_ln_rstd, B // 2 + 2 * a + 3)
                    dve.tensor_tensor(hh, ln_xc, rstd2, ALU.mult).then_inc(s_ln_out, 1)
                    embed(a, 2, ss, xh)
                    if not back:
                        vectors(3)
                if back:
                    dve.wait_ge(s_lo_rstd, B // 2 + b + 2)
                    for c in range(C):
                        dve.scalar_tensor_tensor(y3[:, c, :], final_norm.xc[:, c, :], wc["i_g"][:, c:c + 1], final_norm.rstd,
                                                 ALU.mult, ALU.mult)
                    dve.drain()
                    for c in range(C):
                        last = dve.tensor_scalar(y3[:, c, :], y3[:, c, :], wc["i_be"][:, c:c + 1], None, ALU.add)
                    last.then_inc(s_lo_out, 1)
                if front:
                    dve.drain()
                    embed(a, 3, hh, hh)

            dve.wait_ge(s_tables, 1)
            embed_step(-1, False, True)
            with dve.Fori(0, B - 1) as b:
                embed_step(b, True, True)
            embed_step(B - 1, True, False)
            split_parts(dve, B - 1, qf, qp, xh, s_qf, s_q_out, s_qp)
            split_parts(dve, B - 1, kf, kp, xh, s_kf, s_k_out, s_kp)

            dve.wait_ge(s_rho_mm, 1)
            dve.tensor_reduce(ssq[:, :], view(ps[:, 5, :], [[B, 2], [1, B]]), AX, ALU.add).then_inc(s_rho_sum, 1)
            dve.wait_ge(s_rho_root, 1)
            dve.tensor_scalar(rho[:, :], rho[:, :], 1e-6, None, ALU.add)
            dve.drain()
            dve.tensor_tensor(rho[:, 0:1], rho[:, 0:1], rho[:, 1:2], ALU.mult)
            dve.drain()
            dve.reciprocal(rho[:, 0:1], rho[:, 0:1]).then_inc(s_rho, 1)
            dve.sem_inc(s_max, 2)

            def maximum(hg, n, s):
                i, qc = s % HG, s // HG
                dve.wait_ge(s_s_mm, n + s + 1)
                dve.tensor_reduce(mxs[:, hg % 2, qc, i:i + 1], ps[:, s % 2, :], AX, ALU.max).then_inc(s_max, 1)

            def normalise(g, hg):
                dve.wait_ge(s_z_tr, g + 2)
                dve.reciprocal(zrec[:, :, :], view(ps[:, 7, DH:], [[P, TILES], [SLOT, HG]]))
                dve.drain()
                dve.tensor_tensor(view(zn, [[D, TILES], [DH, HG], [1, DH]], hg * HG * DH),
                                  view(ps[:, 7, :], [[P, TILES], [SLOT, HG], [1, DH]]),
                                  view(zrec[:, :, :], [[HG, TILES], [1, HG], [0, DH]]), ALU.mult).then_inc(s_zn, 1)

            def attention_add(b, o):
                dve.wait_ge(s_wo_mm, b * C + o + 2)
                dve.tensor_tensor(xT[:, o, tok(b)], ps[:, 7, :], xT[:, o, tok(b)], ALU.add).then_inc(s_x3, 1)

            def follow(b, first, final):
                for hg in range(HG):
                    g = b * HG + hg
                    for s in range(16):
                        if s == 0:
                            dve.wait_ge(s_m_tr, g + 1)
                        if not (final and hg >= 2):
                            maximum(hg, (g + 2) * 16, s)
                        if s in (7, 9) and hg == 1 and not first:
                            attention_add(b - 1, (s - 7) // 2)
                        if s == 11 and not (first and hg == 0):
                            normalise(g - 1, (hg - 1) % HG)

            for hg in range(2):
                for s in range(16):
                    maximum(hg, hg * 16, s)
            follow(0, True, False)
            with dve.Fori(1, B - 1) as b:
                follow(b, False, False)
            follow(B - 1, False, True)
            dve.memset(eps32[:, :], float(np.finfo(np.float32).eps))
            dve.sem_inc(s_x4, 1)
            dve.wait_ge(s_ew, 16)
            dve.tensor_reduce(b2s[:, :], fcut("b2", C, E), AX, ALU.add)

            def decoded(b):
                dve.wait_ge(s_wgt_mm, b + 1)
                dve.tensor_copy(view(wgt_all[:, b], [[1, C * D]]), ps[:, b, :]).then_inc(s_wgt_all, 1)

            dve.wait_ge(s_wgt_mm, 1)
            dve.tensor_copy(dbias[:, :, :], ps[:, 4, 0:C * B])
            decoded(0)
            normalise(B * HG - 1, HG - 1)
            decoded(1)
            decoded(2)
            attention_add(B - 1, 0)
            decoded(3)
            attention_add(B - 1, 1)
            if "x3" in dbg:
                dve.wait_ge(s_dbg, 16 * len(dbg))
            dve.wait_ge(s_gate_mm, 1)
            dve.tensor_tensor(lg[:, :, :], view(ps[:, 6, :], [[E, B * TILES], [1, E]]),
                              view(wf["gate_b"], [[0, B * TILES], [1, E]]), ALU.add)
            dve.drain()
            dve.tensor_tensor(lg2[:, :, :], lg[:, :, :], lg[:, :, :], ALU.mult)
            dve.drain()
            dve.tensor_reduce(gs[:, 0, :], lg2[:, :, :], AX, ALU.add).then_inc(s_gate_sq, 1)
            dve.drain()
            dve.tensor_tensor(lg2[:, :, :], lg[:, :, :], view(wf["rms_w"], [[0, B * TILES], [1, E]]), ALU.mult)
            dve.drain()
            dve.wait_ge(s_gate_r, 1)
            dve.tensor_tensor(lg2[:, :, :], lg2[:, :, :], view(gs[:, 1, :], [[1, B * TILES], [0, E]]), ALU.mult)
            dve.drain()
            dve.tensor_reduce(gs[:, 2, :], lg2[:, :, :], AX, ALU.max)
            dve.drain()
            dve.tensor_tensor(lg[:, :, :], lg2[:, :, :], view(gs[:, 2, :], [[1, B * TILES], [0, E]]),
                              ALU.subtract).then_inc(s_gate_d, 1)
            dve.wait_ge(s_gate_e, 1)
            dve.tensor_reduce(gs[:, 0, :], lg[:, :, :], AX, ALU.add)
            dve.drain()
            dve.reciprocal(gs[:, 2, :], gs[:, 0, :])
            dve.drain()
            dve.tensor_scalar(gs[:, 1, :], gs[:, 2, :], 1e-6, None, ALU.add)
            dve.drain()
            dve.reciprocal(gs[:, 0, :], gs[:, 1, :])
            dve.drain()
            dve.tensor_tensor(gs[:, 3, :], gs[:, 2, :], gs[:, 0, :], ALU.mult).then_inc(s_ng, 1)
            for b in range(B):
                dve.wait_ge(s_ngb_mm, b + 1)
                dve.tensor_copy(ngb[:, b * S:(b + 1) * S], ps[:, 7, :]).then_inc(s_ngb, 1)

            def finish(b, turn):
                dve.wait_ge(s_e_mm, (b + 1) * FM + 4)
                for o in range(C):
                    dve.scalar_tensor_tensor(moe[:, o, :], ps[:, 6 * turn + o, :], b2s[:, o:o + 1], ngb[:, tok(b)],
                                             ALU.add, ALU.mult)
                dve.drain()
                dve.tensor_tensor(xT[:, :, tok(b)], xT[:, :, tok(b)], moe, ALU.add).then_inc(s_x4, 1)
                dve.drain()

            dve.drain()
            with dve.Fori(0, B // 2) as i:
                finish(2 * i, 0)
                finish(2 * i + 1, 1)


        @block.gpsimd
        def _(pool):
            for started in (s_mixp, s_qp, s_kp, s_dt):
                pool.sem_inc(started, 1)
            with pool.Fori(0, B) as b:
                for t in range(TILES):
                    n = b * TILES + t
                    u = t % 2
                    pool.wait_ge(s_att, n + 1)
                    pool.tensor_tensor(view(mix[:, u], [[D, POOL_SH], [DH, H], [1, DH]]),
                                       view(att_p[:, u], [[H, POOL_SH], [1, H], [0, DH]]),
                                       view(kx[:, t, :], [[DH, POOL_SH], [DH, H], [1, DH]]),
                                       ALU.mult).then_inc(s_mixp, 1)

            pool.wait_ge(s_h0, B + 1)
            pool.wait_ge(s_x, 16)
            pool.wait_ge(s_ln_xc, B // 2 + 1)
            pool.wait_ge(s_lo_xc, B // 2 + 1)
            pool.sem_inc(s_dt, 1)
            pool.tensor_tensor(xT[:, :, :], xT[:, :, :], hT[:, :, :], ALU.add).then_inc(s_xh0, 1)
            with pool.Fori(0, B) as b:
                for h in range(2):
                    pool.wait_ge(s_rest, 2 * b + h + 1)
                    pool.tensor_tensor(soft_l[:, h], soft_l[:, h], soft_r[:, h], ALU.add)
                    pool.drain()
                    pool.tensor_tensor(dt[:, 2 * h:2 * h + 2, tok(b)], dt[:, 2 * h:2 * h + 2, tok(b)], soft_l[:, h],
                                       ALU.add).then_inc(s_dt, 1)

            def inputs(b, turn):
                pool.wait_ge(s_du, b + 1)
                for n in range(NS):
                    g = n // G
                    pool.wait_ge(s_bcl[g % 2], (b * (NS // G // 2) + g // 2 + 1) * 16)
                    pool.wait_ge(s_y, b * NS + (min(n + 2, 3) if turn == 0 and n < 2 else n + 1))
                    apart(pool)
                    pool.tensor_tensor(state[:, (n + turn) % 3], u2[:, :, tok(b)],
                                       view(bc[:, g % 2, 0, n % G, :], [[0, M], [1, S]]),
                                       ALU.mult).then_inc(s_dbu, 1)

            with pool.Fori(0, B // 2) as i:
                inputs(2 * i, 0)
                inputs(2 * i + 1, 1)
            pool.wait_ge(s_cond2, 16)
            small = view(cw, [[1, 2 * PARTS * D]], COND["cp"][0])
            pw_rest = wc["pw"]
            pool.tensor_copy(pw_p[:, 0:4 * D], pw_rest)
            pool.tensor_copy(small_p, small)
            pool.drain()
            pool.tensor_tensor(pw_rest, pw_rest, pw_p[:, 0:4 * D], ALU.subtract)
            pool.tensor_tensor(small, small, small_p, ALU.subtract)
            pool.drain()
            pool.tensor_copy(pw_p[:, 4 * D:8 * D], pw_rest)
            for part in (1, 2):
                rows = slice(part * GAP, (part + 1) * GAP)
                pool.drain()
                pool.tensor_copy(small_p[rows], small[rows])
            pool.drain()
            pool.tensor_tensor(pw_p[:, 8 * D:12 * D], pw_rest, pw_p[:, 4 * D:8 * D], ALU.subtract)
            pool.drain()
            pool.tensor_tensor(small_p[rows], small[rows], small_p[rows], ALU.subtract).then_inc(s_tables, 1)
            with pool.Fori(0, B - 1) as b:
                split_parts(pool, b, qf, qp, rest_q, s_qf, s_q_out, s_qp)
                split_parts(pool, b, kf, kp, rest_q, s_kf, s_k_out, s_kp)
            pool.wait_ge(s_kp, B + 1)
            pool.wait_ge(s_vs, B + 1)
            pool.memset(kstack[STACK:STACK + 1], -1.0).then_inc(s_ones, 1)
            pool.drain()
            pool.wait_ge(s_k_out, 16 * B + 1)
            pool.memset(va, 0.0)
            pool.drain()
            pool.memset(view(va, [[SLOT, TILES * H]], DH), 1.0)

            def fill_slots(src, hg):
                pool.tensor_copy(view(va, [[H * SLOT, TILES], [SLOT, HG], [1, DH]], hg * HG * SLOT),
                                 view(src, [[D, TILES], [DH, HG], [1, DH]], hg * HG * DH)).then_inc(s_va, 1)

            for hg in range(HG):
                fill_slots(v_all[:, 0], hg)
            with pool.Fori(1, B) as b:
                for hg in range(HG):
                    pool.wait_ge(s_pv, (b * HG + hg) * TILES + 1 - (HG - 1) * TILES)
                    apart(pool)
                    fill_slots(v_all[:, bass.ds(b, 1)], hg)


ARENA = 36000


def chunked(a):
    a = np.asarray(a)
    k = a.shape[0] // P
    return a.reshape(k, P, -1).transpose(1, 0, 2).reshape(P, -1)


def rows(a):
    a = np.asarray(a, np.float32)
    out = np.zeros((P, a.shape[1]), np.float32)
    out[:a.shape[0]] = a
    return out


def pack(spec, width, parts):
    out = np.zeros((P, width), np.float32)
    for name, (at, n) in spec.items():
        a = parts[name]
        assert a.shape == (P, n), (name, a.shape, n)
        out[:, at:at + n] = a
    return out


def host_arrays(i):
    col = lambda v: chunked(np.asarray(v).reshape(-1, 1))
    wide = lambda v: np.broadcast_to(np.asarray(v).reshape(1, -1), (P, np.asarray(v).size))
    x = np.asarray(i["x"]).reshape(N, D).T
    early = pack(EARLY, EARLY_W, dict(
        condT=np.asarray(i["cond_512"]).T, k_aff=np.asarray(i["L0_cond_k_aff_w"]).T,
        o_aff=np.asarray(i["L0_cond_o_aff_w"]).T, c2_aff=np.asarray(i["L0_cond2_affine_w"]).T,
        k_affb=col(i["L0_cond_k_aff_b"]), o_affb=col(i["L0_cond_o_aff_b"]), c2_affb=col(i["L0_cond2_affine_b"]),
        k_w=chunked(np.asarray(i["L0_cond_k_w"]).T), o_w=chunked(np.asarray(i["L0_cond_o_w"]).T),
        ident=np.eye(P, dtype=np.float32), mean=np.full((P, P), 1.0 / D, np.float32),
        ones=np.ones((P, P), np.float32), k_b=wide(i["L0_cond_k_b"]), o_b=col(i["L0_cond_o_b"])))
    w_in = np.asarray(i["L0_attn_W_in"])
    mamba = pack(MAMBA, MAMBA_W, dict(
        gamma=col(i["L0_attn_gamma"]), beta=col(i["L0_attn_beta"]), w_u=chunked(w_in[:, :DI]), spare=np.zeros((P, 2 * C), np.float32),
        conv=chunked(i["L0_attn_conv_w"]), w_z=chunked(w_in[:, DI:]), conv_b=col(i["L0_attn_conv_b"]),
        w_x=chunked(i["L0_attn_W_x"]), w_dt=rows(i["L0_attn_W_dt"]), b_dt=col(i["L0_attn_b_dt"]),
        a_log=chunked(i["L0_attn_A_log"]), d=col(i["L0_attn_D"]), w_out=chunked(i["L0_attn_W_out"])))
    table = lambda g, b: np.concatenate([np.asarray(i[g]), np.asarray(i[b])], axis=1)
    pw = table("L1_cond_pw_g", "L1_cond_pw_b")
    three = lambda f: np.concatenate([f(x) for x in ("mem", "noi", "res")], axis=1)
    wqkv = np.asarray(i["L1_attn_Wqkv"])
    linear = pack(LINEAR, LINEAR_W, dict(
        c2_w=chunked(np.asarray(i["L0_cond2_weight"]).T), c2_b=col(i["L0_cond2_bias"]),
        ffn_w=chunked(np.asarray(i["L0_ffn_weight"]).T), ffn_b=col(i["L0_ffn_bias"])))
    thrice = lambda a: rows(np.concatenate([rows(a)[:GAP]] * PARTS))
    cond = pack(COND, COND_W, dict(
        pw=np.concatenate([rows(pw[:PWK]), rows(pw[PWK:])], axis=1),
        cp=thrice(np.concatenate([table("L1_cond_cp_g", "L1_cond_cp_b"), table("L1_cond_tm_g", "L1_cond_tm_b")], axis=1)),
        ms=thrice(table("L1_cond_ms_g", "L1_cond_ms_b")),
        rows=np.stack([np.arange(P), np.arange(P) + PWK, np.arange(P) % GAP], axis=1).astype(np.float32), aw=wide(i["L1_cond_aw"]),
        v_in=np.concatenate([rows(np.asarray(i[x]).T) for x in ("cond_512", "cond_64", "fside_Bx32_0")], axis=1),
        v_w1=three(lambda x: rows(i[f"L1_cond_{x}_W1"])), v_w2=three(lambda x: chunked(i[f"L1_cond_{x}_W2"])),
        v_b1=three(lambda x: col(i[f"L1_cond_{x}_b1"])), v_b2=three(lambda x: col(i[f"L1_cond_{x}_b2"])),
        v_g=three(lambda x: col(i[f"L1_cond_{x}_g"])), v_be=three(lambda x: col(i[f"L1_cond_{x}_be"])),
        i_w1=chunked(i["L1_cond_int_W1"]), i_w2=chunked(i["L1_cond_int_W2"]), i_b1=col(i["L1_cond_int_b1"]),
        i_b2=col(i["L1_cond_int_b2"]), i_g=col(i["L1_cond_int_g"]), i_be=col(i["L1_cond_int_be"]),
        w_q=chunked(wqkv[:, :D]), w_k=chunked(wqkv[:, D:2 * D]), w_v=chunked(wqkv[:, 2 * D:]),
        s_q=np.tile(np.asarray(i["L1_attn_scale_q"]), P // DH).reshape(P, 1),
        s_k=np.tile(np.asarray(i["L1_attn_scale_k"]), P // DH).reshape(P, 1)))
    ids = np.stack([np.asarray(i[k]).reshape(-1) for k in ("itok_BxS_0_999", "itok_BxS_0_4", "mask_BxS_ik0")])
    per = lambda a: np.asarray(a).transpose(1, 0, 2).reshape(np.asarray(a).shape[1], -1)
    ffn = pack(FFN, FFN_W, dict(
        w_o=chunked(i["L1_attn_Wo"]), v_dec=rows(i["L1_cond2_V"]), gate_w=chunked(np.asarray(i["L1_ffn_gate_w"]).T),
        gate_b=wide(i["L1_ffn_gate_b"]), rms_w=wide(i["L1_ffn_rms_w"]),
        b1=np.asarray(i["L1_ffn_b1"]).reshape(FM, P).T, b2=chunked(np.asarray(i["L1_ffn_b2"]).T),
        w1=chunked(per(i["L1_ffn_w1"])), w2=chunked(np.asarray(i["L1_ffn_w2"]).reshape(E * FH, D))))
    return {
        "cond": cond, "linear": linear, "ffn": ffn, "ids": ids.astype(np.int32), "dec_w": np.asarray(i["L1_cond2_W_dec"]),
        "dec_b": np.ascontiguousarray(np.asarray(i["L1_cond2_b_dec"]).reshape(D + 1, KU).T),
        "mamba": mamba,
        "xT": np.ascontiguousarray(x.reshape(C, P, N).transpose(1, 0, 2)),
        "early": early,
    }


def kernel(**inputs):
    import concourse.bacc as bacc
    from concourse.bass_utils import run_bass_kernel_spmd
    arrays = host_arrays(inputs)
    nc = bacc.Bacc("TRN2", target_bir_lowering=False, num_devices=1)
    t_in = {k: nc.dram_tensor(f"in_{k}", a.shape, mybir.dt.from_np(a.dtype), kind="ExternalInput").ap()
            for k, a in arrays.items()}
    out = nc.dram_tensor("out", (P, C, N), F32, kind="ExternalOutput").ap()
    program(nc, t_in, out)
    r = run_bass_kernel_spmd(nc, [{f"in_{k}": a for k, a in arrays.items()}], core_ids=[0])
    got = r.results[0]["out"]
    return np.ascontiguousarray(got.transpose(1, 0, 2).reshape(D, N).T).reshape(B, S, D)
```
